# Optimizing a Trainium2 kernel written in Bass

```python
import numpy as np
import jax
import jax.numpy as jnp

def _softmax(x, axis=-1):
    return jax.nn.softmax(x, axis=axis)

def _gelu(x):
    return jax.nn.gelu(x, approximate=True)

def _silu(x):
    return jax.nn.silu(x)

def _sigmoid(x):
    return jax.nn.sigmoid(x)

def _layernorm(x, axis=-1, eps=1e-05):
    m = jnp.mean(x, axis=axis, keepdims=True)
    v = jnp.var(x, axis=axis, keepdims=True)
    return (x - m) / jnp.sqrt(v + eps)

def _scatter_add(tgt, idx, src, axis=0):
    return tgt.at[idx].add(src)

def _segment_sum(src, seg, n):
    return jax.ops.segment_sum(src, seg, n)
kernel_name = 'mk_seq_postln_d1_jaxref_r4_208feb'

def setup_inputs(seed: int=0):
    np.random.seed(seed)
    _w = jnp.asarray

    def _L0_attn_setup():
        import jax, jax.numpy as jnp
        import numpy as np
        B, T, D = (2, 512, 256)
        HEAD_DIM, N_HEADS, N_HH, HEAD_V_DIM, CONV_SIZE = (128, 8, 3, 128, 4)

        def _short_conv(x, w):
            cs = w.shape[-1]
            t = x.shape[1]
            xp = jnp.pad(x, ((0, 0), (cs - 1, 0), (0, 0)))
            y = sum((xp[:, i:i + t, :] * w[:, i] for i in range(cs)))
            return jax.nn.silu(y)

        def _l2norm(x, eps=1e-06):
            return x * jax.lax.rsqrt(jnp.sum(x * x, -1, keepdims=True) + eps)

        def _forward(x, Wq, Wk, Wv, Wb, Wa, A_log, dt_bias, conv_q, conv_k, conv_v, Wg, rms_weight, Wo):
            b, t, _ = x.shape
            h, d, dv, nh = (N_HEADS, HEAD_DIM, HEAD_V_DIM, N_HH)
            q = _short_conv(x @ Wq, conv_q).reshape(b, t, h, d)
            k = _short_conv(x @ Wk, conv_k).reshape(b, t, nh, h, d).transpose(0, 1, 3, 2, 4)
            v = _short_conv(x @ Wv, conv_v).reshape(b, t, nh, h, dv).transpose(0, 1, 3, 2, 4)
            beta = 2.0 * jax.nn.sigmoid(x @ Wb).reshape(b, t, nh, h).transpose(0, 1, 3, 2)
            g = -jnp.exp(A_log) * jax.nn.softplus(x @ Wa + dt_bias)
            q = _l2norm(q) * d ** (-0.5)
            k = _l2norm(k)

            def step(S, inp):
                qt, kt, vt, bt, gt = inp
                S = S * jnp.exp(gt)[..., None, None]
                for i in range(nh):
                    ki, vi, bi = (kt[:, :, i], vt[:, :, i], bt[:, :, i])
                    kS = jnp.einsum('bhd,bhde->bhe', ki, S)
                    S = S + bi[..., None, None] * (ki[..., None] * (vi - kS)[:, :, None, :])
                o = jnp.einsum('bhd,bhde->bhe', qt, S)
                return (S, o)
            xs = tuple((jnp.moveaxis(a, 1, 0) for a in (q, k, v, beta, g)))
            S0 = jnp.zeros((b, h, d, dv), x.dtype)
            _, o = jax.lax.scan(step, S0, xs)
            o = jnp.moveaxis(o, 0, 1)
            gate = (x @ Wg).reshape(b, t, h, dv)
            o = o * jax.lax.rsqrt(jnp.mean(o * o, -1, keepdims=True) + 1e-05) * rms_weight
            o = o * jax.nn.silu(gate)
            return o.reshape(b, t, h * dv) @ Wo
        key = jax.random.key(seed)
        ks = jax.random.split(key, 16)
        h, d, dv, nh, cs = (N_HEADS, HEAD_DIM, HEAD_V_DIM, N_HH, CONV_SIZE)
        f = lambda k, shape, s=0.02: jax.random.normal(k, shape, jnp.float32) * s
        return {'x': f(ks[0], (B, T, D), 1.0), 'cos': f(ks[1], (T, d), 1.0), 'sin': f(ks[2], (T, d), 1.0), 'Wq': f(ks[3], (D, h * d)), 'Wk': f(ks[4], (D, h * d * nh)), 'Wv': f(ks[5], (D, h * dv * nh)), 'Wb': f(ks[6], (D, h * nh)), 'Wa': f(ks[7], (D, h)), 'A_log': jnp.log(jax.random.uniform(ks[8], (h,), jnp.float32, 0.5, 8.0)), 'dt_bias': f(ks[9], (h,), 0.1), 'conv_q': f(ks[10], (h * d, cs), 0.5), 'conv_k': f(ks[11], (h * d * nh, cs), 0.5), 'conv_v': f(ks[12], (h * dv * nh, cs), 0.5), 'Wg': f(ks[13], (D, h * dv)), 'rms_weight': jnp.ones((dv,), jnp.float32), 'Wo': f(ks[14], (h * dv, D))}
    _L0_attn_in = _L0_attn_setup()

    def _L0_ffn_setup():
        import jax, jax.numpy as jnp
        import numpy as np
        from jax import lax
        B, S, D = (4, 512, 256)
        E = 8
        K = 2
        F = 816
        NORM_TOPK = True
        key = jax.random.key(seed)
        ks = jax.random.split(key, 8)
        sd = 0.02
        return {'x': jax.random.normal(ks[0], (B, S, D), jnp.float32), 'gate_w': jax.random.normal(ks[1], (E, D), jnp.float32) * sd, 'gate_b': jnp.zeros((E,), jnp.float32), 'up_w': jax.random.normal(ks[2], (E, F, D), jnp.float32) * sd, 'up_b': jnp.zeros((E, F), jnp.float32), 'gp_w': jax.random.normal(ks[3], (E, F, D), jnp.float32) * sd, 'gp_b': jnp.zeros((E, F), jnp.float32), 'down_w': jax.random.normal(ks[4], (E, D, F), jnp.float32) * sd, 'down_b': jnp.zeros((E, D), jnp.float32)}
    _L0_ffn_in = _L0_ffn_setup()
    _d = {'L0_attn_x': _L0_attn_in['x'], 'L0_attn_cos': _L0_attn_in['cos'], 'L0_attn_sin': _L0_attn_in['sin'], 'L0_attn_Wq': _L0_attn_in['Wq'], 'L0_attn_Wk': _L0_attn_in['Wk'], 'L0_attn_Wv': _L0_attn_in['Wv'], 'L0_attn_Wb': _L0_attn_in['Wb'], 'L0_attn_Wa': _L0_attn_in['Wa'], 'L0_attn_A_log': _L0_attn_in['A_log'], 'L0_attn_dt_bias': _L0_attn_in['dt_bias'], 'L0_attn_conv_q': _L0_attn_in['conv_q'], 'L0_attn_conv_k': _L0_attn_in['conv_k'], 'L0_attn_conv_v': _L0_attn_in['conv_v'], 'L0_attn_Wg': _L0_attn_in['Wg'], 'L0_attn_rms_weight': _L0_attn_in['rms_weight'], 'L0_attn_Wo': _L0_attn_in['Wo'], 'L0_ffn_gate_w': _L0_ffn_in['gate_w'], 'L0_ffn_gate_b': _L0_ffn_in['gate_b'], 'L0_ffn_up_w': _L0_ffn_in['up_w'], 'L0_ffn_up_b': _L0_ffn_in['up_b'], 'L0_ffn_gp_w': _L0_ffn_in['gp_w'], 'L0_ffn_gp_b': _L0_ffn_in['gp_b'], 'L0_ffn_down_w': _L0_ffn_in['down_w'], 'L0_ffn_down_b': _L0_ffn_in['down_b']}
    _x0 = _d['L0_attn_x']
    _d['L0_attn_x'] = jax.random.normal(jax.random.fold_in(jax.random.key(seed), 1), (2, 2048, 256), dtype=_x0.dtype)
    del _x0
    return _d

def reference(L0_attn_x, L0_attn_cos, L0_attn_sin, L0_attn_Wq, L0_attn_Wk, L0_attn_Wv, L0_attn_Wb, L0_attn_Wa, L0_attn_A_log, L0_attn_dt_bias, L0_attn_conv_q, L0_attn_conv_k, L0_attn_conv_v, L0_attn_Wg, L0_attn_rms_weight, L0_attn_Wo, L0_ffn_gate_w, L0_ffn_gate_b, L0_ffn_up_w, L0_ffn_up_b, L0_ffn_gp_w, L0_ffn_gp_b, L0_ffn_down_w, L0_ffn_down_b):

    def _L0_attn_ref(x, cos, sin, Wq, Wk, Wv, Wb, Wa, A_log, dt_bias, conv_q, conv_k, conv_v, Wg, rms_weight, Wo):
        import jax, jax.numpy as jnp
        import numpy as np
        B, T, D = (2, 512, 256)
        HEAD_DIM, N_HEADS, N_HH, HEAD_V_DIM, CONV_SIZE = (128, 8, 3, 128, 4)

        def _short_conv(x, w):
            cs = w.shape[-1]
            t = x.shape[1]
            xp = jnp.pad(x, ((0, 0), (cs - 1, 0), (0, 0)))
            y = sum((xp[:, i:i + t, :] * w[:, i] for i in range(cs)))
            return jax.nn.silu(y)

        def _l2norm(x, eps=1e-06):
            return x * jax.lax.rsqrt(jnp.sum(x * x, -1, keepdims=True) + eps)

        def _forward(x, Wq, Wk, Wv, Wb, Wa, A_log, dt_bias, conv_q, conv_k, conv_v, Wg, rms_weight, Wo):
            b, t, _ = x.shape
            h, d, dv, nh = (N_HEADS, HEAD_DIM, HEAD_V_DIM, N_HH)
            q = _short_conv(x @ Wq, conv_q).reshape(b, t, h, d)
            k = _short_conv(x @ Wk, conv_k).reshape(b, t, nh, h, d).transpose(0, 1, 3, 2, 4)
            v = _short_conv(x @ Wv, conv_v).reshape(b, t, nh, h, dv).transpose(0, 1, 3, 2, 4)
            beta = 2.0 * jax.nn.sigmoid(x @ Wb).reshape(b, t, nh, h).transpose(0, 1, 3, 2)
            g = -jnp.exp(A_log) * jax.nn.softplus(x @ Wa + dt_bias)
            q = _l2norm(q) * d ** (-0.5)
            k = _l2norm(k)

            def step(S, inp):
                qt, kt, vt, bt, gt = inp
                S = S * jnp.exp(gt)[..., None, None]
                for i in range(nh):
                    ki, vi, bi = (kt[:, :, i], vt[:, :, i], bt[:, :, i])
                    kS = jnp.einsum('bhd,bhde->bhe', ki, S)
                    S = S + bi[..., None, None] * (ki[..., None] * (vi - kS)[:, :, None, :])
                o = jnp.einsum('bhd,bhde->bhe', qt, S)
                return (S, o)
            xs = tuple((jnp.moveaxis(a, 1, 0) for a in (q, k, v, beta, g)))
            S0 = jnp.zeros((b, h, d, dv), x.dtype)
            _, o = jax.lax.scan(step, S0, xs)
            o = jnp.moveaxis(o, 0, 1)
            gate = (x @ Wg).reshape(b, t, h, dv)
            o = o * jax.lax.rsqrt(jnp.mean(o * o, -1, keepdims=True) + 1e-05) * rms_weight
            o = o * jax.nn.silu(gate)
            return o.reshape(b, t, h * dv) @ Wo
        return _forward(x, Wq, Wk, Wv, Wb, Wa, A_log, dt_bias, conv_q, conv_k, conv_v, Wg, rms_weight, Wo)

    def _L0_ffn_ref(x, gate_w, gate_b, up_w, up_b, gp_w, gp_b, down_w, down_b):
        import jax, jax.numpy as jnp
        import numpy as np
        from jax import lax
        B, S, D = (4, 512, 256)
        E = 8
        K = 2
        F = 816
        NORM_TOPK = True
        bs, slen, dim = x.shape
        xf = x.reshape(-1, dim)
        N = xf.shape[0]
        scores = jax.nn.softmax(xf @ gate_w.T + gate_b, axis=-1)
        top_w, top_idx = lax.top_k(scores, K)
        if NORM_TOPK:
            top_w = top_w / (top_w.sum(-1, keepdims=True) + 1e-20)
        comb = jnp.zeros((N, E), xf.dtype).at[jnp.arange(N)[:, None], top_idx].add(top_w)

        def step(acc, p):
            uw, ub, gw, gb, dw, db, w = p
            h = jax.nn.silu((xf @ gw.T + gb) * (xf @ uw.T + ub))
            return (acc + w[:, None] * (h @ dw.T + db), None)
        y0 = jnp.zeros_like(xf)
        y, _ = lax.scan(step, y0, (up_w, up_b, gp_w, gp_b, down_w, down_b, comb.T))
        return y.reshape(bs, slen, dim)
    x = L0_attn_x
    x = _layernorm(x + _L0_attn_ref(x, L0_attn_cos, L0_attn_sin, L0_attn_Wq, L0_attn_Wk, L0_attn_Wv, L0_attn_Wb, L0_attn_Wa, L0_attn_A_log, L0_attn_dt_bias, L0_attn_conv_q, L0_attn_conv_k, L0_attn_conv_v, L0_attn_Wg, L0_attn_rms_weight, L0_attn_Wo), axis=-1)
    x = _layernorm(x + _L0_ffn_ref(x, L0_ffn_gate_w, L0_ffn_gate_b, L0_ffn_up_w, L0_ffn_up_b, L0_ffn_gp_w, L0_ffn_gp_b, L0_ffn_down_w, L0_ffn_down_b), axis=-1)
    return x

_drawn_inputs = setup_inputs


def setup_inputs(seed=0):
    import zlib

    import numpy as np

    out = dict(_drawn_inputs(seed))
    spreads = {'L0_attn_rms_weight': (1.0, 0.6),
     'L0_ffn_gate_b': (0.0, 0.1),
     'L0_ffn_up_b': (0.0, 0.8),
     'L0_ffn_gp_b': (0.0, 0.8),
     'L0_ffn_down_b': (0.0, 0.1)}
    factors = {'L0_attn_Wb': 5.788, 'L0_attn_Wa': 8.0, 'L0_attn_dt_bias': 8.0}
    for name, (base, spread) in spreads.items():
        noise = np.random.default_rng([zlib.crc32(name.encode()), seed]).standard_normal(out[name].shape)
        drawn = base * np.exp(spread * noise) if base else spread * noise
        out[name] = jnp.asarray(drawn.astype(out[name].dtype))
    for name, factor in factors.items():
        out[name] = (out[name] * factor).astype(out[name].dtype)
    return out
```

```python
from contextlib import ExitStack

import numpy as np
import concourse.bass as bass
from concourse import mybir

F32 = mybir.dt.float32
F16 = mybir.dt.float16
BF16 = mybir.dt.bfloat16
U16 = mybir.dt.uint16
U32 = mybir.dt.uint32
ALU = mybir.AluOpType
ACT = mybir.ActivationFunctionType
AX = mybir.AxisListType

P = 128
B, T, D = 2, 2048, 256
KT = D // P
H, NH, DH = 8, 3, 128
TAPS = 4
CH = 32
UN = 8
TB = CH * UN
NTB = T // TB
NIT = B * H * NTB
XW = T + TAPS
PW = TB + TAPS - 1
NTILE = 2 * NH + 2
NCONV = NTILE - 1
HC = NTILE * DH
LEVELS = 7
E, F = 8, 816
FT = -(-F // P)
FP = FT * P
NTT = B * T // P
NB = B * T // 512
MASKED = -30000.0
EPS_K, EPS_RMS, EPS_LN = 1e-6, 1e-5, 1e-5



def constants():
    p = np.arange(P)
    j, t = p // CH, p % CH
    o = 4 * t + j
    before = (o[:, None] < o[None, :]) & (j[:, None] < NH)
    neg = np.where(before, 0.0, MASKED).astype(np.float32)
    masks = []
    for l in range(LEVELS):
        later, earlier = o[:, None], o[None, :]
        masks.append(((later >> (l + 1)) == (earlier >> (l + 1))) & ((later >> l) & 1 == 1) & ((earlier >> l) & 1 == 0))
    masks = np.stack(masks, 1).astype(np.uint16)
    m0t = masks[:, 0, :].T.astype(np.float32)
    later_t = (t[:, None] > t[None, :]).astype(np.float32)
    upto_t = (t[:, None] <= t[None, :]).astype(np.float32)
    ident = np.eye(P, dtype=np.float32)
    ones = np.ones((P, P), np.float32)
    c = np.concatenate([ident, neg, later_t, upto_t, m0t, ones], 1)
    return c, np.ascontiguousarray(masks.reshape(P, LEVELS * P))


C_ID, C_NEG, C_LATER, C_UPTO, C_M0T, C_ONES = range(6)


def at_least(eng, sem, value):
    if isinstance(value, int) and value <= 0:
        return
    eng.wait_ge(sem, value)


def build(nc, x_t, x_rows, w_all, w_z, conv_w, a_log, dt_bias, rms_w, w_o, consts, masks,
          gate_w, gate_b, up_w, up_b, gp_w, gp_b, down_w, down_b, out):
    y_dram = nc.dram_tensor("y_scratch", (NIT, P, TB), F32).ap()
    w_dram = nc.dram_tensor("w_parts_scratch", (H, P, 2 * KT * HC), U16).ap()
    ctx = ExitStack()
    with ctx:
        def sem(name):
            return ctx.enter_context(nc.semaphore(name))

        attention_scope = ExitStack()
        scope = attention_scope

        def sb(name, shape, dt):
            return scope.enter_context(nc.sbuf_tensor(name, shape, dt))

        bank = [ctx.enter_context(nc.psum_tensor(f"bank{i}", [P, 512], F32)) for i in range(8)]

        cst = sb("cst", [P, 6, P], F32)
        x_parts = sb("x_parts", [P, 2, KT, B, XW], U16)
        tables = sb("tables", [P, NIT, 4, UN], F32)
        g_parts = sb("g_parts", [P, NIT, UN], BF16)
        conv_sb = sb("conv_sb", [P, H, NCONV, TAPS], F32)
        ident16 = sb("ident16", [P, P], F16)
        rep16 = sb("rep16", [P, 4, P], F16)
        negid16 = sb("negid16", [P, P], F16)
        identb = sb("identb", [P, P], BF16)
        negmask = sb("negmask", [P, P], BF16)
        laterb = sb("laterb", [P, P], BF16)
        uptob = sb("uptob", [P, P], BF16)
        onesb = sb("onesb", [P, P], BF16)
        mask0t = sb("mask0t", [P, P], F16)
        mask_sb = sb("mask_sb", [P, LEVELS, P], U16)
        neg_rms = sb("neg_rms", [P, 1], F32)
        rms_raw = sb("rms_raw", [P, 1], F32)
        over_dh = sb("over_dh", [P, P], F32)
        eps_dh = sb("eps_dh", [P, P], F32)

        with ExitStack() as setup_scope:
            scope = setup_scope
            x_stage = sb("x_stage", [P, KT, B, XW], F32)
            w_stage = sb("w_stage", [P, 2, KT, HC], F32)
            w_pair = [sb(f"w_pair{i}", [P, 2, KT, HC], U16) for i in range(2)]
            wz_stage = sb("wz_stage", [P, KT, 32], F32)
            wz_parts = sb("wz_parts", [P, 2, KT, 32], U16)
            x_flat = x_stage[0:32].rearrange("p a b c -> p (a b c)")
            z_t, z_rows = x_flat[:, 0:B * T], x_flat[:, B * T:2 * B * T]
            beta = sb("beta", [P, B * H, T // CH], F32)
            g_full = sb("g_full", [P, B * H, T // CH], F32)
            work_a = sb("work_a", [P, B * H, T // CH], F32)
            work_b = sb("work_b", [P, B * H, T // CH], F32)
            g_hi = sb("g_hi", [P, B * H, T // CH], BF16)
            alog_sb = sb("alog_sb", [96, H], F32)
            dt_sb = sb("dt_sb", [96, H], F32)
            consts_in, x_in, z_in, small_in, x_split_a, x_split_b = map(
                sem, ("consts_in", "x_in", "z_in", "small_in", "x_highs", "x_lows"))
            w_in = [sem("w_in0"), sem("w_in1")]
            w_stored = [sem("w_stored0"), sem("w_stored1")]
            w_high, w_low, wz_high, wz_low = map(sem, ("w_high", "w_low", "wz_high", "wz_low"))
            zp_done, zt_done, tr_done, dv, ac, cum_done, casts, exp_cum = map(
                sem, ("z_projected", "z_evacuated", "z_turned", "setup_dve", "setup_act", "sums_done",
                      "consts_cast", "sums_exp"))
            with nc.Block() as block:
                @block.sync
                def _(sp):
                    sp.dma_start(x_stage[:].rearrange("p a b c -> p (a b c)"), x_t).then_inc(x_in, 16)
                    sp.dma_start(wz_stage[:].rearrange("p a b -> p (a b)"), w_z).then_inc(z_in, 16)
                    sp.dma_start(cst[:].rearrange("p a b -> p (a b)"), consts).then_inc(consts_in, 16)
                    sp.dma_start(mask_sb[:].rearrange("p a b -> p (a b)"), masks).then_inc(consts_in, 16)
                    sp.dma_start(conv_sb[:].rearrange("p a b c -> p (a b c)"), conv_w).then_inc(small_in, 16)
                    sp.dma_start(alog_sb[:], a_log).then_inc(small_in, 16)
                    sp.dma_start(dt_sb[:], dt_bias).then_inc(small_in, 16)
                    sp.dma_start(rms_raw[:], rms_w).then_inc(small_in, 16)
                    def load_head(h):
                        sp.dma_start(w_stage[:, h % 2].rearrange("p a b -> p (a b)"), w_all[h]).then_inc(w_in[h % 2], 16)

                    load_head(0)
                    load_head(1)
                    for h in range(H):
                        sp.wait_ge(w_low, h + 1)
                        sp.dma_start(w_dram[h], w_pair[h % 2][:].rearrange("p a b c -> p (a b c)")).then_inc(w_stored[h % 2], 16)
                        if h + 2 < H:
                            load_head(h + 2)
                    for i in range(2):
                        sp.wait_ge(w_stored[i], 16 * (H // 2))

                @block.gpsimd
                def _(pool):
                    for h in range(H):
                        pool.wait_ge(w_high, h + 1)
                        nc.gpsimd.tensor_tensor(w_pair[h % 2][:, 1].bitcast(BF16), w_stage[:, h % 2],
                                                w_pair[h % 2][:, 0].bitcast(F16), ALU.subtract).then_inc(w_low, 1)

                @block.scalar
                def _(act):
                    act.wait_ge(z_in, 16)
                    nc.scalar.activation(wz_parts[:, 0].bitcast(F16), wz_stage[:], ACT.Copy).then_inc(wz_high, 1)
                    act.wait_ge(x_in, 16)
                    for k in range(KT):
                        nc.scalar.activation(x_parts[:, 0, k].bitcast(F16), x_stage[:, k], ACT.Copy).then_inc(x_split_a, 1)
                    act.wait_ge(small_in, 64)
                    nc.scalar.activation(alog_sb[:], alog_sb[:], ACT.Exp).then_inc(ac, 1)
                    nc.scalar.activation(neg_rms[:], rms_raw[:], ACT.Copy, scale=-1.0)
                    act.wait_ge(dv, 2)
                    nc.scalar.activation(beta[0:96], work_a[0:96], ACT.Exp).then_inc(ac, 1)
                    act.wait_ge(dv, 4)
                    nc.scalar.activation(work_a[0:96], g_full[0:96], ACT.Abs).then_inc(ac, 1)
                    act.wait_ge(ac, 3)
                    nc.scalar.activation(work_a[0:96], work_a[0:96], ACT.Exp, scale=-1.0).then_inc(ac, 1)
                    act.wait_ge(ac, 4)
                    nc.scalar.activation(work_a[0:96], work_a[0:96], ACT.Ln, bias=1.0).then_inc(ac, 1)
                    for i in range(6):
                        act.wait_ge(cum_done, i + 1)
                        kind, half = i // 2, i % 2
                        dst = tables[:, half * (NIT // 2):(half + 1) * (NIT // 2), 1 + kind, :]
                        nc.scalar.activation(dst, bank[i][:].rearrange("p (a b) -> p a b", b=UN), ACT.Exp)\
                            .then_inc(exp_cum, 1)
                    for h in range(H):
                        act.wait_ge(w_in[h % 2], 16 * (h // 2 + 1))
                        if h >= 2:
                            act.wait_ge(w_stored[h % 2], 16 * (h // 2))
                        nc.scalar.activation(w_pair[h % 2][:, 0].bitcast(F16), w_stage[:, h % 2], ACT.Copy).then_inc(w_high, 1)

                @block.tensor
                def _(pe):
                    pe.wait_ge(x_split_b, KT)
                    pe.wait_ge(wz_low, 1)
                    for i in range(NB):
                        b, c0 = i // (NB // B), TAPS - 1 + (i % (NB // B)) * 512
                        first = True
                        for k in range(KT):
                            for wp, xp in ((0, 0), (0, 1), (1, 0)):
                                w = wz_parts[:, wp, k].bitcast(BF16 if wp else F16)
                                xx = x_parts[:, xp, k, b, c0:c0 + 512].bitcast(BF16 if xp else F16)
                                last = nc.tensor.matmul(bank[i][0:32, :], w, xx, start=first,
                                                        stop=(k == KT - 1 and wp == 1))
                                first = False
                        last.then_inc(zp_done, 1)
                    pe.wait_ge(dv, 12)
                    pe.wait_ge(zt_done, NB)
                    for i in range(6):
                        kind, half = i // 2, i % 2
                        w = (laterb, uptob, onesb)[kind]
                        rhs = g_parts[0:96, half * (NIT // 2):(half + 1) * (NIT // 2), :].rearrange("p a b -> p (a b)")
                        nc.tensor.matmul(bank[i][:], w[0:96, :], rhs, start=True, stop=True).then_inc(cum_done, 1)

                @block.vector
                def _(dve):
                    v = nc.vector
                    dve.wait_ge(wz_high, 1)
                    v.tensor_tensor(wz_parts[:, 1].bitcast(BF16), wz_stage[:], wz_parts[:, 0].bitcast(F16),
                                    ALU.subtract).then_inc(wz_low, 1)
                    for k in range(KT):
                        dve.wait_ge(x_split_a, k + 1)
                        v.tensor_tensor(x_parts[:, 1, k].bitcast(BF16), x_stage[:, k], x_parts[:, 0, k].bitcast(F16),
                                        ALU.subtract).then_inc(x_split_b, 1)
                    dve.wait_ge(consts_in, 32)
                    v.tensor_copy(ident16[:], cst[:, C_ID]).then_inc(casts, 1)
                    for u in range(4):
                        v.tensor_copy(rep16[:, u], cst[:, C_ID])
                    v.tensor_scalar(negid16[:], cst[:, C_ID], -1.0, None, ALU.mult)
                    v.tensor_copy(identb[:], cst[:, C_ID])
                    v.tensor_copy(negmask[:], cst[:, C_NEG])
                    v.tensor_copy(laterb[:], cst[:, C_LATER])
                    v.tensor_copy(uptob[:], cst[:, C_UPTO])
                    v.tensor_copy(onesb[:], cst[:, C_ONES])
                    v.tensor_copy(mask0t[:], cst[:, C_M0T])
                    v.memset(over_dh[:], 1.0 / DH)
                    v.memset(eps_dh[:], EPS_RMS * DH)
                    v.memset(beta[96:128], 0.0)
                    v.memset(g_parts[96:128], 0.0)
                    for i in range(NB):
                        dve.wait_ge(zp_done, i + 1)
                        v.tensor_copy(z_t[:, i * 512:(i + 1) * 512], bank[i][0:32, :]).then_inc(zt_done, 1)
                    dve.wait_ge(zt_done, NB)
                    v.transpose(z_rows, z_t).then_inc(tr_done, 1)
                    dve.wait_ge(tr_done, 1)
                    zv = z_rows.rearrange("p (b c j h) -> p b h c j", b=B, j=4, h=H)
                    for b in range(B):
                        for j in range(NH):
                            last = v.tensor_scalar(work_a[32 * j:32 * j + 32, b * H:(b + 1) * H, :], zv[:, b, :, :, j],
                                                   -1.0, 80.0, ALU.mult, ALU.min)
                            last = v.tensor_copy(g_full[32 * j:32 * j + 32, b * H:(b + 1) * H, :], zv[:, b, :, :, 3])
                    last.then_inc(dv, 2)
                    dve.wait_ge(ac, 2)
                    v.tensor_scalar(beta[0:96], beta[0:96], 1.0, None, ALU.add).then_inc(dv, 1)
                    dve.wait_ge(dv, 3)
                    v.reciprocal(beta[0:96], beta[0:96])
                    dve.wait_ge(small_in, 64)
                    dtb = dt_sb[:].rearrange("p (o h u) -> p o h u", o=1, u=1).broadcast_to([96, B, H, T // CH])
                    gv = g_full[0:96].rearrange("p (b h) c -> p b h c", b=B)
                    for b in range(B):
                        last = v.tensor_tensor(gv[:, b], gv[:, b], dtb[:, b], ALU.add)
                    last.then_inc(dv, 1)
                    dve.wait_ge(dv, 4)
                    v.tensor_scalar(beta[0:96], beta[0:96], 2.0, None, ALU.mult)
                    v.tensor_scalar(work_b[0:96], g_full[0:96], 0.0, None, ALU.max).then_inc(dv, 2)
                    dve.wait_ge(ac, 5)
                    dve.wait_ge(dv, 6)
                    v.tensor_tensor(work_a[0:96], work_a[0:96], work_b[0:96], ALU.add).then_inc(dv, 1)
                    dve.wait_ge(dv, 7)
                    ab = alog_sb[:].rearrange("p (h u) -> p h u", u=1).broadcast_to([96, H, T // CH])
                    wa = work_a[0:96].rearrange("p (b h) c -> p b h c", b=B)
                    for b in range(B):
                        last = v.tensor_tensor(gv[:, b], wa[:, b], ab, ALU.mult)
                    last.then_inc(dv, 1)
                    dve.wait_ge(dv, 8)
                    v.tensor_scalar(g_full[0:96], g_full[0:96], -1.0, None, ALU.mult).then_inc(dv, 1)
                    dve.wait_ge(dv, 9)
                    gp = g_parts[:].rearrange("p n u -> p (n u)")
                    gf = g_full[:].rearrange("p n u -> p (n u)")
                    gh = g_hi[:].rearrange("p n u -> p (n u)")
                    v.tensor_copy(gp[0:96], gf[0:96])
                    v.tensor_copy(gh[0:96], gf[0:96]).then_inc(dv, 1)
                    dve.wait_ge(dv, 10)
                    v.tensor_tensor(gf[0:96], gf[0:96], gh[0:96], ALU.subtract).then_inc(dv, 1)
                    dve.wait_ge(dv, 11)
                    v.tensor_copy(gp[32:64], gf[32:64])
                    v.tensor_copy(gh[64:96], gf[64:96]).then_inc(tr_done, 1)
                    dve.wait_ge(tr_done, 2)
                    v.tensor_tensor(gp[64:96], gf[64:96], gh[64:96], ALU.subtract).then_inc(dv, 1)
                    bt = beta[:].rearrange("p a (n u) -> p (a n) u", u=UN)
                    v.tensor_scalar(tables[:, :, 0, :], bt, -1.0, None, ALU.mult)
                    dve.wait_ge(exp_cum, 6)
                    v.tensor_tensor(tables[:, :, 1, :], tables[:, :, 1, :], bt, ALU.mult)
                    v.tensor_scalar(tables[:, :, 2, :], tables[:, :, 2, :], -1.0, None, ALU.mult).then_inc(dv, 1)
                    dve.wait_ge(dv, 13)
                    v.memset(tables[:, ::NTB, 2:4, 0:1], 0.0)

        with ExitStack() as loop_scope:
            scope = loop_scope
            x_cur = [sb(f"x_cur{p}", [P, 2, KT, PW + 1], U16) for p in range(2)]
            w_cur = [sb(f"w_cur{p}", [P, 2, KT, HC], U16) for p in range(2)]
            c_cur = [sb(f"c_cur{p}", [P, NCONV, TAPS], F32) for p in range(2)]
            t_cur = [sb(f"t_cur{p}", [P, 4, UN], F32) for p in range(2)]
            g_cur = [sb(f"g_cur{p}", [P, UN], BF16) for p in range(2)]
            kq_t = [sb(f"kq_t{p}", [P, UN, 4, CH], F32) for p in range(2)]
            k_rows = [sb(f"k_rows{p}", [P, UN, P], F32) for p in range(2)]
            v_rows = [sb(f"v_rows{p}", [P, UN, P], F32) for p in range(2)]
            inv_t = [sb(f"inv_t{p}", [P, UN, P], F32) for p in range(2)]
            gate = [sb(f"gate{p}", [P, TB], F32) for p in range(2)]
            squares = [sb(f"squares{p}", [P, UN, 4, CH], F32) for p in range(2)]
            y_buf = [sb(f"y_buf{p}", [P, TB], F32) for p in range(2)]
            v_t = sb("v_t", [P, UN, NH, CH], F32)
            conv_acc = [sb(f"conv_acc{i}", [P, TB], F32) for i in range(NCONV)]
            g_upto = sb("g_upto", [96, UN, CH], BF16)
            decay = [sb(f"decay{g}", [P, 4, P], F32) for g in range(2)]
            n_t = [sb(f"n_t{g}", [P, 4, P], F32) for g in range(2)]
            n_high = [sb(f"n_high{g}", [P, 4, P], F16) for g in range(2)]
            n_low = [sb(f"n_low{g}", [P, 4, P], BF16) for g in range(2)]
            inv = [sb(f"inv{g}", [P, 4, P], F16) for g in range(2)]
            invt = [sb(f"invt{g}", [P, 4, P], F16) for g in range(2)]
            xs = [sb(f"xs{g}", [P, 4, P], F16) for g in range(2)]
            sv = [sb(f"sv{p}", [P, UN], F32) for p in range(2)]
            k_sq = sb("k_sq", [P, UN], F32)
            ln_k = sb("ln_k", [P, UN], F32)
            ln_v = sb("ln_v", [P, TB], F32)
            eps_var = sb("eps_var", [P, 1], F32)
            r2 = sb("r2", [P, UN], F32)
            c_n = sb("c_n", [P, UN], F32)
            c_k = sb("c_k", [P, UN], F32)
            state = sb("state", [P, P], F32)
            rhs = [sb(f"rhs{i}", [P, P], F32) for i in range(2)]
            w_sol = [sb(f"w_sol{i}", [P, P], F32) for i in range(2)]
            o_sq = sb("o_sq", [P, TB], F32)
            rstd = sb("rstd", [P, TB], F32)
            o_norm = sb("o_norm", [P, TB], F32)

            loaded = [sem("loaded0"), sem("loaded1")]
            (projected, tap0, tap_step, tapped, silu_done, gate_done, squared, grammed, summed, small_step, small_done,
             g_made, decay_sum, decayed, n_made, high_made, low_made, l0_step, l0_made, l0_turned, inv_made, x_made,
             x_kept, y_made, merged, turned, turn_kept, k_turned, k_kept, v_turned, v_kept, res_made, res_kept,
             fix_made, fix_kept, ks_made, rhs_made, sol_made, sol_kept, out_made, upd_made, stated, osq_made,
             var_made, rstd_made, normed, gated, zeroed) = map(sem, (
                "projected", "tap0", "tap_step", "tapped", "silu_done", "gate_done", "squared", "grammed", "summed",
                "small_step", "small_done", "g_made", "decay_sum", "decayed", "n_made", "high_made", "low_made",
                "l0_step", "l0_made", "l0_turned", "inv_made", "x_made", "x_kept", "y_made", "merged", "turned",
                "turn_kept", "k_turned", "k_kept", "v_turned", "v_kept", "res_made", "res_kept", "fix_made",
                "fix_kept", "ks_made", "rhs_made", "sol_made", "sol_kept", "out_made", "upd_made", "stated",
                "osq_made", "var_made", "rstd_made", "normed", "gated", "zeroed"))
            merge_seen = sem("merge_seen")
            ln_made, norm_made, var_ln = sem("ln_made"), sem("norm_made"), sem("var_ln")
            stored = [sem("stored0"), sem("stored1")]
            LV = LEVELS - 1
            OUT = bank[7][:, 0:TB]
            VAR = bank[7][:, TB:2 * TB]
            KS = bank[6][:, 0:P]

            def iterate(eng, body):
                body(0, 0, True, False)
                body(1, 1, True, True)
                with eng.Fori(1, NIT // 2) as m:
                    body(2 * m, 0, True, True)
                    body(2 * m + 1, 1, True, True)
                body(NIT, 0, False, True)

            with nc.Block() as block:
                @block.sync
                def _(sp):
                    def load(n, p):
                        b, h, tb = n // (H * NTB), (n // NTB) % H, n % NTB
                        sp.dma_start(x_cur[p][:, :, :, 0:PW].rearrange("p a b c -> p (a b) c"),
                                     x_parts[:].rearrange("p a k b c -> p (a k) (b c)")[:, :, bass.ds(b * XW + tb * TB, PW)])\
                            .then_inc(loaded[p], 16)
                        sp.dma_start(w_cur[p][:].rearrange("p a b c -> p (a b c)"),
                                     w_dram.rearrange("h p c -> (h p) c")[bass.ds(h * P, P), :])\
                            .then_inc(loaded[p], 16)
                        sp.dma_start(c_cur[p][:].rearrange("p a b -> p (a b)"),
                                     conv_sb[:].rearrange("p h a b -> p (h a b)")[:, bass.ds(h * (NCONV * TAPS), NCONV * TAPS)])\
                            .then_inc(loaded[p], 16)
                        sp.dma_start(t_cur[p][:].rearrange("p a b -> p (a b)"),
                                     tables[:].rearrange("p n a b -> p (n a b)")[:, bass.ds(n * (4 * UN), 4 * UN)])\
                            .then_inc(loaded[p], 16)
                        sp.dma_start(g_cur[p][:], g_parts[:].rearrange("p n a -> p (n a)")[:, bass.ds(n * UN, UN)])\
                            .then_inc(loaded[p], 16)

                    def store(r, p):
                        sp.wait_ge(gated, r + 1)
                        sp.dma_start(y_dram.rearrange("n p t -> (n p) t")[bass.ds(r * P, P), :] if not isinstance(r, int)
                                     else y_dram[r], y_buf[p][:]).then_inc(stored[p], 16)

                    load(0, 0)
                    load(1, 1)

                    def body(n, p, prepare, recur):
                        if recur:
                            store(n - 1, 1 - p)
                        if recur and prepare:
                            pass

                    store(0, 0)
                    with sp.Fori(1, NIT // 2) as m:
                        sp.wait_ge(projected, NTILE * (2 * m - 1))
                        sp.wait_ge(stated, UN * (2 * m - 1))
                        load(2 * m, 0)
                        store(2 * m - 1, 1)
                        load(2 * m + 1, 1)
                        store(2 * m, 0)
                    store(NIT - 1, 1)
                    for p in range(2):
                        sp.wait_ge(stored[p], 16 * (NIT // 2))

                @block.tensor
                def _(pe):
                    mm = nc.tensor.matmul

                    def body(n, p, prepare, recur):
                        q, r = 1 - p, n - 1

                        def project(c):
                            if not prepare:
                                return
                            if c == 0:
                                pe.wait_ge(loaded[p], 80 * ((n - p) // 2 + 1) if isinstance(n, int) else 40 * (n - p) + 80)
                                at_least(pe, tapped, NCONV * n)
                            elif c == 1:
                                at_least(pe, gate_done, n)
                            else:
                                pe.wait_ge(tapped, NCONV * n + c - 1)
                            first = True
                            for k in range(KT):
                                for wp, xp in ((0, 0), (0, 1), (1, 0)):
                                    last = mm(bank[c % 2][:, 0:PW],
                                              w_cur[p][:, wp, k, c * P:(c + 1) * P].bitcast(BF16 if wp else F16),
                                              x_cur[p][:, xp, k, 0:PW].bitcast(BF16 if xp else F16),
                                              start=first, stop=(k == KT - 1 and wp == 1))
                                    first = False
                            last.then_inc(projected, 1)

                        def gram(g):
                            if not prepare:
                                return
                            pe.wait_ge(silu_done, NCONV * n + 4)
                            at_least(pe, v_kept, 2 * n - 1 + g)
                            for u in range(4):
                                a = kq_t[p][:, 4 * g + u].rearrange("p a b -> p (a b)")
                                last = mm(bank[2 + g][:, u * P:(u + 1) * P], a, a, start=True, stop=True)
                            last.then_inc(grammed, 1)

                        def norms():
                            if not prepare:
                                return
                            pe.wait_ge(squared, n + 1)
                            at_least(pe, fix_kept, 2 * n)
                            for u in range(UN):
                                last = mm(bank[5][:, u:u + 1], squares[p][:, u].rearrange("p a b -> p (a b)"),
                                          cst[:, C_ONES, 0:1], start=True, stop=True)
                            last.then_inc(summed, 1)

                        def decays(g):
                            if not prepare:
                                return
                            if g == 0:
                                pe.wait_ge(g_made, n + 1)
                            else:
                                pe.wait_ge(small_done, n + 1)
                            mm(bank[4 + g][:], laterb[0:96, :],
                               g_upto[:, 4 * g:4 * g + 4, None, :].broadcast_to([96, 4, 4, CH]),
                               start=True, stop=False)
                            mm(bank[4 + g][:], identb[:], negmask[:, None, :].broadcast_to([P, 4, P]),
                               start=False, stop=True).then_inc(decay_sum, 1)

                        def turn_keys(g):
                            if not prepare:
                                return
                            pe.wait_ge(n_made, UN * n + 4 * g + 4)
                            for u in range(4):
                                last = nc.tensor.transpose(bank[2 + g][:, u * P:(u + 1) * P],
                                                           kq_t[p][:, 4 * g + u].rearrange("p a b -> p (a b)"), cst[:, C_ID])
                            last.then_inc(k_turned, 1)

                        def turn_values(g):
                            if not prepare:
                                return
                            pe.wait_ge(k_kept, 2 * n + g + 1)
                            pe.wait_ge(silu_done, NCONV * n + NCONV)
                            for u in range(4):
                                last = nc.tensor.transpose(bank[2 + g][0:96, u * P:(u + 1) * P],
                                                           v_t[:, 4 * g + u].rearrange("p a b -> p (a b)"), cst[:, C_ID])
                            last.then_inc(v_turned, 1)

                        def turn(g, src):
                            dst = bank[4 + g][:].bitcast(F16)
                            for u in range(4):
                                last = nc.tensor.transpose(dst[:, u * P:(u + 1) * P], src[:, u], ident16[:])
                            return last

                        def turn0(g):
                            if not prepare:
                                return
                            pe.wait_ge(l0_made, 2 * n + g + 1)
                            turn(g, invt[g]).then_inc(l0_turned, 1)

                        def level_x(l, g):
                            if not prepare:
                                return
                            if l == 1:
                                pe.wait_ge(inv_made, 2 * n + g + 1)
                            else:
                                pe.wait_ge(turn_kept, 2 * LV * n + 2 * (l - 2) + g + 1)
                            for u in range(4):
                                last = mm(bank[4 + g][:, u * P:(u + 1) * P], n_high[g][:, u], inv[g][:, u], start=True, stop=True)
                            last.then_inc(x_made, 1)

                        def level_y(l, g):
                            if not prepare:
                                return
                            pe.wait_ge(x_kept, 2 * LV * n + 2 * (l - 1) + g + 1)
                            for u in range(4):
                                last = mm(bank[4 + g][:, u * P:(u + 1) * P], invt[g][:, u], xs[g][:, u], start=True, stop=True)
                            last.then_inc(y_made, 1)

                        def level_t(l, g):
                            if not prepare:
                                return
                            pe.wait_ge(merged, 2 * LV * n + 2 * (l - 1) + g + 1)
                            turn(g, inv[g]).then_inc(turned, 1)

                        def residual(g):
                            if not prepare:
                                return
                            pe.wait_ge(turn_kept, 2 * LV * n + 2 * (LV - 1) + g + 1)
                            pe.wait_ge(low_made, 2 * n + g + 1)
                            flat = bank[4 + g][:]
                            mm(flat, ident16[:], rep16[:].rearrange("p a b -> p (a b)"), start=True, stop=False)
                            mm(flat, negid16[:], inv[g][:].rearrange("p a b -> p (a b)"), start=False, stop=False)
                            for part in (n_high, n_low):
                                for u in range(4):
                                    last = mm(flat[:, u * P:(u + 1) * P], part[g][:, u], inv[g][:, u], start=False,
                                              stop=(part is n_low and u == 3))
                            last.then_inc(res_made, 1)

                        def fix(g):
                            if not prepare:
                                return
                            pe.wait_ge(res_kept, 2 * n + g + 1)
                            flat = bank[4 + g][:]
                            mm(flat, ident16[:], invt[g][:].rearrange("p a b -> p (a b)"), start=True, stop=False)
                            for u in range(4):
                                last = mm(flat[:, u * P:(u + 1) * P], xs[g][:, u], invt[g][:, u], start=False, stop=(u == 3))
                            last.then_inc(fix_made, 1)

                        def from_state(c):
                            if not recur:
                                return
                            if c == 0:
                                pe.wait_ge(fix_kept, 2 * r + 2)
                                pe.wait_ge(k_kept, 2 * r + 2)
                                at_least(pe, zeroed, 1)
                            at_least(pe, stated, UN * r + c)
                            mm(KS, kq_t[q][:, c].rearrange("p a b -> p (a b)"), state[:], start=True, stop=True)\
                                .then_inc(ks_made, 1)

                        def solve(c):
                            if not recur:
                                return
                            pe.wait_ge(rhs_made, UN * r + c + 1)
                            mm(KS, inv_t[q][:, c], rhs[c % 2][:], start=True, stop=True).then_inc(sol_made, 1)
                            if c == 0:
                                at_least(pe, normed, r)
                            mm(OUT[:, c * CH:(c + 1) * CH], rhs[c % 2][:], inv_t[q][:, c, 96:128], start=True,
                               stop=True).then_inc(out_made, 1)

                        def update(c):
                            if not recur:
                                return
                            pe.wait_ge(sol_kept, UN * r + c + 1)
                            mm(KS, k_rows[q][:, c], w_sol[c % 2][:], start=True, stop=True).then_inc(upd_made, 1)

                        def variance():
                            if not recur:
                                return
                            pe.wait_ge(osq_made, r + 1)
                            mm(VAR, over_dh[:], o_sq[:], start=True, stop=False)
                            mm(VAR, eps_dh[:], squares[q][:, :, 3, :], start=False, stop=True).then_inc(var_made, 1)

                        project(0)
                        project(1)
                        from_state(0)
                        project(2)
                        solve(0)
                        project(3)
                        update(0)
                        from_state(1)
                        gram(0)
                        gram(1)
                        solve(1)
                        norms()
                        update(1)
                        decays(0)
                        decays(1)
                        from_state(2)
                        turn_keys(0)
                        turn_keys(1)
                        solve(2)
                        turn0(0)
                        turn0(1)
                        update(2)
                        for l in range(1, LEVELS):
                            c = l + 2
                            for g in range(2):
                                level_x(l, g)
                            if c < UN:
                                from_state(c)
                            for g in range(2):
                                level_y(l, g)
                            if c < UN:
                                solve(c)
                            if l <= 4:
                                project(3 + l)
                            for g in range(2):
                                level_t(l, g)
                            if c < UN:
                                update(c)
                            if l == 5:
                                variance()
                        residual(0)
                        residual(1)
                        fix(0)
                        fix(1)
                        turn_values(0)
                        turn_values(1)

                    iterate(pe, body)

                @block.scalar
                def _(act):
                    a = nc.scalar.activation

                    def body(n, p, prepare, recur):
                        q, r = 1 - p, n - 1

                        def first_tap(c):
                            if not prepare:
                                return
                            if c == 0:
                                pass
                            act.wait_ge(projected, NTILE * n + c + 1)
                            a(conv_acc[c][:], bank[c % 2][:, 0:TB], ACT.Copy, scale=c_cur[p][:, c, 0:1]).then_inc(tap0, 1)

                        def silu(c):
                            if not prepare:
                                return
                            if c == 4:
                                at_least(act, v_turned, 2 * n)
                            act.wait_ge(tapped, NCONV * n + c + 1)
                            if c == 0:
                                dst = kq_t[p][:, :, 3, :]
                            elif c < 4:
                                dst = kq_t[p][:, :, c - 1, :]
                            else:
                                dst = v_t[:, :, c - 4, :]
                            a(dst, conv_acc[c][:].rearrange("p (u t) -> p u t", u=UN), ACT.Silu).then_inc(silu_done, 1)

                        def gate_silu():
                            if not prepare:
                                return
                            act.wait_ge(projected, NTILE * n + NTILE)
                            at_least(act, gated, n - 1)
                            a(gate[p][:], bank[1][:, TAPS - 1:PW], ACT.Silu).then_inc(gate_done, 1)

                        def exp_decay(g):
                            if not prepare:
                                return
                            at_least(act, n_made, UN * n)
                            act.wait_ge(decay_sum, 2 * n + g + 1)
                            a(decay[g][:].rearrange("p a b -> p (a b)"), bank[4 + g][:], ACT.Exp).then_inc(decayed, 1)

                        def key_norms():
                            if not prepare:
                                return
                            act.wait_ge(small_done, n + 1)
                            a(ln_k[:], k_sq[:], ACT.Ln).then_inc(ln_made, 1)
                            act.wait_ge(ln_made, n + 1)
                            a(sv[p][:], ln_k[:], ACT.Exp, scale=0.5).then_inc(norm_made, 1)

                        def root_variance():
                            if not recur:
                                return
                            act.wait_ge(var_made, r + 1)
                            act.wait_ge(zeroed, 1)
                            a(ln_v[:], VAR, ACT.Ln, bias=eps_var[:, 0:1]).then_inc(var_ln, 1)
                            act.wait_ge(var_ln, r + 1)
                            at_least(act, normed, r)
                            a(rstd[:], ln_v[:], ACT.Exp, scale=-0.5).then_inc(rstd_made, 1)

                        def high(g):
                            if not prepare:
                                return
                            act.wait_ge(n_made, UN * n + 4 * g + 4)
                            a(n_high[g][:], n_t[g][:], ACT.Copy).then_inc(high_made, 1)

                        def keep0(g):
                            if not prepare:
                                return
                            act.wait_ge(l0_turned, 2 * n + g + 1)
                            a(inv[g][:].rearrange("p a b -> p (a b)"), bank[4 + g][:].bitcast(F16)[:, 0:4 * P], ACT.Copy)\
                                .then_inc(inv_made, 1)

                        def keep_x(l, g):
                            if not prepare:
                                return
                            act.wait_ge(x_made, 2 * LV * n + 2 * (l - 1) + g + 1)
                            a(xs[g][:].rearrange("p a b -> p (a b)"), bank[4 + g][:], ACT.Copy).then_inc(x_kept, 1)

                        def keep_t(l, g):
                            if not prepare:
                                return
                            act.wait_ge(turned, 2 * LV * n + 2 * (l - 1) + g + 1)
                            a(invt[g][:].rearrange("p a b -> p (a b)"), bank[4 + g][:].bitcast(F16)[:, 0:4 * P], ACT.Copy)\
                                .then_inc(turn_kept, 1)

                        def keep_res(g):
                            if not prepare:
                                return
                            act.wait_ge(res_made, 2 * n + g + 1)
                            a(xs[g][:].rearrange("p a b -> p (a b)"), bank[4 + g][:], ACT.Copy).then_inc(res_kept, 1)

                        def keep_fix(g):
                            if not prepare:
                                return
                            act.wait_ge(fix_made, 2 * n + g + 1)
                            a(inv_t[p][:, 4 * g:4 * g + 4].rearrange("p a b -> p (a b)"), bank[4 + g][:], ACT.Copy)\
                                .then_inc(fix_kept, 1)

                        def keep_w(c):
                            if not recur:
                                return
                            act.wait_ge(sol_made, UN * r + c + 1)
                            a(w_sol[c % 2][:], KS, ACT.Copy).then_inc(sol_kept, 1)

                        def square_out():
                            if not recur:
                                return
                            act.wait_ge(out_made, UN * r + UN)
                            a(o_sq[:], OUT, ACT.Square).then_inc(osq_made, 1)

                        first_tap(0)
                        first_tap(1)
                        silu(0)
                        first_tap(2)
                        keep_w(0)
                        silu(1)
                        first_tap(3)
                        silu(2)
                        silu(3)
                        keep_w(1)
                        exp_decay(0)
                        exp_decay(1)
                        key_norms()
                        high(0)
                        high(1)
                        keep_w(2)
                        keep0(0)
                        keep0(1)
                        for l in range(1, LEVELS):
                            c = l + 2
                            for g in range(2):
                                keep_x(l, g)
                            if c < UN:
                                keep_w(c)
                            if l <= 3:
                                first_tap(3 + l)
                            for g in range(2):
                                keep_t(l, g)
                            if l == 5:
                                square_out()
                        root_variance()
                        keep_res(0)
                        keep_res(1)
                        silu(4)
                        silu(5)
                        silu(6)
                        keep_fix(0)
                        keep_fix(1)
                        gate_silu()

                    iterate(act, body)

                @block.vector
                def _(dve):
                    v = nc.vector
                    v.memset(state[:], 0.0)
                    v.memset(eps_var[:], EPS_RMS * DH * EPS_K)
                    for p in range(2):
                        last = v.memset(v_rows[p][96:128], 0.0)
                    last.then_inc(zeroed, 1)

                    def body(n, p, prepare, recur):
                        q, r = 1 - p, n - 1

                        def taps(c):
                            if not prepare:
                                return
                            acc = conv_acc[c][:]
                            dve.wait_ge(tap0, NCONV * n + c + 1)
                            for i in range(1, TAPS):
                                ins = v.scalar_tensor_tensor(acc, bank[c % 2][:, i:i + TB], c_cur[p][:, c, i:i + 1], acc,
                                                             ALU.mult, ALU.add)
                                if i < TAPS - 1:
                                    ins.then_inc(tap_step, 1)
                                    dve.wait_ge(tap_step, (TAPS - 2) * (NCONV * n + c) + i)
                                else:
                                    ins.then_inc(tapped, 1)

                        def small():
                            if not prepare:
                                return
                            dve.wait_ge(summed, n + 1)
                            at_least(dve, ln_made, n)
                            v.tensor_scalar(k_sq[:], bank[5][:, 0:UN], EPS_K, None, ALU.add).then_inc(small_done, 1)
                            dve.wait_ge(small_done, n + 1)
                            v.reciprocal(r2[:], k_sq[:]).then_inc(small_step, 1)
                            dve.wait_ge(small_step, 3 * n + 1)
                            v.tensor_tensor(c_n[:], r2[:], t_cur[p][:, 0, :], ALU.mult).then_inc(small_step, 1)
                            v.tensor_tensor(c_k[:], r2[:], t_cur[p][:, 1, :], ALU.mult).then_inc(small_step, 1)

                        def system(g):
                            if not prepare:
                                return
                            dve.wait_ge(small_step, 3 * n + 3)
                            dve.wait_ge(grammed, 2 * n + g + 1)
                            dve.wait_ge(decayed, 2 * n + g + 1)
                            at_least(dve, low_made, 2 * n)
                            for u in range(4):
                                v.scalar_tensor_tensor(n_t[g][:, u], bank[2 + g][:, u * P:(u + 1) * P],
                                                       c_n[:, 4 * g + u:4 * g + u + 1], decay[g][:, u],
                                                       ALU.mult, ALU.mult).then_inc(n_made, 1)

                        def level0(g):
                            if not prepare:
                                return
                            dve.wait_ge(high_made, 2 * n + g + 1)
                            at_least(dve, fix_made, 2 * n)
                            v.tensor_tensor(invt[g][:], n_high[g][:], mask0t[:, None, :].broadcast_to([P, 4, P]), ALU.mult)\
                                .then_inc(l0_step, 1)
                            dve.wait_ge(l0_step, 2 * n + g + 1)
                            v.tensor_tensor(invt[g][:], invt[g][:], rep16[:], ALU.add).then_inc(l0_made, 1)

                        def keep_k(g):
                            if not prepare:
                                return
                            dve.wait_ge(k_turned, 2 * n + g + 1)
                            v.tensor_tensor(k_rows[p][:, 4 * g:4 * g + 4], bank[2 + g][:].rearrange("p (a b) -> p a b", a=4),
                                            c_k[:, 4 * g:4 * g + 4, None].broadcast_to([P, 4, P]), ALU.mult).then_inc(k_kept, 1)

                        def keep_v(g):
                            if not prepare:
                                return
                            dve.wait_ge(v_turned, 2 * n + g + 1)
                            dve.wait_ge(norm_made, n + 1)
                            v.tensor_tensor(v_rows[p][0:96, 4 * g:4 * g + 4],
                                            bank[2 + g][0:96, :].rearrange("p (a b) -> p a b", a=4),
                                            sv[p][0:96, 4 * g:4 * g + 4, None].broadcast_to([96, 4, P]), ALU.mult).then_inc(v_kept, 1)

                        def merge(l, g):
                            if not prepare:
                                return
                            dve.wait_ge(y_made, 2 * LV * n + 2 * (l - 1) + g + 1)
                            dve.sem_inc(merge_seen, 1)
                            v.copy_predicated(inv[g][:], mask_sb[:, l, None, :].broadcast_to([P, 4, P]),
                                              bank[4 + g][:].rearrange("p (a b) -> p a b", a=4)).then_inc(merged, 1)

                        def right_side(c):
                            if not recur:
                                return
                            dve.wait_ge(ks_made, UN * r + c + 1)
                            if c == 0:
                                dve.wait_ge(v_kept, 2 * r + 2)
                            v.scalar_tensor_tensor(rhs[c % 2][:], KS, t_cur[q][:, 2, c:c + 1], v_rows[q][:, c],
                                                   ALU.mult, ALU.add).then_inc(rhs_made, 1)

                        def new_state(c):
                            if not recur:
                                return
                            dve.wait_ge(upd_made, UN * r + c + 1)
                            v.scalar_tensor_tensor(state[:], state[:], t_cur[q][:, 3, c:c + 1], KS,
                                                   ALU.mult, ALU.add).then_inc(stated, 1)

                        def normalize():
                            if not recur:
                                return
                            dve.wait_ge(rstd_made, r + 1)
                            at_least(dve, gated, r)
                            v.scalar_tensor_tensor(o_norm[:], OUT, neg_rms[:, 0:1], rstd[:], ALU.mult, ALU.mult)\
                                .then_inc(normed, 1)

                        taps(0)
                        right_side(0)
                        taps(1)
                        new_state(0)
                        taps(2)
                        taps(3)
                        right_side(1)
                        small()
                        new_state(1)
                        system(0)
                        system(1)
                        right_side(2)
                        level0(0)
                        level0(1)
                        keep_k(0)
                        keep_k(1)
                        new_state(2)
                        for l in range(1, LEVELS):
                            c = l + 2
                            if c < UN:
                                right_side(c)
                            merge(l, 0)
                            merge(l, 1)
                            if l <= 3:
                                taps(3 + l)
                            if c < UN:
                                new_state(c)
                        normalize()
                        keep_v(0)
                        keep_v(1)

                    iterate(dve, body)

                @block.gpsimd
                def _(pool):
                    def body(n, p, prepare, recur):
                        q, r = 1 - p, n - 1
                        if prepare:
                            pool.wait_ge(loaded[p], 80 * ((n - p) // 2 + 1) if isinstance(n, int) else 40 * (n - p) + 80)
                            at_least(pool, decay_sum, 2 * n)
                            nc.gpsimd.tensor_tensor(g_upto[:], g_cur[p][0:96, :, None].broadcast_to([96, UN, CH]),
                                                    uptob[0:96, None, 0:CH].broadcast_to([96, UN, CH]), ALU.mult)\
                                .then_inc(g_made, 1)
                            at_least(pool, var_made, n - 1)
                            pool.wait_ge(silu_done, NCONV * n + 4)
                            nc.gpsimd.tensor_tensor(squares[p][:], kq_t[p][:], kq_t[p][:], ALU.mult).then_inc(squared, 1)
                            for g in range(2):
                                pool.wait_ge(high_made, 2 * n + g + 1)
                                at_least(pool, res_made, 2 * n)
                                nc.gpsimd.tensor_tensor(n_low[g][:], n_t[g][:], n_high[g][:], ALU.subtract)\
                                    .then_inc(low_made, 1)
                        if recur:
                            pool.wait_ge(normed, r + 1)
                            pool.wait_ge(gate_done, r + 1)
                            if not (isinstance(r, int) and r < 2):
                                pool.wait_ge(stored[q], 16 * (r // 2) if isinstance(r, int) else 8 * (r - q))
                            nc.gpsimd.tensor_tensor(y_buf[q][:], o_norm[:], gate[q][:], ALU.mult).then_inc(gated, 1)

                    body(0, 0, True, False)
                    body(1, 1, True, True)
                    body(2, 0, True, True)
                    body(3, 1, True, True)
                    with pool.Fori(2, NIT // 2) as m:
                        body(2 * m, 0, True, True)
                        body(2 * m + 1, 1, True, True)
                    body(NIT, 0, False, True)

        attention_scope.close()
        experts(nc, ctx, bank, y_dram, x_rows, w_o, consts, gate_w, gate_b, up_w, up_b, gp_w, gp_b, down_w, down_b, out)


def experts(nc, ctx, bank, y_dram, x_rows, w_o, consts, gate_w, gate_b, up_w, up_b, gp_w, gp_b, down_w, down_b, out):
    def sem(name):
        return ctx.enter_context(nc.semaphore(name))

    def sb(name, shape, dt):
        return ctx.enter_context(nc.sbuf_tensor(name, shape, dt))

    wo = sb("wo", [P, H, D], F32)
    x2 = sb("x2", [P, NTT, D], F32)
    x2_parts = sb("x2_parts", [P, 2, KT, B * T], U16)
    y_in = [sb(f"y_in{i}", [P, H, P], F32) for i in range(2)]
    x_in_b = [sb(f"x_in{i}", [P, D], F32) for i in range(2)]
    xr = [sb(f"xr{i}", [P, D], F32) for i in range(2)]
    x2t = [sb(f"x2t{i}", [P, KT, P], F32) for i in range(2)]
    stats = sb("stats", [P, 6], F32)
    mv = sb("mv", [P, NTT, 2], F32)
    sd = sb("sd", [P, NTT], F32)
    rs = sb("rs", [P, NTT], F32)
    eps_ln = sb("eps_ln", [P, 1], F32)
    idf = sb("idf", [P, P], F32)
    gw = sb("gw", [P, KT, E], F32)
    gb = sb("gb", [P, E], F32)
    logits = sb("logits", [P, NTT, E], F32)
    top = sb("top", [P, NTT, 8], F32)
    topi = sb("topi", [P, NTT, 8], U32)
    topf = sb("topf", [P, NTT, 8], F32)
    prob = sb("prob", [P, NTT, E], F32)
    tmp = sb("tmp", [P, NTT, E], F32)
    pick = sb("pick", [P, NTT, E], F32)
    zsum = sb("zsum", [P, NTT], F32)
    idx = sb("idx", [P, E], F32)
    comb_t = [sb(f"comb_t{i}", [E, P], F32) for i in range(2)]
    dbias = sb("dbias", [E, D], F32)
    upb = sb("upb", [P, E, FT], F32)
    gpb = sb("gpb", [P, E, FT], F32)
    WCOL = max(KT * FP, FT * D)
    stage = sb("stage", [P, WCOL], F32)
    wparts = [[sb(f"ew{i}_{k}", [P, 2, WCOL], U16) for k in range(3)] for i in range(2)]
    u_sb = [sb(f"u_sb{i}", [P, 512], F32) for i in range(2)]
    prod = [sb(f"prod{i}", [P, 512], F32) for i in range(2)]
    h_sb = [sb(f"h_sb{i}", [P, 512], F32) for i in range(2)]
    h_hi = sb("h_hi", [P, FT, 512], F16)
    h_lo = sb("h_lo", [P, FT, 512], BF16)

    b_small = sem("b_small")
    y_ld = [sem("y_ld0"), sem("y_ld1")]
    (outp, added, st_made, ag_made, rs_made, x2_made, x2_turn, x2t_kept, x2_hi, x2_lo, logit, logit_kept) = map(sem, (
        "outp", "added", "st_made", "ag_made", "rs_made", "x2_made", "x2_turn", "x2t_kept", "x2_hi", "x2_lo", "logit",
        "logit_kept"))
    idx_set = sem("idx_set")
    sd_made = sem("sd_made")
    with nc.Block() as block:
        @block.sync
        def _(sp):
            for dst, src in ((wo[:].rearrange("p a b -> p (a b)"), w_o), (idf[:], consts[:, 0:P]),
                             (gw[:].rearrange("p a b -> p (a b)"), gate_w), (gb[:], gate_b), (dbias[:], down_b),
                             (upb[:].rearrange("p a b -> p (a b)"), up_b), (gpb[:].rearrange("p a b -> p (a b)"), gp_b)):
                sp.dma_start(dst, src).then_inc(b_small, 16)
            yv = y_dram.rearrange("(b h t) p c -> b t p h c", b=B, h=H)
            for i in range(NTT):
                b, tb, half = i // (NTT // B), (i % (NTT // B)) // 2, i % 2
                if i >= 2:
                    sp.wait_ge(outp, i - 1)
                    sp.wait_ge(added, i - 1)
                sp.dma_start(y_in[i % 2][:], yv[b, tb, :, :, half * P:(half + 1) * P]).then_inc(y_ld[i % 2], 16)
                sp.dma_start(x_in_b[i % 2][:], x_rows[i * P:(i + 1) * P, :]).then_inc(y_ld[i % 2], 16)

        @block.gpsimd
        def _(pool):
            nc.gpsimd.memset(eps_ln[:], EPS_LN).then_inc(idx_set, 1)
            nc.gpsimd.iota(topi[:, 0, :], pattern=[[1, E]], base=0, channel_multiplier=0).then_inc(idx_set, 1)
            pool.wait_ge(idx_set, 2)
            nc.gpsimd.tensor_copy(idx[:], topi[:, 0, :]).then_inc(idx_set, 1)
            for i in range(NTT):
                pool.wait_ge(x2_hi, i + 1)
                nc.gpsimd.tensor_tensor(x2_parts[:, 1, :, i * P:(i + 1) * P].bitcast(BF16), x2t[i % 2][:],
                                        x2_parts[:, 0, :, i * P:(i + 1) * P].bitcast(F16), ALU.subtract).then_inc(x2_lo, 1)

        @block.scalar
        def _(act):
            act.wait_ge(idx_set, 2)

            def deviation(i):
                act.wait_ge(ag_made, i + 1)
                nc.scalar.activation(sd[:, i:i + 1], mv[:, i, 1:2], ACT.Sqrt, bias=eps_ln[:, 0:1]).then_inc(sd_made, 1)

            deviation(0)
            for i in range(NTT):
                if i + 1 < NTT:
                    deviation(i + 1)
                act.wait_ge(x2_turn, i + 1)
                if i >= 2:
                    act.wait_ge(x2_lo, i - 1)
                    act.wait_ge(logit, i - 1)
                nc.scalar.activation(x2t[i % 2][:].rearrange("p a b -> p (a b)"), bank[2 + i % 2][:, 0:D], ACT.Copy).then_inc(x2t_kept, 1)
                act.wait_ge(x2t_kept, i + 1)
                nc.scalar.activation(x2_parts[:, 0, :, i * P:(i + 1) * P].bitcast(F16), x2t[i % 2][:], ACT.Copy).then_inc(x2_hi, 1)
                act.wait_ge(logit, i + 1)
                nc.scalar.activation(logits[:, i], bank[4 + i % 2][:, 0:E], ACT.Copy).then_inc(logit_kept, 1)

        @block.tensor
        def _(pe):
            mm = nc.tensor.matmul

            def project(i):
                pe.wait_ge(y_ld[i % 2], 32 * (i // 2 + 1))
                if i == 0:
                    pe.wait_ge(b_small, 112)
                if i >= 2:
                    pe.wait_ge(added, i - 1)
                for h in range(H):
                    last = mm(bank[i % 2][:, 0:D], y_in[i % 2][:, h], wo[:, h], start=(h == 0), stop=(h == H - 1))
                last.then_inc(outp, 1)

            def route(i):
                pe.wait_ge(x2_made, i + 1)
                if i >= 2:
                    pe.wait_ge(x2t_kept, i - 1)
                for k in range(KT):
                    last = nc.tensor.transpose(bank[2 + i % 2][:, k * P:(k + 1) * P], x2[:, i, k * P:(k + 1) * P], idf[:])
                last.then_inc(x2_turn, 1)
                pe.wait_ge(x2t_kept, i + 1)
                if i >= 2:
                    pe.wait_ge(logit_kept, i - 1)
                for k in range(KT):
                    last = mm(bank[4 + i % 2][:, 0:E], x2t[i % 2][:, k], gw[:, k], start=(k == 0), stop=(k == KT - 1))
                last.then_inc(logit, 1)

            project(0)
            for i in range(NTT):
                if i + 1 < NTT:
                    project(i + 1)
                route(i)

        @block.vector
        def _(dve):
            v = nc.vector

            def scale_rows(i):
                dve.wait_ge(sd_made, i + 1)
                v.reciprocal(rs[:, i:i + 1], sd[:, i:i + 1]).then_inc(rs_made, 1)
                dve.wait_ge(rs_made, i + 1)
                v.tensor_scalar(x2[:, i], xr[i % 2][:], mv[:, i, 0:1], rs[:, i:i + 1], ALU.subtract, ALU.mult)\
                    .then_inc(x2_made, 1)

            for i in range(NTT):
                dve.wait_ge(outp, i + 1)
                dve.wait_ge(y_ld[i % 2], 32 * (i // 2 + 1))
                v.tensor_tensor(xr[i % 2][:], bank[i % 2][:, 0:D], x_in_b[i % 2][:], ALU.add).then_inc(added, 1)
                dve.wait_ge(added, i + 1)
                v.bn_stats(stats[:], xr[i % 2][:]).then_inc(st_made, 1)
                dve.wait_ge(st_made, i + 1)
                v.bn_aggr(mv[:, i], stats[:]).then_inc(ag_made, 1)
                if i:
                    scale_rows(i - 1)
            scale_rows(NTT - 1)

    rt, ra, r_top, comb_turn, comb_kept, bias_made, acc_made = map(sem, (
        "route_dve", "route_act", "route_top", "comb_turn", "comb_kept", "bias_made", "acc_made"))
    with nc.Block() as block:
        @block.scalar
        def _(act):
            act.wait_ge(rt, 3)
            nc.scalar.activation(prob[:], tmp[:], ACT.Exp).then_inc(ra, 1)
            for i in range(NTT):
                act.wait_ge(comb_turn, i + 1)
                if i >= 2:
                    act.wait_ge(bias_made, i - 1)
                nc.scalar.activation(comb_t[i % 2][:], bank[i % 2][0:E, 0:P], ACT.Copy).then_inc(comb_kept, 1)

        @block.tensor
        def _(pe):
            pe.wait_ge(rt, 13)
            for i in range(NTT):
                if i >= 2:
                    pe.wait_ge(comb_kept, i - 1)
                nc.tensor.transpose(bank[i % 2][0:E, 0:P], pick[:, i], idf[:]).then_inc(comb_turn, 1)
                pe.wait_ge(comb_kept, i + 1)
                if i >= 2:
                    pe.wait_ge(acc_made, i - 1)
                nc.tensor.matmul(bank[2 + i % 2][:, 0:D], comb_t[i % 2][:], dbias[:], start=True, stop=True).then_inc(bias_made, 1)

        @block.vector
        def _(dve):
            v = nc.vector

            def step(ins, value):
                ins.then_inc(rt, 1)
                dve.wait_ge(rt, value)
            step(v.tensor_tensor(logits[:], logits[:], gb[:, None, :].broadcast_to([P, NTT, E]), ALU.add), 1)
            step(v.tensor_reduce(zsum[:], logits[:], AX.X, ALU.max), 2)
            step(v.tensor_tensor(tmp[:], logits[:], zsum[:, :, None].broadcast_to([P, NTT, E]), ALU.subtract), 3)
            dve.wait_ge(ra, 1)
            step(v.tensor_reduce(zsum[:], prob[:], AX.X, ALU.add), 4)
            step(v.reciprocal(zsum[:], zsum[:]), 5)
            step(v.tensor_tensor(prob[:], prob[:], zsum[:, :, None].broadcast_to([P, NTT, E]), ALU.mult), 6)
            for i in range(NTT):
                v.max(top[:, i], prob[:, i]).then_inc(r_top, 1)
            dve.wait_ge(r_top, NTT)
            for i in range(NTT):
                v.max_index(topi[:, i], top[:, i], prob[:, i]).then_inc(r_top, 1)
            dve.wait_ge(r_top, 2 * NTT)
            step(v.tensor_copy(topf[:], topi[:]), 7)
            ib = idx[:, None, :].broadcast_to([P, NTT, E])
            v.tensor_tensor(pick[:], ib, topf[:, :, 0:1].broadcast_to([P, NTT, E]), ALU.is_equal)
            step(v.tensor_tensor(tmp[:], ib, topf[:, :, 1:2].broadcast_to([P, NTT, E]), ALU.is_equal), 8)
            step(v.tensor_tensor(pick[:], pick[:], tmp[:], ALU.add), 9)
            step(v.tensor_tensor(zsum[:], top[:, :, 0], top[:, :, 1], ALU.add), 10)
            v.tensor_tensor(pick[:], pick[:], prob[:], ALU.mult)
            step(v.tensor_scalar(zsum[:], zsum[:], 1e-20, None, ALU.add), 11)
            step(v.reciprocal(zsum[:], zsum[:]), 12)
            step(v.tensor_tensor(pick[:], pick[:], zsum[:, :, None].broadcast_to([P, NTT, E]), ALU.mult), 13)
            for i in range(NTT):
                dve.wait_ge(bias_made, i + 1)
                v.tensor_tensor(x2[:, i], bank[2 + i % 2][:, 0:D], x2[:, i], ALU.add).then_inc(acc_made, 1)

    w_in = sem("ew_in")
    (w_hi, w_lo, ups, gates, u_kept, prods, h_made, h_high, h_low, downs, accs) = map(sem, (
        "ew_hi", "ew_lo", "ups", "gates", "u_kept", "prods", "h_made", "h_high", "h_low", "downs", "accs"))
    srcs = (up_w, gp_w, down_w)
    with nc.Block() as block:
        def width(k):
            return KT * FP if k < 2 else FT * D

        @block.sync
        def _(sp):
            for e in range(E):
                for k in range(3):
                    if e or k:
                        sp.wait_ge(w_lo, 3 * e + k)
                    sp.dma_start(stage[:, 0:width(k)], srcs[k][e]).then_inc(w_in, 16)

        @block.gpsimd
        def _(pool):
            def split(e):
                i = e % 2
                for k in range(3):
                    if e >= 2:
                        pool.wait_ge(downs, 4 * NB * (e - 1))
                    pool.wait_ge(w_in, 16 * (3 * e + k + 1))
                    nc.gpsimd.tensor_copy(wparts[i][k][:, 0, 0:width(k)].bitcast(F16), stage[:, 0:width(k)]).then_inc(w_hi, 1)
                    pool.wait_ge(w_hi, 3 * e + k + 1)
                    nc.gpsimd.tensor_tensor(wparts[i][k][:, 1, 0:width(k)].bitcast(BF16), stage[:, 0:width(k)],
                                            wparts[i][k][:, 0, 0:width(k)].bitcast(F16), ALU.subtract).then_inc(w_lo, 1)

            for e in range(E):
                split(e)

        @block.tensor
        def _(pe):
            mm = nc.tensor.matmul

            def three(out_ap, w, x, start, stop):
                pairs = ((0, 0), (0, 1), (1, 0))
                for j, (wp, xp) in enumerate(pairs):
                    last = mm(out_ap, w(wp), x(xp), start=(start and j == 0), stop=(stop and j == 2))
                return last

            for e in range(E):
                i = e % 2
                wu, wg, wd = wparts[i]
                pe.wait_ge(w_lo, 3 * e + 3)
                with pe.Fori(0, NB) as tb:
                    n = tb + e * NB
                    for f in range(FT):
                        m = P
                        ff = FT * n + f
                        for which, w in ((0, wu), (1, wg)):
                            b = bank[2 * (f % 2) + which]
                            if f >= 2 or e:
                                pe.wait_ge(prods, ff - 1)
                            for k in range(KT):
                                last = three(b[0:m, :],
                                             lambda wp: w[:, wp, k * FP + f * P:k * FP + f * P + m].bitcast(BF16 if wp else F16),
                                             lambda xp: x2_parts[:, xp, k, bass.ds(tb * 512, 512)].bitcast(BF16 if xp else F16),
                                             k == 0, k == KT - 1)
                            last.then_inc(ups if which == 0 else gates, 1)
                    pe.wait_ge(h_low, FT * (n + 1))
                    for s in range(4):
                        b = bank[4 + s]
                        if e:
                            pe.wait_ge(accs, 4 * (n - 1) + s + 1)
                        for f in range(FT):
                            m = P
                            last = three(b[:, 0:D],
                                         lambda hp: (h_lo if hp else h_hi)[0:m, f, s * P:(s + 1) * P],
                                         lambda wp: wd[0:m, wp, f * D:(f + 1) * D].bitcast(BF16 if wp else F16),
                                         f == 0, f == FT - 1)
                        last.then_inc(downs, 1)

        @block.scalar
        def _(act):
            a = nc.scalar.activation
            for e in range(E):
                with act.Fori(0, NB) as tb:
                    n = tb + e * NB

                    def silu(f):
                        m = P
                        act.wait_ge(prods, FT * n + f + 1)
                        if f >= 2 or e:
                            act.wait_ge(h_low, FT * n + f - 1)
                        a(h_sb[f % 2][0:m, :], prod[f % 2][0:m, :], ACT.Silu).then_inc(h_made, 1)
                        if f == 0 and e:
                            act.wait_ge(downs, 4 * n)
                        act.wait_ge(h_made, FT * n + f + 1)
                        a(h_hi[0:m, f, :], h_sb[f % 2][0:m, :], ACT.Copy).then_inc(h_high, 1)

                    for f in range(FT):
                        m = P
                        act.wait_ge(ups, FT * n + f + 1)
                        if f >= 2 or e:
                            act.wait_ge(prods, FT * n + f - 1)
                        a(u_sb[f % 2][0:m, :], bank[2 * (f % 2)][0:m, :], ACT.Identity, bias=upb[0:m, e, f:f + 1]).then_inc(u_kept, 1)
                        if f:
                            silu(f - 1)
                    silu(FT - 1)

        @block.vector
        def _(dve):
            v = nc.vector
            for e in range(E):
                with dve.Fori(0, NB) as tb:
                    n = tb + e * NB

                    def low(f):
                        m = P
                        dve.wait_ge(h_high, FT * n + f + 1)
                        v.tensor_tensor(h_lo[0:m, f, :], h_sb[f % 2][0:m, :], h_hi[0:m, f, :], ALU.subtract).then_inc(h_low, 1)

                    for f in range(FT):
                        m = P
                        dve.wait_ge(u_kept, FT * n + f + 1)
                        dve.wait_ge(gates, FT * n + f + 1)
                        if f >= 2 or e:
                            dve.wait_ge(h_made, FT * n + f - 1)
                        v.scalar_tensor_tensor(prod[f % 2][0:m, :], bank[2 * (f % 2) + 1][0:m, :], gpb[0:m, e, f:f + 1],
                                               u_sb[f % 2][0:m, :], ALU.add, ALU.mult).then_inc(prods, 1)
                        if f:
                            low(f - 1)
                    low(FT - 1)
                    for s in range(4):
                        dve.wait_ge(downs, 4 * n + s + 1)
                        acc = x2[:].rearrange("p a b -> p (a b)")[:, bass.ds((tb * 4 + s) * D, D)]
                        w = pick[:].rearrange("p a b -> p (a b)")[:, bass.ds((tb * 4 + s) * E + e, 1)]
                        v.scalar_tensor_tensor(acc, bank[4 + s][:, 0:D], w, acc, ALU.mult, ALU.add).then_inc(accs, 1)

    o_buf = [sb(f"o_buf{i}", [P, D], F32) for i in range(2)]
    f_stats = [sb(f"f_stats{i}", [P, 6], F32) for i in range(2)]
    f_st, f_ag, f_sd, f_rs, f_made = map(sem, ("f_st", "f_ag", "f_sd", "f_rs", "f_made"))
    f_out = [sem("f_out0"), sem("f_out1")]
    with nc.Block() as block:
        @block.sync
        def _(sp):
            for i in range(NTT):
                sp.wait_ge(f_made, i + 1)
                sp.dma_start(out[i * P:(i + 1) * P, :], o_buf[i % 2][:]).then_inc(f_out[i % 2], 16)
            for i in range(2):
                sp.wait_ge(f_out[i], 16 * (NTT // 2))

        @block.scalar
        def _(act):
            act.wait_ge(f_ag, NTT)
            nc.scalar.activation(sd[:], mv[:, :, 1], ACT.Sqrt, bias=eps_ln[:, 0:1]).then_inc(f_sd, 1)

        @block.vector
        def _(dve):
            v = nc.vector
            for i in range(NTT):
                if i >= 2:
                    dve.wait_ge(f_ag, i - 1)
                v.bn_stats(f_stats[i % 2][:], x2[:, i]).then_inc(f_st, 1)
                dve.wait_ge(f_st, i + 1)
                v.bn_aggr(mv[:, i], f_stats[i % 2][:]).then_inc(f_ag, 1)
            dve.wait_ge(f_sd, 1)
            v.reciprocal(rs[:], sd[:]).then_inc(f_rs, 1)
            dve.wait_ge(f_rs, 1)
            for i in range(NTT):
                if i >= 2:
                    dve.wait_ge(f_out[i % 2], 16 * (i // 2))
                v.tensor_scalar(o_buf[i % 2][:], x2[:, i], mv[:, i, 0:1], rs[:, i:i + 1], ALU.subtract, ALU.mult)\
                    .then_inc(f_made, 1)






def kernel(**inputs):
    import concourse.bacc as _bacc
    from concourse.bass_utils import run_bass_kernel_spmd as _run

    g = {k.replace("L0_attn_", "a_").replace("L0_ffn_", "f_"): np.asarray(v) for k, v in inputs.items()}
    x = g["a_x"]
    xt = np.zeros((P, KT, B, XW), np.float32)
    xt[:, :, :, TAPS - 1:TAPS - 1 + T] = x.reshape(B, T, KT, P).transpose(3, 2, 0, 1)

    def heads(w, n):
        return w.reshape(KT, P, n, H, DH).transpose(3, 1, 0, 2, 4)
    w_all = np.concatenate([heads(g["a_Wq"], 1), heads(g["a_Wk"], NH), heads(g["a_Wv"], NH), heads(g["a_Wg"], 1)], 3)
    wz = np.concatenate([g["a_Wb"], g["a_Wa"]], 1).reshape(KT, P, 32).transpose(1, 0, 2)

    def convs(w, n):
        return w.reshape(n, H, DH, TAPS).transpose(2, 1, 0, 3)
    cw = np.concatenate([convs(g["a_conv_q"], 1), convs(g["a_conv_k"], NH), convs(g["a_conv_v"], NH)], 2)
    consts, masks = constants()

    def padded(b):
        z = np.zeros((E, FT * P), np.float32)
        z[:, :F] = b
        return z.reshape(E, FT, P).transpose(2, 0, 1).reshape(P, E * FT)
    dw = np.zeros((E, FT * P, D), np.float32)
    dw[:, :F] = g["f_down_w"].transpose(0, 2, 1)

    def up(w):
        z = np.zeros((E, D, FP), np.float32)
        z[:, :, :F] = w.transpose(0, 2, 1)
        return z.reshape(E, KT, P, FP).transpose(0, 2, 1, 3).reshape(E, P, KT * FP)
    arrays = {
        "x_t": xt.reshape(P, -1), "x_rows": x.reshape(B * T, D), "w_all": w_all.reshape(H, P, KT * HC),
        "w_z": wz.reshape(P, -1), "conv_w": cw.reshape(P, -1),
        "a_log": np.broadcast_to(g["a_A_log"][None], (96, H)), "dt_bias": np.broadcast_to(g["a_dt_bias"][None], (96, H)),
        "rms_w": g["a_rms_weight"].reshape(P, 1),
        "w_o": g["a_Wo"].reshape(H, DH, D).transpose(1, 0, 2).reshape(P, H * D), "consts": consts, "masks": masks,
        "gate_w": g["f_gate_w"].T.reshape(KT, P, E).transpose(1, 0, 2).reshape(P, KT * E),
        "gate_b": np.broadcast_to(g["f_gate_b"][None], (P, E)),
        "up_w": up(g["f_up_w"]), "up_b": padded(g["f_up_b"]), "gp_w": up(g["f_gp_w"]), "gp_b": padded(g["f_gp_b"]),
        "down_w": dw.reshape(E, FT, P, D).transpose(0, 2, 1, 3).reshape(E, P, FT * D), "down_b": g["f_down_b"],
    }
    nc = _bacc.Bacc("TRN2", target_bir_lowering=False, num_devices=1)
    args, feed = [], {}
    for name, a in arrays.items():
        a = np.ascontiguousarray(a)
        feed["in_" + name] = a
        args.append(nc.dram_tensor("in_" + name, a.shape, mybir.dt.from_np(a.dtype), kind="ExternalInput").ap())
    args.append(nc.dram_tensor("out_y", (B * T, D), F32, kind="ExternalOutput").ap())
    build(nc, *args)
    r = _run(nc, [feed], core_ids=[0])
    return r.results[0]["out_y"].reshape(B, T, D)
```

```python
from contextlib import ExitStack

import numpy as np
import concourse.bass as bass
from concourse import mybir

F32 = mybir.dt.float32
F16 = mybir.dt.float16
BF16 = mybir.dt.bfloat16
U16 = mybir.dt.uint16
U32 = mybir.dt.uint32
ALU = mybir.AluOpType
ACT = mybir.ActivationFunctionType
AX = mybir.AxisListType

P = 128
B, T, D = 2, 2048, 256
KT = D // P
H, NH, DH = 8, 3, 128
TAPS = 4
CH = 32
UN = 8
TB = CH * UN
NTB = T // TB
NIT = B * H * NTB
XW = T + TAPS
PW = TB + TAPS - 1
NTILE = 2 * NH + 2
NCONV = NTILE - 1
HC = NTILE * DH
LEVELS = 7
E, F = 8, 816
FT = -(-F // P)
FP = FT * P
NTT = B * T // P
NB = B * T // 512
RING = 3
STAGES = 4
PEELED = 5
MASKED = -30000.0
EPS_K, EPS_RMS, EPS_LN = 1e-6, 1e-5, 1e-5



def constants():
    p = np.arange(P)
    j, t = p // CH, p % CH
    o = 4 * t + j
    before = (o[:, None] < o[None, :]) & (j[:, None] < NH)
    neg = np.where(before, 0.0, MASKED).astype(np.float32)
    masks = []
    for l in range(LEVELS):
        later, earlier = o[:, None], o[None, :]
        masks.append(((later >> (l + 1)) == (earlier >> (l + 1))) & ((later >> l) & 1 == 1) & ((earlier >> l) & 1 == 0))
    masks = np.stack(masks, 1).astype(np.uint16)
    m0t = masks[:, 0, :].T.astype(np.float32)
    later_t = (t[:, None] > t[None, :]).astype(np.float32)
    upto_t = (t[:, None] <= t[None, :]).astype(np.float32)
    ident = np.eye(P, dtype=np.float32)
    ones = np.ones((P, P), np.float32)
    c = np.concatenate([ident, neg, later_t, upto_t, m0t, ones], 1)
    return c, np.ascontiguousarray(masks.reshape(P, LEVELS * P))


C_ID, C_NEG, C_LATER, C_UPTO, C_M0T, C_ONES = range(6)


def at_least(eng, sem, value):
    if isinstance(value, int) and value <= 0:
        return
    eng.wait_ge(sem, value)


def build(nc, x_t, x_rows, w_all, w_z, conv_w, a_log, dt_bias, rms_w, w_o, consts, masks,
          gate_w, gate_b, up_w, up_b, gp_w, gp_b, down_w, down_b, out):
    y_dram = nc.dram_tensor("y_scratch", (NIT, P, TB), F32).ap()
    w_dram = nc.dram_tensor("w_parts_scratch", (H, P, 2 * KT * HC), U16).ap()
    ctx = ExitStack()
    with ctx:
        def sem(name):
            return ctx.enter_context(nc.semaphore(name))

        attention_scope = ExitStack()
        scope = attention_scope

        def sb(name, shape, dt):
            return scope.enter_context(nc.sbuf_tensor(name, shape, dt))

        bank = [ctx.enter_context(nc.psum_tensor(f"bank{i}", [P, 512], F32)) for i in range(8)]

        cst = sb("cst", [P, 6, P], F32)
        x_parts = sb("x_parts", [P, 2, KT, B, XW], U16)
        tables = sb("tables", [P, NIT, 4, UN], F32)
        g_parts = sb("g_parts", [P, NIT, UN], BF16)
        conv_sb = sb("conv_sb", [P, H, NCONV, TAPS], F32)
        ident16 = sb("ident16", [P, P], F16)
        rep16 = sb("rep16", [P, 4, P], F16)
        negid16 = sb("negid16", [P, P], F16)
        identb = sb("identb", [P, P], BF16)
        negmask = sb("negmask", [P, P], BF16)
        laterb = sb("laterb", [P, P], BF16)
        uptob = sb("uptob", [P, P], BF16)
        onesb = sb("onesb", [P, P], BF16)
        mask0t = sb("mask0t", [P, P], F16)
        mask_sb = sb("mask_sb", [P, LEVELS, P], U16)
        neg_rms = sb("neg_rms", [P, 1], F32)
        rms_raw = sb("rms_raw", [P, 1], F32)
        over_dh = sb("over_dh", [P, P], F32)
        eps_dh = sb("eps_dh", [P, P], F32)

        with ExitStack() as setup_scope:
            scope = setup_scope
            x_stage = sb("x_stage", [P, KT, B, XW], F32)
            w_stage = sb("w_stage", [P, 2, KT, HC], F32)
            w_pair = [sb(f"w_pair{i}", [P, 2, KT, HC], U16) for i in range(2)]
            wz_stage = sb("wz_stage", [P, KT, 32], F32)
            wz_parts = sb("wz_parts", [P, 2, KT, 32], U16)
            x_flat = x_stage[0:32].rearrange("p a b c -> p (a b c)")
            z_t, z_rows = x_flat[:, 0:B * T], x_flat[:, B * T:2 * B * T]
            beta = sb("beta", [P, B * H, T // CH], F32)
            g_full = sb("g_full", [P, B * H, T // CH], F32)
            work_a = sb("work_a", [P, B * H, T // CH], F32)
            work_b = sb("work_b", [P, B * H, T // CH], F32)
            g_hi = sb("g_hi", [P, B * H, T // CH], BF16)
            alog_sb = sb("alog_sb", [96, H], F32)
            dt_sb = sb("dt_sb", [96, H], F32)
            consts_in, x_in, z_in, small_in, x_split_a, x_split_b = map(
                sem, ("consts_in", "x_in", "z_in", "small_in", "x_highs", "x_lows"))
            w_in = [sem("w_in0"), sem("w_in1")]
            w_stored = [sem("w_stored0"), sem("w_stored1")]
            w_high, w_low, wz_high, wz_low = map(sem, ("w_high", "w_low", "wz_high", "wz_low"))
            zp_done, zt_done, tr_done, dv, ac, cum_done, casts, exp_cum = map(
                sem, ("z_projected", "z_evacuated", "z_turned", "setup_dve", "setup_act", "sums_done",
                      "consts_cast", "sums_exp"))
            with nc.Block() as block:
                @block.sync
                def _(sp):
                    sp.dma_start(x_stage[:].rearrange("p a b c -> p (a b c)"), x_t).then_inc(x_in, 16)
                    sp.dma_start(wz_stage[:].rearrange("p a b -> p (a b)"), w_z).then_inc(z_in, 16)
                    sp.dma_start(cst[:].rearrange("p a b -> p (a b)"), consts).then_inc(consts_in, 16)
                    sp.dma_start(mask_sb[:].rearrange("p a b -> p (a b)"), masks).then_inc(consts_in, 16)
                    sp.dma_start(conv_sb[:].rearrange("p a b c -> p (a b c)"), conv_w).then_inc(small_in, 16)
                    sp.dma_start(alog_sb[:], a_log).then_inc(small_in, 16)
                    sp.dma_start(dt_sb[:], dt_bias).then_inc(small_in, 16)
                    sp.dma_start(rms_raw[:], rms_w).then_inc(small_in, 16)
                    def load_head(h):
                        sp.dma_start(w_stage[:, h % 2].rearrange("p a b -> p (a b)"), w_all[h]).then_inc(w_in[h % 2], 16)

                    load_head(0)
                    load_head(1)
                    for h in range(H):
                        sp.wait_ge(w_low, h + 1)
                        sp.dma_start(w_dram[h], w_pair[h % 2][:].rearrange("p a b c -> p (a b c)")).then_inc(w_stored[h % 2], 16)
                        if h + 2 < H:
                            load_head(h + 2)
                    for i in range(2):
                        sp.wait_ge(w_stored[i], 16 * (H // 2))

                @block.gpsimd
                def _(pool):
                    for h in range(H):
                        pool.wait_ge(w_high, h + 1)
                        nc.gpsimd.tensor_tensor(w_pair[h % 2][:, 1].bitcast(BF16), w_stage[:, h % 2],
                                                w_pair[h % 2][:, 0].bitcast(F16), ALU.subtract).then_inc(w_low, 1)

                @block.scalar
                def _(act):
                    act.wait_ge(z_in, 16)
                    nc.scalar.activation(wz_parts[:, 0].bitcast(F16), wz_stage[:], ACT.Copy).then_inc(wz_high, 1)
                    act.wait_ge(x_in, 16)
                    for k in range(KT):
                        nc.scalar.activation(x_parts[:, 0, k].bitcast(F16), x_stage[:, k], ACT.Copy).then_inc(x_split_a, 1)
                    act.wait_ge(small_in, 64)
                    nc.scalar.activation(alog_sb[:], alog_sb[:], ACT.Exp).then_inc(ac, 1)
                    nc.scalar.activation(neg_rms[:], rms_raw[:], ACT.Copy, scale=-1.0)
                    act.wait_ge(dv, 2)
                    nc.scalar.activation(beta[0:96], work_a[0:96], ACT.Exp).then_inc(ac, 1)
                    act.wait_ge(dv, 4)
                    nc.scalar.activation(work_a[0:96], g_full[0:96], ACT.Abs).then_inc(ac, 1)
                    act.wait_ge(ac, 3)
                    nc.scalar.activation(work_a[0:96], work_a[0:96], ACT.Exp, scale=-1.0).then_inc(ac, 1)
                    act.wait_ge(ac, 4)
                    nc.scalar.activation(work_a[0:96], work_a[0:96], ACT.Ln, bias=1.0).then_inc(ac, 1)
                    for i in range(6):
                        act.wait_ge(cum_done, i + 1)
                        kind, half = i // 2, i % 2
                        dst = tables[:, half * (NIT // 2):(half + 1) * (NIT // 2), 1 + kind, :]
                        nc.scalar.activation(dst, bank[i][:].rearrange("p (a b) -> p a b", b=UN), ACT.Exp)\
                            .then_inc(exp_cum, 1)
                    for h in range(H):
                        act.wait_ge(w_in[h % 2], 16 * (h // 2 + 1))
                        if h >= 2:
                            act.wait_ge(w_stored[h % 2], 16 * (h // 2))
                        nc.scalar.activation(w_pair[h % 2][:, 0].bitcast(F16), w_stage[:, h % 2], ACT.Copy).then_inc(w_high, 1)

                @block.tensor
                def _(pe):
                    pe.wait_ge(x_split_b, KT)
                    pe.wait_ge(wz_low, 1)
                    for i in range(NB):
                        b, c0 = i // (NB // B), TAPS - 1 + (i % (NB // B)) * 512
                        first = True
                        for k in range(KT):
                            for wp, xp in ((0, 0), (0, 1), (1, 0)):
                                w = wz_parts[:, wp, k].bitcast(BF16 if wp else F16)
                                xx = x_parts[:, xp, k, b, c0:c0 + 512].bitcast(BF16 if xp else F16)
                                last = nc.tensor.matmul(bank[i][0:32, :], w, xx, start=first,
                                                        stop=(k == KT - 1 and wp == 1))
                                first = False
                        last.then_inc(zp_done, 1)
                    pe.wait_ge(dv, 12)
                    pe.wait_ge(zt_done, NB)
                    for i in range(6):
                        kind, half = i // 2, i % 2
                        w = (laterb, uptob, onesb)[kind]
                        rhs = g_parts[0:96, half * (NIT // 2):(half + 1) * (NIT // 2), :].rearrange("p a b -> p (a b)")
                        nc.tensor.matmul(bank[i][:], w[0:96, :], rhs, start=True, stop=True).then_inc(cum_done, 1)

                @block.vector
                def _(dve):
                    v = nc.vector
                    dve.wait_ge(wz_high, 1)
                    v.tensor_tensor(wz_parts[:, 1].bitcast(BF16), wz_stage[:], wz_parts[:, 0].bitcast(F16),
                                    ALU.subtract).then_inc(wz_low, 1)
                    for k in range(KT):
                        dve.wait_ge(x_split_a, k + 1)
                        v.tensor_tensor(x_parts[:, 1, k].bitcast(BF16), x_stage[:, k], x_parts[:, 0, k].bitcast(F16),
                                        ALU.subtract).then_inc(x_split_b, 1)
                    dve.wait_ge(consts_in, 32)
                    v.tensor_copy(ident16[:], cst[:, C_ID]).then_inc(casts, 1)
                    for u in range(4):
                        v.tensor_copy(rep16[:, u], cst[:, C_ID])
                    v.tensor_scalar(negid16[:], cst[:, C_ID], -1.0, None, ALU.mult)
                    v.tensor_copy(identb[:], cst[:, C_ID])
                    v.tensor_copy(negmask[:], cst[:, C_NEG])
                    v.tensor_copy(laterb[:], cst[:, C_LATER])
                    v.tensor_copy(uptob[:], cst[:, C_UPTO])
                    v.tensor_copy(onesb[:], cst[:, C_ONES])
                    v.tensor_copy(mask0t[:], cst[:, C_M0T])
                    v.memset(over_dh[:], 1.0 / DH)
                    v.memset(eps_dh[:], EPS_RMS * DH)
                    v.memset(beta[96:128], 0.0)
                    v.memset(g_parts[96:128], 0.0)
                    for i in range(NB):
                        dve.wait_ge(zp_done, i + 1)
                        v.tensor_copy(z_t[:, i * 512:(i + 1) * 512], bank[i][0:32, :]).then_inc(zt_done, 1)
                    dve.wait_ge(zt_done, NB)
                    v.transpose(z_rows, z_t).then_inc(tr_done, 1)
                    dve.wait_ge(tr_done, 1)
                    zv = z_rows.rearrange("p (b c j h) -> p b h c j", b=B, j=4, h=H)
                    for b in range(B):
                        for j in range(NH):
                            last = v.tensor_scalar(work_a[32 * j:32 * j + 32, b * H:(b + 1) * H, :], zv[:, b, :, :, j],
                                                   -1.0, 80.0, ALU.mult, ALU.min)
                            last = v.tensor_copy(g_full[32 * j:32 * j + 32, b * H:(b + 1) * H, :], zv[:, b, :, :, 3])
                    last.then_inc(dv, 2)
                    dve.wait_ge(ac, 2)
                    v.tensor_scalar(beta[0:96], beta[0:96], 1.0, None, ALU.add).then_inc(dv, 1)
                    dve.wait_ge(dv, 3)
                    v.reciprocal(beta[0:96], beta[0:96])
                    dve.wait_ge(small_in, 64)
                    dtb = dt_sb[:].rearrange("p (o h u) -> p o h u", o=1, u=1).broadcast_to([96, B, H, T // CH])
                    gv = g_full[0:96].rearrange("p (b h) c -> p b h c", b=B)
                    for b in range(B):
                        last = v.tensor_tensor(gv[:, b], gv[:, b], dtb[:, b], ALU.add)
                    last.then_inc(dv, 1)
                    dve.wait_ge(dv, 4)
                    v.tensor_scalar(beta[0:96], beta[0:96], 2.0, None, ALU.mult)
                    v.tensor_scalar(work_b[0:96], g_full[0:96], 0.0, None, ALU.max).then_inc(dv, 2)
                    dve.wait_ge(ac, 5)
                    dve.wait_ge(dv, 6)
                    v.tensor_tensor(work_a[0:96], work_a[0:96], work_b[0:96], ALU.add).then_inc(dv, 1)
                    dve.wait_ge(dv, 7)
                    ab = alog_sb[:].rearrange("p (h u) -> p h u", u=1).broadcast_to([96, H, T // CH])
                    wa = work_a[0:96].rearrange("p (b h) c -> p b h c", b=B)
                    for b in range(B):
                        last = v.tensor_tensor(gv[:, b], wa[:, b], ab, ALU.mult)
                    last.then_inc(dv, 1)
                    dve.wait_ge(dv, 8)
                    v.tensor_scalar(g_full[0:96], g_full[0:96], -1.0, None, ALU.mult).then_inc(dv, 1)
                    dve.wait_ge(dv, 9)
                    gp = g_parts[:].rearrange("p n u -> p (n u)")
                    gf = g_full[:].rearrange("p n u -> p (n u)")
                    gh = g_hi[:].rearrange("p n u -> p (n u)")
                    v.tensor_copy(gp[0:96], gf[0:96])
                    v.tensor_copy(gh[0:96], gf[0:96]).then_inc(dv, 1)
                    dve.wait_ge(dv, 10)
                    v.tensor_tensor(gf[0:96], gf[0:96], gh[0:96], ALU.subtract).then_inc(dv, 1)
                    dve.wait_ge(dv, 11)
                    v.tensor_copy(gp[32:64], gf[32:64])
                    v.tensor_copy(gh[64:96], gf[64:96]).then_inc(tr_done, 1)
                    dve.wait_ge(tr_done, 2)
                    v.tensor_tensor(gp[64:96], gf[64:96], gh[64:96], ALU.subtract).then_inc(dv, 1)
                    bt = beta[:].rearrange("p a (n u) -> p (a n) u", u=UN)
                    v.tensor_scalar(tables[:, :, 0, :], bt, -1.0, None, ALU.mult)
                    dve.wait_ge(exp_cum, 6)
                    v.tensor_tensor(tables[:, :, 1, :], tables[:, :, 1, :], bt, ALU.mult)
                    v.tensor_scalar(tables[:, :, 2, :], tables[:, :, 2, :], -1.0, None, ALU.mult).then_inc(dv, 1)
                    dve.wait_ge(dv, 13)
                    v.memset(tables[:, ::NTB, 2:4, 0:1], 0.0)

        with ExitStack() as loop_scope:
            scope = loop_scope

            def ring(name, shape, dt):
                return [sb(f"{name}{i}", shape, dt) for i in range(RING)]

            x_cur = ring("x_cur", [P, 2, KT, PW + 1], U16)
            w_cur = ring("w_cur", [P, 2, KT, HC], U16)
            c_cur = ring("c_cur", [P, NCONV, TAPS], F32)
            t_cur = ring("t_cur", [P, 4, UN], F32)
            g_cur = ring("g_cur", [P, UN], BF16)
            kq_t = ring("kq_t", [P, UN, 4, CH], F32)
            k_rows = ring("k_rows", [P, UN, P], F32)
            v_rows = ring("v_rows", [P, UN, P], F32)
            inv_t = ring("inv_t", [P, UN, P], F32)
            gate = ring("gate", [P, TB], F32)
            squares = ring("squares", [P, UN, 4, CH], F32)
            y_buf = ring("y_buf", [P, TB], F32)
            v_t = ring("v_t", [P, UN, NH, CH], F32)
            conv_acc = [sb(f"conv_acc{i}", [P, TB], F32) for i in range(2)]
            g_upto = sb("g_upto", [96, UN, CH], BF16)
            decay = [sb(f"decay{g}", [P, 4, P], F32) for g in range(2)]
            n_t = [sb(f"n_t{g}", [P, 4, P], F32) for g in range(2)]
            n_high = [sb(f"n_high{g}", [P, 4, P], F16) for g in range(2)]
            n_low = [sb(f"n_low{g}", [P, 4, P], BF16) for g in range(2)]
            inv = [sb(f"inv{g}", [P, 4, P], F16) for g in range(2)]
            invt = [sb(f"invt{g}", [P, 4, P], F16) for g in range(2)]
            xs = [sb(f"xs{g}", [P, 4, P], F16) for g in range(2)]
            sv = sb("sv", [P, UN], F32)
            k_sq = sb("k_sq", [P, UN], F32)
            ln_k = sb("ln_k", [P, UN], F32)
            ln_v = sb("ln_v", [P, TB], F32)
            eps_var = sb("eps_var", [P, 1], F32)
            r2 = sb("r2", [P, UN], F32)
            c_n = sb("c_n", [P, UN], F32)
            c_k = sb("c_k", [P, UN], F32)
            state = sb("state", [P, P], F32)
            rhs = [sb(f"rhs{i}", [P, P], F32) for i in range(2)]
            w_sol = [sb(f"w_sol{i}", [P, P], F32) for i in range(2)]
            o_sq = sb("o_sq", [P, TB], F32)
            rstd = sb("rstd", [P, TB], F32)
            o_norm = sb("o_norm", [P, TB], F32)

            loaded = [sem(f"loaded{i}") for i in range(RING)]
            tabled = [sem(f"tabled{i}") for i in range(RING)]
            stored = [sem(f"stored{i}") for i in range(RING)]
            sp_waited = sem("sp_waited")
            projected, tap0, tap_step, tapped, silu_done, gate_done, squared, summed, k_sq_made, small_step, g_made = map(
                sem, ("projected", "tap0", "tap_step", "tapped", "silu_done", "gate_done", "squared", "summed",
                      "k_sq_made", "small_step", "g_made"))
            (grammed, decay_sum, decayed, ln_made, norm_made, n_made, high_made, low_made, l0_step, l0_made, l0_turned,
             inv_made, x_made, x_kept, y_made, merge_seen, merged, turned, turn_kept, k_turned, k_kept, v_turned,
             v_kept, res_made, res_kept, fix_made, fix_kept) = map(sem, (
                "grammed", "decay_sum", "decayed", "ln_made", "norm_made", "n_made", "high_made", "low_made",
                "l0_step", "l0_made", "l0_turned", "inv_made", "x_made", "x_kept", "y_made", "merge_seen", "merged",
                "turned", "turn_kept", "k_turned", "k_kept", "v_turned", "v_kept", "res_made", "res_kept",
                "fix_made", "fix_kept"))
            zeroed, ks_made, rhs_made, sol_made, sol_kept, out_made, upd_made, stated, osq_made, var_made, var_ln, \
                rstd_made, normed, gated = map(sem, (
                    "zeroed", "ks_made", "rhs_made", "sol_made", "sol_kept", "out_made", "upd_made", "stated",
                    "osq_made", "var_made", "var_ln", "rstd_made", "normed", "gated"))
            LV = LEVELS - 1
            OUT = bank[7][:, 0:TB]
            VAR = bank[7][:, TB:2 * TB]
            KS = bank[6][:, 0:P]

            def run_bodies(eng, body, peeled=PEELED):
                for n in range(peeled):
                    body(n, n // RING, n % RING)
                rounds = (NIT - peeled) // RING
                assert peeled + rounds * RING == NIT
                with eng.Fori(0, rounds) as m:
                    for i in range(peeled, peeled + RING):
                        turn = m + i // RING
                        body(RING * turn + i % RING, turn, i % RING)
                for n in range(NIT, NIT + STAGES - 1):
                    body(n, n // RING, n % RING)

            def stage(n, turn, res, back):
                runs = not isinstance(n, int) or 0 <= n - back < NIT
                return runs, n - back, (res - back) % RING, turn - (1 if res < back else 0)

            def skip(stage_index):
                def wrap(f):
                    def g(*args):
                        if stage_index[0]:
                            f(*args)
                    return g
                return wrap

            with nc.Block() as block:
                @block.sync
                def _(sp):
                    def load(n, res):
                        b, h, tb = n // (H * NTB), (n // NTB) % H, n % NTB
                        sp.dma_start(x_cur[res][:, :, :, 0:PW].rearrange("p a b c -> p (a b) c"),
                                     x_parts[:].rearrange("p a k b c -> p (a k) (b c)")[:, :, bass.ds(b * XW + tb * TB, PW)])\
                            .then_inc(loaded[res], 16)
                        sp.dma_start(w_cur[res][:].rearrange("p a b c -> p (a b c)"),
                                     w_dram.rearrange("h p c -> (h p) c")[bass.ds(h * P, P), :]).then_inc(loaded[res], 16)
                        sp.dma_start(c_cur[res][:].rearrange("p a b -> p (a b)"),
                                     conv_sb[:].rearrange("p h a b -> p (h a b)")[:, bass.ds(h * (NCONV * TAPS), NCONV * TAPS)])\
                            .then_inc(loaded[res], 16)
                        sp.dma_start(g_cur[res][:], g_parts[:].rearrange("p n a -> p (n a)")[:, bass.ds(n * UN, UN)])\
                            .then_inc(loaded[res], 16)

                    def body(n, turn, res):
                        (a, _, _, _), (d, nd, rd, _) = stage(n, turn, res, 0), stage(n, turn, res, 3)
                        if a:
                            at_least(sp, stated, UN * (n - 2))
                            sp.sem_inc(sp_waited, 1)
                            sp.dma_start(t_cur[res][:].rearrange("p a b -> p (a b)"),
                                         tables[:].rearrange("p n a b -> p (n a b)")[:, bass.ds(n * (4 * UN), 4 * UN)])\
                                .then_inc(tabled[res], 16)
                        if a and not (isinstance(n, int) and n + 1 >= NIT):
                            for used, count in ((projected, NTILE), (tapped, NCONV), (g_made, 1)):
                                at_least(sp, used, count * (n - 1))
                                sp.sem_inc(sp_waited, 1)
                            load(n + 1, (res + 1) % RING)
                        if d:
                            sp.wait_ge(gated, nd + 1)
                            sp.sem_inc(sp_waited, 1)
                            dst = y_dram[nd] if isinstance(nd, int) else y_dram.rearrange("n p t -> (n p) t")[bass.ds(nd * P, P), :]
                            sp.dma_start(dst, y_buf[rd][:]).then_inc(stored[rd], 16)

                    load(0, 0)
                    for n in range(PEELED):
                        body(n, n // RING, n % RING)
                    rounds = (NIT - PEELED) // RING - 1
                    with sp.Fori(0, rounds) as m:
                        for i in range(PEELED, PEELED + RING):
                            turn = m + i // RING
                            body(RING * turn + i % RING, turn, i % RING)
                    for n in range(NIT - RING, NIT + STAGES - 1):
                        body(n, n // RING, n % RING)
                    for i in range(RING):
                        sp.wait_ge(stored[i], 16 * len(range(i, NIT, RING)))

                @block.tensor
                def _(pe):
                    mm = nc.tensor.matmul

                    def body(n, turn, res):
                        sa, sb_, sc = (stage(n, turn, res, k) for k in range(3))
                        nb, rb = sb_[1:3]
                        r, rc = sc[1:3]

                        @skip(sa)
                        def project(c):
                            if c == 0:
                                pe.wait_ge(loaded[res], 64 * (turn + 1))
                                at_least(pe, k_sq_made, n)
                            elif c == 1:
                                at_least(pe, gate_done, n)
                            else:
                                pe.wait_ge(tapped, NCONV * n + c - 1)
                            first = True
                            for k in range(KT):
                                for wp, xp in ((0, 0), (0, 1), (1, 0)):
                                    last = mm(bank[c % 2][:, 0:PW],
                                              w_cur[res][:, wp, k, c * P:(c + 1) * P].bitcast(BF16 if wp else F16),
                                              x_cur[res][:, xp, k, 0:PW].bitcast(BF16 if xp else F16),
                                              start=first, stop=(k == KT - 1 and wp == 1))
                                    first = False
                            last.then_inc(projected, 1)

                        @skip(sa)
                        def norms():
                            pe.wait_ge(squared, n + 1)
                            pe.wait_ge(tapped, NCONV * n + NCONV)
                            for u in range(UN):
                                last = mm(bank[0][:, u:u + 1], squares[res][:, u].rearrange("p a b -> p (a b)"),
                                          cst[:, C_ONES, 0:1], start=True, stop=True)
                            last.then_inc(summed, 1)

                        @skip(sb_)
                        def gram(g):
                            if g == 0:
                                pe.wait_ge(silu_done, NCONV * nb + 4)
                            at_least(pe, v_kept, 2 * nb - 1 + g)
                            for u in range(4):
                                a = kq_t[rb][:, 4 * g + u].rearrange("p a b -> p (a b)")
                                last = mm(bank[2 + g][:, u * P:(u + 1) * P], a, a, start=True, stop=True)
                            last.then_inc(grammed, 1)

                        @skip(sb_)
                        def decays(g):
                            if g == 0:
                                pe.wait_ge(g_made, nb + 1)
                            at_least(pe, fix_kept, 2 * nb - 1 + g)
                            mm(bank[4 + g][:], laterb[0:96, :],
                               g_upto[:, 4 * g:4 * g + 4, None, :].broadcast_to([96, 4, 4, CH]),
                               start=True, stop=False)
                            mm(bank[4 + g][:], identb[:], negmask[:, None, :].broadcast_to([P, 4, P]),
                               start=False, stop=True).then_inc(decay_sum, 1)

                        @skip(sb_)
                        def turn_keys(g):
                            pe.wait_ge(n_made, UN * nb + 4 * g + 4)
                            for u in range(4):
                                last = nc.tensor.transpose(bank[2 + g][:, u * P:(u + 1) * P],
                                                           kq_t[rb][:, 4 * g + u].rearrange("p a b -> p (a b)"), cst[:, C_ID])
                            last.then_inc(k_turned, 1)

                        @skip(sb_)
                        def turn_values(g):
                            pe.wait_ge(k_kept, 2 * nb + g + 1)
                            pe.wait_ge(silu_done, NCONV * nb + NCONV)
                            for u in range(4):
                                last = nc.tensor.transpose(bank[2 + g][0:96, u * P:(u + 1) * P],
                                                           v_t[rb][:, 4 * g + u].rearrange("p a b -> p (a b)"), cst[:, C_ID])
                            last.then_inc(v_turned, 1)

                        def turn_units(g, src):
                            dst = bank[4 + g][:].bitcast(F16)
                            for u in range(4):
                                last = nc.tensor.transpose(dst[:, u * P:(u + 1) * P], src[:, u], ident16[:])
                            return last

                        @skip(sb_)
                        def turn0(g):
                            pe.wait_ge(l0_made, 2 * nb + g + 1)
                            turn_units(g, invt[g]).then_inc(l0_turned, 1)

                        @skip(sb_)
                        def level_x(l, g):
                            if l == 1:
                                pe.wait_ge(inv_made, 2 * nb + g + 1)
                            else:
                                pe.wait_ge(turn_kept, 2 * LV * nb + 2 * (l - 2) + g + 1)
                            for u in range(4):
                                last = mm(bank[4 + g][:, u * P:(u + 1) * P], n_high[g][:, u], inv[g][:, u], start=True, stop=True)
                            last.then_inc(x_made, 1)

                        @skip(sb_)
                        def level_y(l, g):
                            pe.wait_ge(x_kept, 2 * LV * nb + 2 * (l - 1) + g + 1)
                            for u in range(4):
                                last = mm(bank[4 + g][:, u * P:(u + 1) * P], invt[g][:, u], xs[g][:, u], start=True, stop=True)
                            last.then_inc(y_made, 1)

                        @skip(sb_)
                        def level_t(l, g):
                            pe.wait_ge(merged, 2 * LV * nb + 2 * (l - 1) + g + 1)
                            turn_units(g, inv[g]).then_inc(turned, 1)

                        @skip(sb_)
                        def residual(g):
                            pe.wait_ge(turn_kept, 2 * LV * nb + 2 * (LV - 1) + g + 1)
                            pe.wait_ge(low_made, 2 * nb + g + 1)
                            flat = bank[4 + g][:]
                            mm(flat, ident16[:], rep16[:].rearrange("p a b -> p (a b)"), start=True, stop=False)
                            mm(flat, negid16[:], inv[g][:].rearrange("p a b -> p (a b)"), start=False, stop=False)
                            for part in (n_high, n_low):
                                for u in range(4):
                                    last = mm(flat[:, u * P:(u + 1) * P], part[g][:, u], inv[g][:, u], start=False,
                                              stop=(part is n_low and u == 3))
                            last.then_inc(res_made, 1)

                        @skip(sb_)
                        def fix(g):
                            pe.wait_ge(res_kept, 2 * nb + g + 1)
                            flat = bank[4 + g][:]
                            mm(flat, ident16[:], invt[g][:].rearrange("p a b -> p (a b)"), start=True, stop=False)
                            for u in range(4):
                                last = mm(flat[:, u * P:(u + 1) * P], xs[g][:, u], invt[g][:, u], start=False, stop=(u == 3))
                            last.then_inc(fix_made, 1)

                        @skip(sc)
                        def from_state(c):
                            if c == 0:
                                pe.wait_ge(fix_kept, 2 * r + 2)
                                pe.wait_ge(zeroed, 1)
                            at_least(pe, stated, UN * r + c)
                            mm(KS, kq_t[rc][:, c].rearrange("p a b -> p (a b)"), state[:], start=True, stop=True)\
                                .then_inc(ks_made, 1)

                        @skip(sc)
                        def solve(c):
                            pe.wait_ge(rhs_made, UN * r + c + 1)
                            mm(KS, inv_t[rc][:, c], rhs[c % 2][:], start=True, stop=True).then_inc(sol_made, 1)

                        @skip(sc)
                        def output(c):
                            if c == 0:
                                at_least(pe, normed, r)
                            mm(OUT[:, c * CH:(c + 1) * CH], rhs[c % 2][:], inv_t[rc][:, c, 96:128], start=True,
                               stop=True).then_inc(out_made, 1)

                        @skip(sc)
                        def update(c):
                            pe.wait_ge(sol_kept, UN * r + c + 1)
                            mm(KS, k_rows[rc][:, c], w_sol[c % 2][:], start=True, stop=True).then_inc(upd_made, 1)

                        @skip(sc)
                        def variance():
                            pe.wait_ge(osq_made, r + 1)
                            mm(VAR, over_dh[:], o_sq[:], start=True, stop=False)
                            mm(VAR, eps_dh[:], squares[rc][:, :, 3, :], start=False, stop=True).then_inc(var_made, 1)

                        decays(0)
                        decays(1)
                        gram(0)
                        gram(1)
                        from_state(0)
                        project(0)
                        solve(0)
                        project(1)
                        update(0)
                        turn0(0)
                        turn0(1)
                        from_state(1)
                        turn_keys(0)
                        output(0)
                        turn_keys(1)
                        for l in range(1, LEVELS):
                            c = l + 1
                            level_x(l, 0)
                            if l == 1:
                                solve(1)
                                output(1)
                            level_x(l, 1)
                            if l == 1:
                                update(1)
                            from_state(c)
                            project(l + 1)
                            level_y(l, 0)
                            solve(c)
                            level_y(l, 1)
                            output(c)
                            if l == 2:
                                turn_values(0)
                            if l == 3:
                                turn_values(1)
                            level_t(l, 0)
                            update(c)
                            level_t(l, 1)
                        residual(0)
                        variance()
                        residual(1)
                        norms()
                        fix(0)
                        fix(1)

                    run_bodies(pe, body)

                @block.scalar
                def _(act):
                    a = nc.scalar.activation

                    def body(n, turn, res):
                        sa, sb_, sc, sd = (stage(n, turn, res, k) for k in range(4))
                        nb, rb = sb_[1:3]
                        r = sc[1]
                        d = sd[1]

                        @skip(sa)
                        def first_tap(c):
                            act.wait_ge(projected, NTILE * n + c + 1)
                            at_least(act, silu_done, NCONV * n + max(c - 1, 0))
                            a(conv_acc[c % 2][:], bank[c % 2][:, 0:TB], ACT.Copy, scale=c_cur[res][:, c, 0:1]).then_inc(tap0, 1)

                        @skip(sa)
                        def silu(c):
                            act.wait_ge(tapped, NCONV * n + c + 1)
                            if c == 0:
                                dst = kq_t[res][:, :, 3, :]
                            elif c < 4:
                                dst = kq_t[res][:, :, c - 1, :]
                            else:
                                dst = v_t[res][:, :, c - 4, :]
                            a(dst, conv_acc[c % 2][:].rearrange("p (u t) -> p u t", u=UN), ACT.Silu).then_inc(silu_done, 1)

                        @skip(sa)
                        def gate_silu():
                            act.wait_ge(projected, NTILE * n + NTILE)
                            at_least(act, gated, n - 2)
                            a(gate[res][:], bank[1][:, TAPS - 1:PW], ACT.Silu).then_inc(gate_done, 1)

                        @skip(sb_)
                        def exp_decay(g):
                            act.wait_ge(decay_sum, 2 * nb + g + 1)
                            a(decay[g][:].rearrange("p a b -> p (a b)"), bank[4 + g][:], ACT.Exp).then_inc(decayed, 1)

                        @skip(sb_)
                        def key_norms():
                            act.wait_ge(k_sq_made, nb + 1)
                            a(ln_k[:], k_sq[:], ACT.Ln).then_inc(ln_made, 1)
                            act.wait_ge(ln_made, nb + 1)
                            a(sv[:], ln_k[:], ACT.Exp, scale=0.5).then_inc(norm_made, 1)

                        @skip(sd)
                        def root_variance():
                            act.wait_ge(var_made, d + 1)
                            act.wait_ge(zeroed, 1)
                            a(ln_v[:], VAR, ACT.Ln, bias=eps_var[:, 0:1]).then_inc(var_ln, 1)
                            act.wait_ge(var_ln, d + 1)
                            a(rstd[:], ln_v[:], ACT.Exp, scale=-0.5).then_inc(rstd_made, 1)

                        @skip(sb_)
                        def high(g):
                            act.wait_ge(n_made, UN * nb + 4 * g + 4)
                            a(n_high[g][:], n_t[g][:], ACT.Copy).then_inc(high_made, 1)

                        @skip(sb_)
                        def keep0(g):
                            act.wait_ge(l0_turned, 2 * nb + g + 1)
                            a(inv[g][:].rearrange("p a b -> p (a b)"), bank[4 + g][:].bitcast(F16)[:, 0:4 * P], ACT.Copy)\
                                .then_inc(inv_made, 1)

                        @skip(sb_)
                        def keep_x(l, g):
                            act.wait_ge(x_made, 2 * LV * nb + 2 * (l - 1) + g + 1)
                            a(xs[g][:].rearrange("p a b -> p (a b)"), bank[4 + g][:], ACT.Copy).then_inc(x_kept, 1)

                        @skip(sb_)
                        def keep_t(l, g):
                            act.wait_ge(turned, 2 * LV * nb + 2 * (l - 1) + g + 1)
                            a(invt[g][:].rearrange("p a b -> p (a b)"), bank[4 + g][:].bitcast(F16)[:, 0:4 * P], ACT.Copy)\
                                .then_inc(turn_kept, 1)

                        @skip(sb_)
                        def keep_res(g):
                            act.wait_ge(res_made, 2 * nb + g + 1)
                            a(xs[g][:].rearrange("p a b -> p (a b)"), bank[4 + g][:], ACT.Copy).then_inc(res_kept, 1)

                        @skip(sb_)
                        def keep_fix(g):
                            act.wait_ge(fix_made, 2 * nb + g + 1)
                            a(inv_t[rb][:, 4 * g:4 * g + 4].rearrange("p a b -> p (a b)"), bank[4 + g][:], ACT.Copy)\
                                .then_inc(fix_kept, 1)

                        @skip(sc)
                        def keep_w(c):
                            act.wait_ge(sol_made, UN * r + c + 1)
                            a(w_sol[c % 2][:], KS, ACT.Copy).then_inc(sol_kept, 1)

                        @skip(sc)
                        def square_out():
                            act.wait_ge(out_made, UN * r + UN)
                            a(o_sq[:], OUT, ACT.Square).then_inc(osq_made, 1)

                        nc.scalar.preload_act_table_set("natural_log_exp_and_others")
                        root_variance()
                        exp_decay(0)
                        exp_decay(1)
                        key_norms()
                        keep_w(0)
                        high(0)
                        high(1)
                        first_tap(0)
                        keep0(0)
                        keep0(1)
                        first_tap(1)
                        silu(0)
                        for l in range(1, LEVELS):
                            c = l + 1
                            keep_x(l, 0)
                            if l == 1:
                                keep_w(1)
                            keep_x(l, 1)
                            if c < NCONV:
                                first_tap(c)
                            keep_w(c)
                            if l == LV:
                                square_out()
                            keep_t(l, 0)
                            silu(l)
                            keep_t(l, 1)
                        keep_res(0)
                        keep_res(1)
                        gate_silu()
                        keep_fix(0)
                        keep_fix(1)

                    run_bodies(act, body)

                @block.vector
                def _(dve):
                    v = nc.vector
                    v.memset(state[:], 0.0)
                    v.memset(eps_var[:], EPS_RMS * DH * EPS_K)
                    for i in range(RING):
                        last = v.memset(v_rows[i][96:128], 0.0)
                    last.then_inc(zeroed, 1)

                    def body(n, turn, res):
                        sa, sb_, sc, sd = (stage(n, turn, res, k) for k in range(4))
                        nb, rb = sb_[1:3]
                        r, rc = sc[1:3]
                        d = sd[1]

                        @skip(sa)
                        def taps(c):
                            acc = conv_acc[c % 2][:]
                            dve.wait_ge(tap0, NCONV * n + c + 1)
                            for i in range(1, TAPS):
                                ins = v.scalar_tensor_tensor(acc, bank[c % 2][:, i:i + TB], c_cur[res][:, c, i:i + 1], acc,
                                                             ALU.mult, ALU.add)
                                if i < TAPS - 1:
                                    ins.then_inc(tap_step, 1)
                                    dve.wait_ge(tap_step, (TAPS - 2) * (NCONV * n + c) + i)
                                else:
                                    ins.then_inc(tapped, 1)

                        @skip(sa)
                        def small():
                            dve.wait_ge(summed, n + 1)
                            at_least(dve, ln_made, n)
                            v.tensor_scalar(k_sq[:], bank[0][:, 0:UN], EPS_K, None, ALU.add).then_inc(k_sq_made, 1)
                            dve.wait_ge(k_sq_made, n + 1)
                            v.reciprocal(r2[:], k_sq[:]).then_inc(small_step, 1)
                            dve.wait_ge(small_step, 3 * n + 1)
                            dve.wait_ge(tabled[res], 16 * (turn + 1))
                            v.tensor_tensor(c_n[:], r2[:], t_cur[res][:, 0, :], ALU.mult).then_inc(small_step, 1)
                            v.tensor_tensor(c_k[:], r2[:], t_cur[res][:, 1, :], ALU.mult).then_inc(small_step, 1)

                        @skip(sb_)
                        def system(g):
                            dve.wait_ge(small_step, 3 * nb + 3)
                            dve.wait_ge(grammed, 2 * nb + g + 1)
                            dve.wait_ge(decayed, 2 * nb + g + 1)
                            at_least(dve, low_made, 2 * nb)
                            for u in range(4):
                                v.scalar_tensor_tensor(n_t[g][:, u], bank[2 + g][:, u * P:(u + 1) * P],
                                                       c_n[:, 4 * g + u:4 * g + u + 1], decay[g][:, u],
                                                       ALU.mult, ALU.mult).then_inc(n_made, 1)

                        @skip(sb_)
                        def level0(g):
                            dve.wait_ge(high_made, 2 * nb + g + 1)
                            v.tensor_tensor(invt[g][:], n_high[g][:], mask0t[:, None, :].broadcast_to([P, 4, P]), ALU.mult)\
                                .then_inc(l0_step, 1)
                            dve.wait_ge(l0_step, 2 * nb + g + 1)
                            v.tensor_tensor(invt[g][:], invt[g][:], rep16[:], ALU.add).then_inc(l0_made, 1)

                        @skip(sb_)
                        def keep_k(g):
                            dve.wait_ge(k_turned, 2 * nb + g + 1)
                            v.tensor_tensor(k_rows[rb][:, 4 * g:4 * g + 4], bank[2 + g][:].rearrange("p (a b) -> p a b", a=4),
                                            c_k[:, 4 * g:4 * g + 4, None].broadcast_to([P, 4, P]), ALU.mult).then_inc(k_kept, 1)

                        @skip(sb_)
                        def keep_v(g):
                            dve.wait_ge(v_turned, 2 * nb + g + 1)
                            dve.wait_ge(norm_made, nb + 1)
                            v.tensor_tensor(v_rows[rb][0:96, 4 * g:4 * g + 4],
                                            bank[2 + g][0:96, :].rearrange("p (a b) -> p a b", a=4),
                                            sv[0:96, 4 * g:4 * g + 4, None].broadcast_to([96, 4, P]), ALU.mult).then_inc(v_kept, 1)

                        @skip(sb_)
                        def merge(l, g):
                            dve.wait_ge(y_made, 2 * LV * nb + 2 * (l - 1) + g + 1)
                            dve.sem_inc(merge_seen, 1)
                            v.copy_predicated(inv[g][:], mask_sb[:, l, None, :].broadcast_to([P, 4, P]),
                                              bank[4 + g][:].rearrange("p (a b) -> p a b", a=4)).then_inc(merged, 1)

                        @skip(sc)
                        def right_side(c):
                            dve.wait_ge(ks_made, UN * r + c + 1)
                            v.scalar_tensor_tensor(rhs[c % 2][:], KS, t_cur[rc][:, 2, c:c + 1], v_rows[rc][:, c],
                                                   ALU.mult, ALU.add).then_inc(rhs_made, 1)

                        @skip(sc)
                        def new_state(c):
                            dve.wait_ge(upd_made, UN * r + c + 1)
                            v.scalar_tensor_tensor(state[:], state[:], t_cur[rc][:, 3, c:c + 1], KS,
                                                   ALU.mult, ALU.add).then_inc(stated, 1)

                        @skip(sd)
                        def normalize():
                            dve.wait_ge(rstd_made, d + 1)
                            at_least(dve, gated, d)
                            v.scalar_tensor_tensor(o_norm[:], OUT, neg_rms[:, 0:1], rstd[:], ALU.mult, ALU.mult)\
                                .then_inc(normed, 1)

                        right_side(0)
                        system(0)
                        system(1)
                        normalize()
                        level0(0)
                        level0(1)
                        new_state(0)
                        taps(0)
                        right_side(1)
                        keep_k(0)
                        taps(1)
                        keep_k(1)
                        for l in range(1, LEVELS):
                            c = l + 1
                            if l == 1:
                                new_state(1)
                            right_side(c)
                            merge(l, 0)
                            if c < NCONV:
                                taps(c)
                            merge(l, 1)
                            if l == 2:
                                keep_v(0)
                            if l == 3:
                                keep_v(1)
                            new_state(c)
                        small()

                    run_bodies(dve, body)

                @block.gpsimd
                def _(pool):
                    tt = nc.gpsimd.tensor_tensor

                    def body(n, turn, res):
                        a, b, d = (stage(n, turn, res, k) for k in (0, 1, 3))
                        if d[0]:
                            _, nd, rd, td = d
                            pool.wait_ge(normed, nd + 1)
                            pool.wait_ge(gate_done, nd + 1)
                            at_least(pool, stored[rd], 16 * td)
                            tt(y_buf[rd][:], o_norm[:], gate[rd][:], ALU.mult).then_inc(gated, 1)
                        if b[0]:
                            nb = b[1]
                            for g in range(2):
                                pool.wait_ge(high_made, 2 * nb + g + 1)
                                at_least(pool, res_made, 2 * nb)
                                tt(n_low[g][:], n_t[g][:], n_high[g][:], ALU.subtract).then_inc(low_made, 1)
                        if a[0]:
                            pool.wait_ge(loaded[res], 64 * (turn + 1))
                            at_least(pool, decay_sum, 2 * n)
                            tt(g_upto[:], g_cur[res][0:96, :, None].broadcast_to([96, UN, CH]),
                               uptob[0:96, None, 0:CH].broadcast_to([96, UN, CH]), ALU.mult).then_inc(g_made, 1)
                            pool.wait_ge(silu_done, NCONV * n + 4)
                            tt(squares[res][:], kq_t[res][:], kq_t[res][:], ALU.mult).then_inc(squared, 1)

                    run_bodies(pool, body, PEELED + RING)

        attention_scope.close()
        experts(nc, ctx, bank, y_dram, x_rows, w_o, consts, gate_w, gate_b, up_w, up_b, gp_w, gp_b, down_w, down_b, out)


def experts(nc, ctx, bank, y_dram, x_rows, w_o, consts, gate_w, gate_b, up_w, up_b, gp_w, gp_b, down_w, down_b, out):
    def sem(name):
        return ctx.enter_context(nc.semaphore(name))

    def sb(name, shape, dt):
        return ctx.enter_context(nc.sbuf_tensor(name, shape, dt))

    wo = sb("wo", [P, H, D], F32)
    x2 = sb("x2", [P, NTT, D], F32)
    x2_parts = sb("x2_parts", [P, 2, KT, B * T], U16)
    y_in = [sb(f"y_in{i}", [P, H, P], F32) for i in range(2)]
    x_in_b = [sb(f"x_in{i}", [P, D], F32) for i in range(2)]
    xr = [sb(f"xr{i}", [P, D], F32) for i in range(2)]
    x2t = [sb(f"x2t{i}", [P, KT, P], F32) for i in range(2)]
    stats = sb("stats", [P, 6], F32)
    mv = sb("mv", [P, NTT, 2], F32)
    sd = sb("sd", [P, NTT], F32)
    rs = sb("rs", [P, NTT], F32)
    eps_ln = sb("eps_ln", [P, 1], F32)
    idf = sb("idf", [P, P], F32)
    gw = sb("gw", [P, KT, E], F32)
    gb = sb("gb", [P, E], F32)
    logits = sb("logits", [P, NTT, E], F32)
    top = sb("top", [P, NTT, 8], F32)
    topi = sb("topi", [P, NTT, 8], U32)
    topf = sb("topf", [P, NTT, 8], F32)
    prob = sb("prob", [P, NTT, E], F32)
    tmp = sb("tmp", [P, NTT, E], F32)
    pick = sb("pick", [P, NTT, E], F32)
    zsum = sb("zsum", [P, NTT], F32)
    idx = sb("idx", [P, E], F32)
    comb_t = [sb(f"comb_t{i}", [E, P], F32) for i in range(2)]
    dbias = sb("dbias", [E, D], F32)
    upb = sb("upb", [P, E, FT], F32)
    gpb = sb("gpb", [P, E, FT], F32)
    WCOL = max(KT * FP, FT * D)
    stage = sb("stage", [P, WCOL], F32)
    wparts = [[sb(f"ew{i}_{k}", [P, 2, WCOL], U16) for k in range(3)] for i in range(2)]
    u_sb = [sb(f"u_sb{i}", [P, 512], F32) for i in range(2)]
    prod = [sb(f"prod{i}", [P, 512], F32) for i in range(2)]
    h_sb = [sb(f"h_sb{i}", [P, 512], F32) for i in range(2)]
    h_hi = sb("h_hi", [P, FT, 512], F16)
    h_lo = sb("h_lo", [P, FT, 512], BF16)

    b_small = sem("b_small")
    y_ld = [sem("y_ld0"), sem("y_ld1")]
    (outp, added, st_made, ag_made, rs_made, x2_made, x2_turn, x2t_kept, x2_hi, x2_lo, logit, logit_kept) = map(sem, (
        "outp", "added", "st_made", "ag_made", "rs_made", "x2_made", "x2_turn", "x2t_kept", "x2_hi", "x2_lo", "logit",
        "logit_kept"))
    idx_set = sem("idx_set")
    sd_made = sem("sd_made")
    with nc.Block() as block:
        @block.sync
        def _(sp):
            for dst, src in ((wo[:].rearrange("p a b -> p (a b)"), w_o), (idf[:], consts[:, 0:P]),
                             (gw[:].rearrange("p a b -> p (a b)"), gate_w), (gb[:], gate_b), (dbias[:], down_b),
                             (upb[:].rearrange("p a b -> p (a b)"), up_b), (gpb[:].rearrange("p a b -> p (a b)"), gp_b)):
                sp.dma_start(dst, src).then_inc(b_small, 16)
            yv = y_dram.rearrange("(b h t) p c -> b t p h c", b=B, h=H)
            for i in range(NTT):
                b, tb, half = i // (NTT // B), (i % (NTT // B)) // 2, i % 2
                if i >= 2:
                    sp.wait_ge(outp, i - 1)
                    sp.wait_ge(added, i - 1)
                sp.dma_start(y_in[i % 2][:], yv[b, tb, :, :, half * P:(half + 1) * P]).then_inc(y_ld[i % 2], 16)
                sp.dma_start(x_in_b[i % 2][:], x_rows[i * P:(i + 1) * P, :]).then_inc(y_ld[i % 2], 16)

        @block.gpsimd
        def _(pool):
            nc.gpsimd.memset(eps_ln[:], EPS_LN).then_inc(idx_set, 1)
            nc.gpsimd.iota(topi[:, 0, :], pattern=[[1, E]], base=0, channel_multiplier=0).then_inc(idx_set, 1)
            pool.wait_ge(idx_set, 2)
            nc.gpsimd.tensor_copy(idx[:], topi[:, 0, :]).then_inc(idx_set, 1)
            for i in range(NTT):
                pool.wait_ge(x2_hi, i + 1)
                nc.gpsimd.tensor_tensor(x2_parts[:, 1, :, i * P:(i + 1) * P].bitcast(BF16), x2t[i % 2][:],
                                        x2_parts[:, 0, :, i * P:(i + 1) * P].bitcast(F16), ALU.subtract).then_inc(x2_lo, 1)

        @block.scalar
        def _(act):
            act.wait_ge(idx_set, 2)

            def deviation(i):
                act.wait_ge(ag_made, i + 1)
                nc.scalar.activation(sd[:, i:i + 1], mv[:, i, 1:2], ACT.Sqrt, bias=eps_ln[:, 0:1]).then_inc(sd_made, 1)

            deviation(0)
            for i in range(NTT):
                if i + 1 < NTT:
                    deviation(i + 1)
                act.wait_ge(x2_turn, i + 1)
                if i >= 2:
                    act.wait_ge(x2_lo, i - 1)
                    act.wait_ge(logit, i - 1)
                nc.scalar.activation(x2t[i % 2][:].rearrange("p a b -> p (a b)"), bank[2 + i % 2][:, 0:D], ACT.Copy).then_inc(x2t_kept, 1)
                act.wait_ge(x2t_kept, i + 1)
                nc.scalar.activation(x2_parts[:, 0, :, i * P:(i + 1) * P].bitcast(F16), x2t[i % 2][:], ACT.Copy).then_inc(x2_hi, 1)
                act.wait_ge(logit, i + 1)
                nc.scalar.activation(logits[:, i], bank[4 + i % 2][:, 0:E], ACT.Copy).then_inc(logit_kept, 1)

        @block.tensor
        def _(pe):
            mm = nc.tensor.matmul

            def project(i):
                pe.wait_ge(y_ld[i % 2], 32 * (i // 2 + 1))
                if i == 0:
                    pe.wait_ge(b_small, 112)
                if i >= 2:
                    pe.wait_ge(added, i - 1)
                for h in range(H):
                    last = mm(bank[i % 2][:, 0:D], y_in[i % 2][:, h], wo[:, h], start=(h == 0), stop=(h == H - 1))
                last.then_inc(outp, 1)

            def route(i):
                pe.wait_ge(x2_made, i + 1)
                if i >= 2:
                    pe.wait_ge(x2t_kept, i - 1)
                for k in range(KT):
                    last = nc.tensor.transpose(bank[2 + i % 2][:, k * P:(k + 1) * P], x2[:, i, k * P:(k + 1) * P], idf[:])
                last.then_inc(x2_turn, 1)
                pe.wait_ge(x2t_kept, i + 1)
                if i >= 2:
                    pe.wait_ge(logit_kept, i - 1)
                for k in range(KT):
                    last = mm(bank[4 + i % 2][:, 0:E], x2t[i % 2][:, k], gw[:, k], start=(k == 0), stop=(k == KT - 1))
                last.then_inc(logit, 1)

            project(0)
            for i in range(NTT):
                if i + 1 < NTT:
                    project(i + 1)
                route(i)

        @block.vector
        def _(dve):
            v = nc.vector

            def scale_rows(i):
                dve.wait_ge(sd_made, i + 1)
                v.reciprocal(rs[:, i:i + 1], sd[:, i:i + 1]).then_inc(rs_made, 1)
                dve.wait_ge(rs_made, i + 1)
                v.tensor_scalar(x2[:, i], xr[i % 2][:], mv[:, i, 0:1], rs[:, i:i + 1], ALU.subtract, ALU.mult)\
                    .then_inc(x2_made, 1)

            for i in range(NTT):
                dve.wait_ge(outp, i + 1)
                dve.wait_ge(y_ld[i % 2], 32 * (i // 2 + 1))
                v.tensor_tensor(xr[i % 2][:], bank[i % 2][:, 0:D], x_in_b[i % 2][:], ALU.add).then_inc(added, 1)
                dve.wait_ge(added, i + 1)
                v.bn_stats(stats[:], xr[i % 2][:]).then_inc(st_made, 1)
                dve.wait_ge(st_made, i + 1)
                v.bn_aggr(mv[:, i], stats[:]).then_inc(ag_made, 1)
                if i:
                    scale_rows(i - 1)
            scale_rows(NTT - 1)

    rt, ra, r_top, comb_turn, comb_kept, bias_made, acc_made = map(sem, (
        "route_dve", "route_act", "route_top", "comb_turn", "comb_kept", "bias_made", "acc_made"))
    with nc.Block() as block:
        @block.scalar
        def _(act):
            act.wait_ge(rt, 3)
            nc.scalar.activation(prob[:], tmp[:], ACT.Exp).then_inc(ra, 1)
            for i in range(NTT):
                act.wait_ge(comb_turn, i + 1)
                if i >= 2:
                    act.wait_ge(bias_made, i - 1)
                nc.scalar.activation(comb_t[i % 2][:], bank[i % 2][0:E, 0:P], ACT.Copy).then_inc(comb_kept, 1)

        @block.tensor
        def _(pe):
            pe.wait_ge(rt, 13)
            for i in range(NTT):
                if i >= 2:
                    pe.wait_ge(comb_kept, i - 1)
                nc.tensor.transpose(bank[i % 2][0:E, 0:P], pick[:, i], idf[:]).then_inc(comb_turn, 1)
                pe.wait_ge(comb_kept, i + 1)
                if i >= 2:
                    pe.wait_ge(acc_made, i - 1)
                nc.tensor.matmul(bank[2 + i % 2][:, 0:D], comb_t[i % 2][:], dbias[:], start=True, stop=True).then_inc(bias_made, 1)

        @block.vector
        def _(dve):
            v = nc.vector

            def step(ins, value):
                ins.then_inc(rt, 1)
                dve.wait_ge(rt, value)
            step(v.tensor_tensor(logits[:], logits[:], gb[:, None, :].broadcast_to([P, NTT, E]), ALU.add), 1)
            step(v.tensor_reduce(zsum[:], logits[:], AX.X, ALU.max), 2)
            step(v.tensor_tensor(tmp[:], logits[:], zsum[:, :, None].broadcast_to([P, NTT, E]), ALU.subtract), 3)
            dve.wait_ge(ra, 1)
            step(v.tensor_reduce(zsum[:], prob[:], AX.X, ALU.add), 4)
            step(v.reciprocal(zsum[:], zsum[:]), 5)
            step(v.tensor_tensor(prob[:], prob[:], zsum[:, :, None].broadcast_to([P, NTT, E]), ALU.mult), 6)
            for i in range(NTT):
                v.max(top[:, i], prob[:, i]).then_inc(r_top, 1)
            dve.wait_ge(r_top, NTT)
            for i in range(NTT):
                v.max_index(topi[:, i], top[:, i], prob[:, i]).then_inc(r_top, 1)
            dve.wait_ge(r_top, 2 * NTT)
            step(v.tensor_copy(topf[:], topi[:]), 7)
            ib = idx[:, None, :].broadcast_to([P, NTT, E])
            v.tensor_tensor(pick[:], ib, topf[:, :, 0:1].broadcast_to([P, NTT, E]), ALU.is_equal)
            step(v.tensor_tensor(tmp[:], ib, topf[:, :, 1:2].broadcast_to([P, NTT, E]), ALU.is_equal), 8)
            step(v.tensor_tensor(pick[:], pick[:], tmp[:], ALU.add), 9)
            step(v.tensor_tensor(zsum[:], top[:, :, 0], top[:, :, 1], ALU.add), 10)
            v.tensor_tensor(pick[:], pick[:], prob[:], ALU.mult)
            step(v.tensor_scalar(zsum[:], zsum[:], 1e-20, None, ALU.add), 11)
            step(v.reciprocal(zsum[:], zsum[:]), 12)
            step(v.tensor_tensor(pick[:], pick[:], zsum[:, :, None].broadcast_to([P, NTT, E]), ALU.mult), 13)
            for i in range(NTT):
                dve.wait_ge(bias_made, i + 1)
                v.tensor_tensor(x2[:, i], bank[2 + i % 2][:, 0:D], x2[:, i], ALU.add).then_inc(acc_made, 1)

    w_in = sem("ew_in")
    (w_hi, w_lo, ups, gates, u_kept, prods, h_made, h_high, h_low, downs, accs) = map(sem, (
        "ew_hi", "ew_lo", "ups", "gates", "u_kept", "prods", "h_made", "h_high", "h_low", "downs", "accs"))
    srcs = (up_w, gp_w, down_w)
    with nc.Block() as block:
        def width(k):
            return KT * FP if k < 2 else FT * D

        @block.sync
        def _(sp):
            for e in range(E):
                for k in range(3):
                    if e or k:
                        sp.wait_ge(w_lo, 3 * e + k)
                    sp.dma_start(stage[:, 0:width(k)], srcs[k][e]).then_inc(w_in, 16)

        @block.gpsimd
        def _(pool):
            def split(e):
                i = e % 2
                for k in range(3):
                    if e >= 2:
                        pool.wait_ge(downs, 4 * NB * (e - 1))
                    pool.wait_ge(w_in, 16 * (3 * e + k + 1))
                    nc.gpsimd.tensor_copy(wparts[i][k][:, 0, 0:width(k)].bitcast(F16), stage[:, 0:width(k)]).then_inc(w_hi, 1)
                    pool.wait_ge(w_hi, 3 * e + k + 1)
                    nc.gpsimd.tensor_tensor(wparts[i][k][:, 1, 0:width(k)].bitcast(BF16), stage[:, 0:width(k)],
                                            wparts[i][k][:, 0, 0:width(k)].bitcast(F16), ALU.subtract).then_inc(w_lo, 1)

            for e in range(E):
                split(e)

        @block.tensor
        def _(pe):
            mm = nc.tensor.matmul

            def three(out_ap, w, x, start, stop):
                pairs = ((0, 0), (0, 1), (1, 0))
                for j, (wp, xp) in enumerate(pairs):
                    last = mm(out_ap, w(wp), x(xp), start=(start and j == 0), stop=(stop and j == 2))
                return last

            for e in range(E):
                i = e % 2
                wu, wg, wd = wparts[i]
                pe.wait_ge(w_lo, 3 * e + 3)
                with pe.Fori(0, NB) as tb:
                    n = tb + e * NB
                    for f in range(FT):
                        m = P
                        ff = FT * n + f
                        for which, w in ((0, wu), (1, wg)):
                            b = bank[2 * (f % 2) + which]
                            if f >= 2 or e:
                                pe.wait_ge(prods, ff - 1)
                            for k in range(KT):
                                last = three(b[0:m, :],
                                             lambda wp: w[:, wp, k * FP + f * P:k * FP + f * P + m].bitcast(BF16 if wp else F16),
                                             lambda xp: x2_parts[:, xp, k, bass.ds(tb * 512, 512)].bitcast(BF16 if xp else F16),
                                             k == 0, k == KT - 1)
                            last.then_inc(ups if which == 0 else gates, 1)
                    pe.wait_ge(h_low, FT * (n + 1))
                    for s in range(4):
                        b = bank[4 + s]
                        if e:
                            pe.wait_ge(accs, 4 * (n - 1) + s + 1)
                        for f in range(FT):
                            m = P
                            last = three(b[:, 0:D],
                                         lambda hp: (h_lo if hp else h_hi)[0:m, f, s * P:(s + 1) * P],
                                         lambda wp: wd[0:m, wp, f * D:(f + 1) * D].bitcast(BF16 if wp else F16),
                                         f == 0, f == FT - 1)
                        last.then_inc(downs, 1)

        @block.scalar
        def _(act):
            a = nc.scalar.activation
            for e in range(E):
                with act.Fori(0, NB) as tb:
                    n = tb + e * NB

                    def silu(f):
                        m = P
                        act.wait_ge(prods, FT * n + f + 1)
                        if f >= 2 or e:
                            act.wait_ge(h_low, FT * n + f - 1)
                        a(h_sb[f % 2][0:m, :], prod[f % 2][0:m, :], ACT.Silu).then_inc(h_made, 1)
                        if f == 0 and e:
                            act.wait_ge(downs, 4 * n)
                        act.wait_ge(h_made, FT * n + f + 1)
                        a(h_hi[0:m, f, :], h_sb[f % 2][0:m, :], ACT.Copy).then_inc(h_high, 1)

                    for f in range(FT):
                        m = P
                        act.wait_ge(ups, FT * n + f + 1)
                        if f >= 2 or e:
                            act.wait_ge(prods, FT * n + f - 1)
                        a(u_sb[f % 2][0:m, :], bank[2 * (f % 2)][0:m, :], ACT.Identity, bias=upb[0:m, e, f:f + 1]).then_inc(u_kept, 1)
                        if f:
                            silu(f - 1)
                    silu(FT - 1)

        @block.vector
        def _(dve):
            v = nc.vector
            for e in range(E):
                with dve.Fori(0, NB) as tb:
                    n = tb + e * NB

                    def low(f):
                        m = P
                        dve.wait_ge(h_high, FT * n + f + 1)
                        v.tensor_tensor(h_lo[0:m, f, :], h_sb[f % 2][0:m, :], h_hi[0:m, f, :], ALU.subtract).then_inc(h_low, 1)

                    for f in range(FT):
                        m = P
                        dve.wait_ge(u_kept, FT * n + f + 1)
                        dve.wait_ge(gates, FT * n + f + 1)
                        if f >= 2 or e:
                            dve.wait_ge(h_made, FT * n + f - 1)
                        v.scalar_tensor_tensor(prod[f % 2][0:m, :], bank[2 * (f % 2) + 1][0:m, :], gpb[0:m, e, f:f + 1],
                                               u_sb[f % 2][0:m, :], ALU.add, ALU.mult).then_inc(prods, 1)
                        if f:
                            low(f - 1)
                    low(FT - 1)
                    for s in range(4):
                        dve.wait_ge(downs, 4 * n + s + 1)
                        acc = x2[:].rearrange("p a b -> p (a b)")[:, bass.ds((tb * 4 + s) * D, D)]
                        w = pick[:].rearrange("p a b -> p (a b)")[:, bass.ds((tb * 4 + s) * E + e, 1)]
                        v.scalar_tensor_tensor(acc, bank[4 + s][:, 0:D], w, acc, ALU.mult, ALU.add).then_inc(accs, 1)

    o_buf = [sb(f"o_buf{i}", [P, D], F32) for i in range(2)]
    f_stats = [sb(f"f_stats{i}", [P, 6], F32) for i in range(2)]
    f_st, f_ag, f_sd, f_rs, f_made = map(sem, ("f_st", "f_ag", "f_sd", "f_rs", "f_made"))
    f_out = [sem("f_out0"), sem("f_out1")]
    with nc.Block() as block:
        @block.sync
        def _(sp):
            for i in range(NTT):
                sp.wait_ge(f_made, i + 1)
                sp.dma_start(out[i * P:(i + 1) * P, :], o_buf[i % 2][:]).then_inc(f_out[i % 2], 16)
            for i in range(2):
                sp.wait_ge(f_out[i], 16 * (NTT // 2))

        @block.scalar
        def _(act):
            act.wait_ge(f_ag, NTT)
            nc.scalar.activation(sd[:], mv[:, :, 1], ACT.Sqrt, bias=eps_ln[:, 0:1]).then_inc(f_sd, 1)

        @block.vector
        def _(dve):
            v = nc.vector
            for i in range(NTT):
                if i >= 2:
                    dve.wait_ge(f_ag, i - 1)
                v.bn_stats(f_stats[i % 2][:], x2[:, i]).then_inc(f_st, 1)
                dve.wait_ge(f_st, i + 1)
                v.bn_aggr(mv[:, i], f_stats[i % 2][:]).then_inc(f_ag, 1)
            dve.wait_ge(f_sd, 1)
            v.reciprocal(rs[:], sd[:]).then_inc(f_rs, 1)
            dve.wait_ge(f_rs, 1)
            for i in range(NTT):
                if i >= 2:
                    dve.wait_ge(f_out[i % 2], 16 * (i // 2))
                v.tensor_scalar(o_buf[i % 2][:], x2[:, i], mv[:, i, 0:1], rs[:, i:i + 1], ALU.subtract, ALU.mult)\
                    .then_inc(f_made, 1)






def kernel(**inputs):
    import concourse.bacc as _bacc
    from concourse.bass_utils import run_bass_kernel_spmd as _run

    g = {k.replace("L0_attn_", "a_").replace("L0_ffn_", "f_"): np.asarray(v) for k, v in inputs.items()}
    x = g["a_x"]
    xt = np.zeros((P, KT, B, XW), np.float32)
    xt[:, :, :, TAPS - 1:TAPS - 1 + T] = x.reshape(B, T, KT, P).transpose(3, 2, 0, 1)

    def heads(w, n):
        return w.reshape(KT, P, n, H, DH).transpose(3, 1, 0, 2, 4)
    w_all = np.concatenate([heads(g["a_Wq"], 1), heads(g["a_Wk"], NH), heads(g["a_Wv"], NH), heads(g["a_Wg"], 1)], 3)
    wz = np.concatenate([g["a_Wb"], g["a_Wa"]], 1).reshape(KT, P, 32).transpose(1, 0, 2)

    def convs(w, n):
        return w.reshape(n, H, DH, TAPS).transpose(2, 1, 0, 3)
    cw = np.concatenate([convs(g["a_conv_q"], 1), convs(g["a_conv_k"], NH), convs(g["a_conv_v"], NH)], 2)
    consts, masks = constants()

    def padded(b):
        z = np.zeros((E, FT * P), np.float32)
        z[:, :F] = b
        return z.reshape(E, FT, P).transpose(2, 0, 1).reshape(P, E * FT)
    dw = np.zeros((E, FT * P, D), np.float32)
    dw[:, :F] = g["f_down_w"].transpose(0, 2, 1)

    def up(w):
        z = np.zeros((E, D, FP), np.float32)
        z[:, :, :F] = w.transpose(0, 2, 1)
        return z.reshape(E, KT, P, FP).transpose(0, 2, 1, 3).reshape(E, P, KT * FP)
    arrays = {
        "x_t": xt.reshape(P, -1), "x_rows": x.reshape(B * T, D), "w_all": w_all.reshape(H, P, KT * HC),
        "w_z": wz.reshape(P, -1), "conv_w": cw.reshape(P, -1),
        "a_log": np.broadcast_to(g["a_A_log"][None], (96, H)), "dt_bias": np.broadcast_to(g["a_dt_bias"][None], (96, H)),
        "rms_w": g["a_rms_weight"].reshape(P, 1),
        "w_o": g["a_Wo"].reshape(H, DH, D).transpose(1, 0, 2).reshape(P, H * D), "consts": consts, "masks": masks,
        "gate_w": g["f_gate_w"].T.reshape(KT, P, E).transpose(1, 0, 2).reshape(P, KT * E),
        "gate_b": np.broadcast_to(g["f_gate_b"][None], (P, E)),
        "up_w": up(g["f_up_w"]), "up_b": padded(g["f_up_b"]), "gp_w": up(g["f_gp_w"]), "gp_b": padded(g["f_gp_b"]),
        "down_w": dw.reshape(E, FT, P, D).transpose(0, 2, 1, 3).reshape(E, P, FT * D), "down_b": g["f_down_b"],
    }
    nc = _bacc.Bacc("TRN2", target_bir_lowering=False, num_devices=1)
    args, feed = [], {}
    for name, a in arrays.items():
        a = np.ascontiguousarray(a)
        feed["in_" + name] = a
        args.append(nc.dram_tensor("in_" + name, a.shape, mybir.dt.from_np(a.dtype), kind="ExternalInput").ap())
    args.append(nc.dram_tensor("out_y", (B * T, D), F32, kind="ExternalOutput").ap())
    build(nc, *args)
    r = _run(nc, [feed], core_ids=[0])
    return r.results[0]["out_y"].reshape(B, T, D)
```

```python
from contextlib import ExitStack

import numpy as np
import concourse.bass as bass
from concourse import mybir

F32 = mybir.dt.float32
F16 = mybir.dt.float16
BF16 = mybir.dt.bfloat16
U16 = mybir.dt.uint16
U32 = mybir.dt.uint32
ALU = mybir.AluOpType
ACT = mybir.ActivationFunctionType
AX = mybir.AxisListType

P = 128
B, T, D = 2, 2048, 256
KT = D // P
H, NH, DH = 8, 3, 128
TAPS = 4
CH = 32
UN = 8
TB = CH * UN
NTB = T // TB
NIT = B * H * NTB
XW = T + TAPS
PW = TB + TAPS - 1
NTILE = 2 * NH + 2
NCONV = NTILE - 1
HC = NTILE * DH
LEVELS = 7
E, F = 8, 816
FT = -(-F // P)
FP = FT * P
NTT = B * T // P
NB = B * T // 512
RING = 3
STAGES = 4
PEELED = 5
MASKED = -30000.0
EPS_K, EPS_RMS, EPS_LN = 1e-6, 1e-5, 1e-5



def constants():
    p = np.arange(P)
    j, t = p // CH, p % CH
    o = 4 * t + j
    before = (o[:, None] < o[None, :]) & (j[:, None] < NH)
    neg = np.where(before, 0.0, MASKED).astype(np.float32)
    masks = []
    for l in range(LEVELS):
        later, earlier = o[:, None], o[None, :]
        masks.append(((later >> (l + 1)) == (earlier >> (l + 1))) & ((later >> l) & 1 == 1) & ((earlier >> l) & 1 == 0))
    masks = np.stack([m.T for m in masks], 1).astype(np.float16)
    later_t = (t[:, None] > t[None, :]).astype(np.float32)
    upto_t = (t[:, None] <= t[None, :]).astype(np.float32)
    ident = np.eye(P, dtype=np.float32)
    ones = np.ones((P, P), np.float32)
    c = np.concatenate([ident, neg, later_t, upto_t, ones], 1)
    return c, np.ascontiguousarray(masks.reshape(P, LEVELS * P))


C_ID, C_NEG, C_LATER, C_UPTO, C_ONES = range(5)


def at_least(eng, sem, value):
    if isinstance(value, int) and value <= 0:
        return
    eng.wait_ge(sem, value)


def build(nc, x_t, x_rows, w_all, w_z, conv_w, a_log, dt_bias, rms_w, w_o, consts, masks,
          gate_w, gate_b, up_w, up_b, gp_w, gp_b, down_w, down_b, out):
    y_dram = nc.dram_tensor("y_scratch", (NIT, P, TB), F32).ap()
    w_dram = nc.dram_tensor("w_parts_scratch", (H, P, 2 * KT * HC), U16).ap()
    ctx = ExitStack()
    with ctx:
        def sem(name):
            return ctx.enter_context(nc.semaphore(name))

        attention_scope = ExitStack()
        scope = attention_scope

        def sb(name, shape, dt):
            return scope.enter_context(nc.sbuf_tensor(name, shape, dt))

        bank = [ctx.enter_context(nc.psum_tensor(f"bank{i}", [P, 512], F32)) for i in range(8)]

        cst = sb("cst", [P, 5, P], F32)
        x_parts = sb("x_parts", [P, 2, KT, B, XW], U16)
        tables = sb("tables", [P, NIT, 4, UN], F32)
        g_parts = sb("g_parts", [P, NIT, UN], BF16)
        conv_sb = sb("conv_sb", [P, H, NCONV, TAPS], F32)
        ident16 = sb("ident16", [P, P], F16)
        rep16 = sb("rep16", [P, 4, P], F16)
        negid16 = sb("negid16", [P, P], F16)
        identb = sb("identb", [P, P], BF16)
        negmask = sb("negmask", [P, P], BF16)
        laterb = sb("laterb", [P, P], BF16)
        uptob = sb("uptob", [P, P], BF16)
        onesb = sb("onesb", [P, P], BF16)
        mask_sb = sb("mask_sb", [P, LEVELS, P], F16)
        neg_rms = sb("neg_rms", [P, 1], F32)
        rms_raw = sb("rms_raw", [P, 1], F32)
        over_dh = sb("over_dh", [P, P], F32)
        eps_dh = sb("eps_dh", [P, P], F32)

        with ExitStack() as setup_scope:
            scope = setup_scope
            x_stage = sb("x_stage", [P, KT, B, XW], F32)
            w_stage = sb("w_stage", [P, 2, KT, HC], F32)
            w_pair = [sb(f"w_pair{i}", [P, 2, KT, HC], U16) for i in range(2)]
            wz_stage = sb("wz_stage", [P, KT, 32], F32)
            wz_parts = sb("wz_parts", [P, 2, KT, 32], U16)
            x_flat = x_stage[0:32].rearrange("p a b c -> p (a b c)")
            z_t, z_rows = x_flat[:, 0:B * T], x_flat[:, B * T:2 * B * T]
            beta = sb("beta", [P, B * H, T // CH], F32)
            g_full = sb("g_full", [P, B * H, T // CH], F32)
            work_a = sb("work_a", [P, B * H, T // CH], F32)
            work_b = sb("work_b", [P, B * H, T // CH], F32)
            g_hi = sb("g_hi", [P, B * H, T // CH], BF16)
            alog_sb = sb("alog_sb", [96, H], F32)
            dt_sb = sb("dt_sb", [96, H], F32)
            consts_in, x_in, z_in, small_in, x_split_a, x_split_b = map(
                sem, ("consts_in", "x_in", "z_in", "small_in", "x_highs", "x_lows"))
            w_in = [sem("w_in0"), sem("w_in1")]
            w_stored = [sem("w_stored0"), sem("w_stored1")]
            w_high, w_low, wz_high, wz_low = map(sem, ("w_high", "w_low", "wz_high", "wz_low"))
            zp_done, zt_done, tr_done, dv, ac, cum_done, casts, exp_cum = map(
                sem, ("z_projected", "z_evacuated", "z_turned", "setup_dve", "setup_act", "sums_done",
                      "consts_cast", "sums_exp"))
            with nc.Block() as block:
                @block.sync
                def _(sp):
                    sp.dma_start(x_stage[:].rearrange("p a b c -> p (a b c)"), x_t).then_inc(x_in, 16)
                    sp.dma_start(wz_stage[:].rearrange("p a b -> p (a b)"), w_z).then_inc(z_in, 16)
                    sp.dma_start(cst[:].rearrange("p a b -> p (a b)"), consts).then_inc(consts_in, 16)
                    sp.dma_start(mask_sb[:].rearrange("p a b -> p (a b)"), masks).then_inc(consts_in, 16)
                    sp.dma_start(conv_sb[:].rearrange("p a b c -> p (a b c)"), conv_w).then_inc(small_in, 16)
                    sp.dma_start(alog_sb[:], a_log).then_inc(small_in, 16)
                    sp.dma_start(dt_sb[:], dt_bias).then_inc(small_in, 16)
                    sp.dma_start(rms_raw[:], rms_w).then_inc(small_in, 16)
                    def load_head(h):
                        sp.dma_start(w_stage[:, h % 2].rearrange("p a b -> p (a b)"), w_all[h]).then_inc(w_in[h % 2], 16)

                    load_head(0)
                    load_head(1)
                    for h in range(H):
                        sp.wait_ge(w_low, h + 1)
                        sp.dma_start(w_dram[h], w_pair[h % 2][:].rearrange("p a b c -> p (a b c)")).then_inc(w_stored[h % 2], 16)
                        if h + 2 < H:
                            load_head(h + 2)
                    for i in range(2):
                        sp.wait_ge(w_stored[i], 16 * (H // 2))

                @block.gpsimd
                def _(pool):
                    for h in range(H):
                        pool.wait_ge(w_high, h + 1)
                        nc.gpsimd.tensor_tensor(w_pair[h % 2][:, 1].bitcast(BF16), w_stage[:, h % 2],
                                                w_pair[h % 2][:, 0].bitcast(F16), ALU.subtract).then_inc(w_low, 1)

                @block.scalar
                def _(act):
                    act.wait_ge(z_in, 16)
                    nc.scalar.activation(wz_parts[:, 0].bitcast(F16), wz_stage[:], ACT.Copy).then_inc(wz_high, 1)
                    act.wait_ge(x_in, 16)
                    for k in range(KT):
                        nc.scalar.activation(x_parts[:, 0, k].bitcast(F16), x_stage[:, k], ACT.Copy).then_inc(x_split_a, 1)
                    act.wait_ge(small_in, 64)
                    nc.scalar.activation(alog_sb[:], alog_sb[:], ACT.Exp).then_inc(ac, 1)
                    nc.scalar.activation(neg_rms[:], rms_raw[:], ACT.Copy, scale=-1.0)
                    act.wait_ge(dv, 2)
                    nc.scalar.activation(beta[0:96], work_a[0:96], ACT.Exp).then_inc(ac, 1)
                    act.wait_ge(dv, 4)
                    nc.scalar.activation(work_a[0:96], g_full[0:96], ACT.Abs).then_inc(ac, 1)
                    act.wait_ge(ac, 3)
                    nc.scalar.activation(work_a[0:96], work_a[0:96], ACT.Exp, scale=-1.0).then_inc(ac, 1)
                    act.wait_ge(ac, 4)
                    nc.scalar.activation(work_a[0:96], work_a[0:96], ACT.Ln, bias=1.0).then_inc(ac, 1)
                    for i in range(6):
                        act.wait_ge(cum_done, i + 1)
                        kind, half = i // 2, i % 2
                        dst = tables[:, half * (NIT // 2):(half + 1) * (NIT // 2), 1 + kind, :]
                        nc.scalar.activation(dst, bank[i][:].rearrange("p (a b) -> p a b", b=UN), ACT.Exp)\
                            .then_inc(exp_cum, 1)
                    for h in range(H):
                        act.wait_ge(w_in[h % 2], 16 * (h // 2 + 1))
                        if h >= 2:
                            act.wait_ge(w_stored[h % 2], 16 * (h // 2))
                        nc.scalar.activation(w_pair[h % 2][:, 0].bitcast(F16), w_stage[:, h % 2], ACT.Copy).then_inc(w_high, 1)

                @block.tensor
                def _(pe):
                    pe.wait_ge(x_split_b, KT)
                    pe.wait_ge(wz_low, 1)
                    for i in range(NB):
                        b, c0 = i // (NB // B), TAPS - 1 + (i % (NB // B)) * 512
                        first = True
                        for k in range(KT):
                            for wp, xp in ((0, 0), (0, 1), (1, 0)):
                                w = wz_parts[:, wp, k].bitcast(BF16 if wp else F16)
                                xx = x_parts[:, xp, k, b, c0:c0 + 512].bitcast(BF16 if xp else F16)
                                last = nc.tensor.matmul(bank[i][0:32, :], w, xx, start=first,
                                                        stop=(k == KT - 1 and wp == 1))
                                first = False
                        last.then_inc(zp_done, 1)
                    pe.wait_ge(dv, 12)
                    pe.wait_ge(zt_done, NB)
                    for i in range(6):
                        kind, half = i // 2, i % 2
                        w = (laterb, uptob, onesb)[kind]
                        rhs = g_parts[0:96, half * (NIT // 2):(half + 1) * (NIT // 2), :].rearrange("p a b -> p (a b)")
                        nc.tensor.matmul(bank[i][:], w[0:96, :], rhs, start=True, stop=True).then_inc(cum_done, 1)

                @block.vector
                def _(dve):
                    v = nc.vector
                    dve.wait_ge(wz_high, 1)
                    v.tensor_tensor(wz_parts[:, 1].bitcast(BF16), wz_stage[:], wz_parts[:, 0].bitcast(F16),
                                    ALU.subtract).then_inc(wz_low, 1)
                    for k in range(KT):
                        dve.wait_ge(x_split_a, k + 1)
                        v.tensor_tensor(x_parts[:, 1, k].bitcast(BF16), x_stage[:, k], x_parts[:, 0, k].bitcast(F16),
                                        ALU.subtract).then_inc(x_split_b, 1)
                    dve.wait_ge(consts_in, 32)
                    v.tensor_copy(ident16[:], cst[:, C_ID]).then_inc(casts, 1)
                    for u in range(4):
                        v.tensor_copy(rep16[:, u], cst[:, C_ID])
                    v.tensor_scalar(negid16[:], cst[:, C_ID], -1.0, None, ALU.mult)
                    v.tensor_copy(identb[:], cst[:, C_ID])
                    v.tensor_copy(negmask[:], cst[:, C_NEG])
                    v.tensor_copy(laterb[:], cst[:, C_LATER])
                    v.tensor_copy(uptob[:], cst[:, C_UPTO])
                    v.tensor_copy(onesb[:], cst[:, C_ONES])
                    v.memset(over_dh[:], 1.0 / DH)
                    v.memset(eps_dh[:], EPS_RMS * DH)
                    v.memset(beta[96:128], 0.0)
                    v.memset(g_parts[96:128], 0.0)
                    for i in range(NB):
                        dve.wait_ge(zp_done, i + 1)
                        v.tensor_copy(z_t[:, i * 512:(i + 1) * 512], bank[i][0:32, :]).then_inc(zt_done, 1)
                    dve.wait_ge(zt_done, NB)
                    v.transpose(z_rows, z_t).then_inc(tr_done, 1)
                    dve.wait_ge(tr_done, 1)
                    zv = z_rows.rearrange("p (b c j h) -> p b h c j", b=B, j=4, h=H)
                    for b in range(B):
                        for j in range(NH):
                            last = v.tensor_scalar(work_a[32 * j:32 * j + 32, b * H:(b + 1) * H, :], zv[:, b, :, :, j],
                                                   -1.0, 80.0, ALU.mult, ALU.min)
                            last = v.tensor_copy(g_full[32 * j:32 * j + 32, b * H:(b + 1) * H, :], zv[:, b, :, :, 3])
                    last.then_inc(dv, 2)
                    dve.wait_ge(ac, 2)
                    v.tensor_scalar(beta[0:96], beta[0:96], 1.0, None, ALU.add).then_inc(dv, 1)
                    dve.wait_ge(dv, 3)
                    v.reciprocal(beta[0:96], beta[0:96])
                    dve.wait_ge(small_in, 64)
                    dtb = dt_sb[:].rearrange("p (o h u) -> p o h u", o=1, u=1).broadcast_to([96, B, H, T // CH])
                    gv = g_full[0:96].rearrange("p (b h) c -> p b h c", b=B)
                    for b in range(B):
                        last = v.tensor_tensor(gv[:, b], gv[:, b], dtb[:, b], ALU.add)
                    last.then_inc(dv, 1)
                    dve.wait_ge(dv, 4)
                    v.tensor_scalar(beta[0:96], beta[0:96], 2.0, None, ALU.mult)
                    v.tensor_scalar(work_b[0:96], g_full[0:96], 0.0, None, ALU.max).then_inc(dv, 2)
                    dve.wait_ge(ac, 5)
                    dve.wait_ge(dv, 6)
                    v.tensor_tensor(work_a[0:96], work_a[0:96], work_b[0:96], ALU.add).then_inc(dv, 1)
                    dve.wait_ge(dv, 7)
                    ab = alog_sb[:].rearrange("p (h u) -> p h u", u=1).broadcast_to([96, H, T // CH])
                    wa = work_a[0:96].rearrange("p (b h) c -> p b h c", b=B)
                    for b in range(B):
                        last = v.tensor_tensor(gv[:, b], wa[:, b], ab, ALU.mult)
                    last.then_inc(dv, 1)
                    dve.wait_ge(dv, 8)
                    v.tensor_scalar(g_full[0:96], g_full[0:96], -1.0, None, ALU.mult).then_inc(dv, 1)
                    dve.wait_ge(dv, 9)
                    gp = g_parts[:].rearrange("p n u -> p (n u)")
                    gf = g_full[:].rearrange("p n u -> p (n u)")
                    gh = g_hi[:].rearrange("p n u -> p (n u)")
                    v.tensor_copy(gp[0:96], gf[0:96])
                    v.tensor_copy(gh[0:96], gf[0:96]).then_inc(dv, 1)
                    dve.wait_ge(dv, 10)
                    v.tensor_tensor(gf[0:96], gf[0:96], gh[0:96], ALU.subtract).then_inc(dv, 1)
                    dve.wait_ge(dv, 11)
                    v.tensor_copy(gp[32:64], gf[32:64])
                    v.tensor_copy(gh[64:96], gf[64:96]).then_inc(tr_done, 1)
                    dve.wait_ge(tr_done, 2)
                    v.tensor_tensor(gp[64:96], gf[64:96], gh[64:96], ALU.subtract).then_inc(dv, 1)
                    bt = beta[:].rearrange("p a (n u) -> p (a n) u", u=UN)
                    v.tensor_scalar(tables[:, :, 0, :], bt, -1.0, None, ALU.mult)
                    dve.wait_ge(exp_cum, 6)
                    v.tensor_tensor(tables[:, :, 1, :], tables[:, :, 1, :], bt, ALU.mult)
                    v.tensor_scalar(tables[:, :, 2, :], tables[:, :, 2, :], -1.0, None, ALU.mult).then_inc(dv, 1)
                    dve.wait_ge(dv, 13)
                    v.memset(tables[:, ::NTB, 2:4, 0:1], 0.0)

        with ExitStack() as loop_scope:
            scope = loop_scope

            def ring(name, shape, dt):
                return [sb(f"{name}{i}", shape, dt) for i in range(RING)]

            x_cur = ring("x_cur", [P, 2, KT, PW + 1], U16)
            w_cur = ring("w_cur", [P, 2, KT, HC], U16)
            c_cur = ring("c_cur", [P, NCONV, TAPS], F32)
            t_cur = ring("t_cur", [P, 4, UN], F32)
            g_cur = ring("g_cur", [P, UN], BF16)
            kq_t = ring("kq_t", [P, UN, 4, CH], F32)
            k_rows = ring("k_rows", [P, UN, P], F32)
            v_rows = ring("v_rows", [P, UN, P], F32)
            inv_t = ring("inv_t", [P, UN, P], F32)
            gate = ring("gate", [P, TB], F32)
            squares = ring("squares", [P, UN, 4, CH], F32)
            y_buf = ring("y_buf", [P, TB], F32)
            v_t = ring("v_t", [P, UN, NH, CH], F32)
            conv_acc = [sb(f"conv_acc{i}", [P, TB], F32) for i in range(2)]
            g_upto = sb("g_upto", [96, UN, CH], BF16)
            decay = [sb(f"decay{g}", [P, 4, P], F32) for g in range(2)]
            n_t = [sb(f"n_t{g}", [P, 4, P], F32) for g in range(2)]
            n_high = [sb(f"n_high{g}", [P, 4, P], F16) for g in range(2)]
            n_low = [sb(f"n_low{g}", [P, 4, P], BF16) for g in range(2)]
            inv = [sb(f"inv{g}", [P, 4, P], F16) for g in range(2)]
            invt = [sb(f"invt{g}", [P, 4, P], F16) for g in range(2)]
            xs = [sb(f"xs{g}", [P, 4, P], F16) for g in range(2)]
            n_lev = [[sb(f"n_lev{g}_{i}", [P, 4, P], F16) for i in range(2)] for g in range(2)]
            sv = sb("sv", [P, UN], F32)
            k_sq = sb("k_sq", [P, UN], F32)
            ln_k = sb("ln_k", [P, UN], F32)
            ln_v = sb("ln_v", [P, TB], F32)
            eps_var = sb("eps_var", [P, 1], F32)
            r2 = sb("r2", [P, UN], F32)
            c_n = sb("c_n", [P, UN], F32)
            c_k = sb("c_k", [P, UN], F32)
            state = sb("state", [P, P], F32)
            rhs = [sb(f"rhs{i}", [P, P], F32) for i in range(2)]
            w_sol = [sb(f"w_sol{i}", [P, P], F32) for i in range(2)]
            o_sq = sb("o_sq", [P, TB], F32)
            rstd = sb("rstd", [P, TB], F32)
            o_norm = sb("o_norm", [P, TB], F32)

            loaded = [sem(f"loaded{i}") for i in range(RING)]
            tabled = [sem(f"tabled{i}") for i in range(RING)]
            stored = [sem(f"stored{i}") for i in range(RING)]
            sp_waited = sem("sp_waited")
            projected, tap0, tap_step, tapped, silu_done, gate_done, squared, summed, k_sq_made, small_step, g_made = map(
                sem, ("projected", "tap0", "tap_step", "tapped", "silu_done", "gate_done", "squared", "summed",
                      "k_sq_made", "small_step", "g_made"))
            (grammed, decay_sum, decayed, ln_made, norm_made, n_made, high_made, low_made, l0_step, l0_made, l0_turned,
             inv_made, levelled, x_made, x_kept, t_made, tt_made, t_kept, tt_kept, k_turned, k_kept, v_turned,
             v_kept, res_made, res_kept, fix_made, fix_kept) = map(sem, (
                "grammed", "decay_sum", "decayed", "ln_made", "norm_made", "n_made", "high_made", "low_made",
                "l0_step", "l0_made", "l0_turned", "inv_made", "levelled", "x_made", "x_kept", "t_made", "tt_made",
                "t_kept", "tt_kept", "k_turned", "k_kept", "v_turned", "v_kept", "res_made", "res_kept",
                "fix_made", "fix_kept"))
            zeroed, ks_made, rhs_made, sol_made, sol_kept, out_made, upd_made, stated, osq_made, var_made, var_ln, \
                rstd_made, normed, gated = map(sem, (
                    "zeroed", "ks_made", "rhs_made", "sol_made", "sol_kept", "out_made", "upd_made", "stated",
                    "osq_made", "var_made", "var_ln", "rstd_made", "normed", "gated"))
            LV = LEVELS - 1
            OUT = bank[7][:, 0:TB]
            VAR = bank[7][:, TB:2 * TB]
            KS = bank[6][:, 0:P]

            def run_bodies(eng, body, peeled=PEELED):
                for n in range(peeled):
                    body(n, n // RING, n % RING)
                rounds = (NIT - peeled) // RING
                assert peeled + rounds * RING == NIT
                with eng.Fori(0, rounds) as m:
                    for i in range(peeled, peeled + RING):
                        turn = m + i // RING
                        body(RING * turn + i % RING, turn, i % RING)
                for n in range(NIT, NIT + STAGES - 1):
                    body(n, n // RING, n % RING)

            def stage(n, turn, res, back):
                runs = not isinstance(n, int) or 0 <= n - back < NIT
                return runs, n - back, (res - back) % RING, turn - (1 if res < back else 0)

            def skip(stage_index):
                def wrap(f):
                    def g(*args):
                        if stage_index[0]:
                            f(*args)
                    return g
                return wrap

            with nc.Block() as block:
                @block.sync
                def _(sp):
                    def load(n, res):
                        b, h, tb = n // (H * NTB), (n // NTB) % H, n % NTB
                        sp.dma_start(x_cur[res][:, :, :, 0:PW].rearrange("p a b c -> p (a b) c"),
                                     x_parts[:].rearrange("p a k b c -> p (a k) (b c)")[:, :, bass.ds(b * XW + tb * TB, PW)])\
                            .then_inc(loaded[res], 16)
                        sp.dma_start(w_cur[res][:].rearrange("p a b c -> p (a b c)"),
                                     w_dram.rearrange("h p c -> (h p) c")[bass.ds(h * P, P), :]).then_inc(loaded[res], 16)
                        sp.dma_start(c_cur[res][:].rearrange("p a b -> p (a b)"),
                                     conv_sb[:].rearrange("p h a b -> p (h a b)")[:, bass.ds(h * (NCONV * TAPS), NCONV * TAPS)])\
                            .then_inc(loaded[res], 16)
                        sp.dma_start(g_cur[res][:], g_parts[:].rearrange("p n a -> p (n a)")[:, bass.ds(n * UN, UN)])\
                            .then_inc(loaded[res], 16)

                    def body(n, turn, res):
                        (a, _, _, _), (d, nd, rd, _) = stage(n, turn, res, 0), stage(n, turn, res, 3)
                        if a:
                            at_least(sp, stated, UN * (n - 2))
                            sp.sem_inc(sp_waited, 1)
                            sp.dma_start(t_cur[res][:].rearrange("p a b -> p (a b)"),
                                         tables[:].rearrange("p n a b -> p (n a b)")[:, bass.ds(n * (4 * UN), 4 * UN)])\
                                .then_inc(tabled[res], 16)
                        if a and not (isinstance(n, int) and n + 1 >= NIT):
                            for used, count in ((projected, NTILE), (tapped, NCONV), (g_made, 1)):
                                at_least(sp, used, count * (n - 1))
                                sp.sem_inc(sp_waited, 1)
                            load(n + 1, (res + 1) % RING)
                        if d:
                            sp.wait_ge(gated, nd + 1)
                            sp.sem_inc(sp_waited, 1)
                            dst = y_dram[nd] if isinstance(nd, int) else y_dram.rearrange("n p t -> (n p) t")[bass.ds(nd * P, P), :]
                            sp.dma_start(dst, y_buf[rd][:]).then_inc(stored[rd], 16)

                    load(0, 0)
                    for n in range(PEELED):
                        body(n, n // RING, n % RING)
                    rounds = (NIT - PEELED) // RING - 1
                    with sp.Fori(0, rounds) as m:
                        for i in range(PEELED, PEELED + RING):
                            turn = m + i // RING
                            body(RING * turn + i % RING, turn, i % RING)
                    for n in range(NIT - RING, NIT + STAGES - 1):
                        body(n, n // RING, n % RING)
                    for i in range(RING):
                        sp.wait_ge(stored[i], 16 * len(range(i, NIT, RING)))

                @block.tensor
                def _(pe):
                    mm = nc.tensor.matmul

                    def body(n, turn, res):
                        sa, sb_, sc = (stage(n, turn, res, k) for k in range(3))
                        nb, rb = sb_[1:3]

                        def nth(l, g):
                            return 2 * LV * nb + 2 * (l - 1) + g

                        r, rc = sc[1:3]

                        @skip(sa)
                        def project(c):
                            if c == 0:
                                pe.wait_ge(loaded[res], 64 * (turn + 1))
                                at_least(pe, k_sq_made, n)
                            elif c == 1:
                                at_least(pe, gate_done, n)
                            else:
                                pe.wait_ge(tapped, NCONV * n + c - 1)
                            first = True
                            for k in range(KT):
                                for wp, xp in ((0, 0), (0, 1), (1, 0)):
                                    last = mm(bank[c % 2][:, 0:PW],
                                              w_cur[res][:, wp, k, c * P:(c + 1) * P].bitcast(BF16 if wp else F16),
                                              x_cur[res][:, xp, k, 0:PW].bitcast(BF16 if xp else F16),
                                              start=first, stop=(k == KT - 1 and wp == 1))
                                    first = False
                            last.then_inc(projected, 1)

                        @skip(sa)
                        def norms():
                            pe.wait_ge(squared, n + 1)
                            pe.wait_ge(tapped, NCONV * n + NCONV)
                            for u in range(UN):
                                last = mm(bank[0][:, u:u + 1], squares[res][:, u].rearrange("p a b -> p (a b)"),
                                          cst[:, C_ONES, 0:1], start=True, stop=True)
                            last.then_inc(summed, 1)

                        @skip(sb_)
                        def gram(g):
                            if g == 0:
                                pe.wait_ge(silu_done, NCONV * nb + 4)
                            if g == 0:
                                at_least(pe, v_kept, 2 * nb)
                            else:
                                at_least(pe, tt_kept, 2 * LV * nb)
                            for u in range(4):
                                a = kq_t[rb][:, 4 * g + u].rearrange("p a b -> p (a b)")
                                last = mm(bank[2 + g][:, u * P:(u + 1) * P], a, a, start=True, stop=True)
                            last.then_inc(grammed, 1)

                        @skip(sb_)
                        def decays(g):
                            if g == 0:
                                pe.wait_ge(g_made, nb + 1)
                            at_least(pe, fix_kept, 2 * nb - 1 + g)
                            mm(bank[4 + g][:], laterb[0:96, :],
                               g_upto[:, 4 * g:4 * g + 4, None, :].broadcast_to([96, 4, 4, CH]),
                               start=True, stop=False)
                            mm(bank[4 + g][:], identb[:], negmask[:, None, :].broadcast_to([P, 4, P]),
                               start=False, stop=True).then_inc(decay_sum, 1)

                        @skip(sb_)
                        def turn_keys(g):
                            if g == 0:
                                pe.wait_ge(n_made, UN * nb + 4)
                            else:
                                pe.wait_ge(k_kept, 2 * nb + 1)
                            for u in range(4):
                                last = nc.tensor.transpose(bank[2][:, u * P:(u + 1) * P],
                                                           kq_t[rb][:, 4 * g + u].rearrange("p a b -> p (a b)"), cst[:, C_ID])
                            last.then_inc(k_turned, 1)

                        @skip(sb_)
                        def turn_values(g):
                            if g == 0:
                                pe.wait_ge(k_kept, 2 * nb + 2)
                            else:
                                pe.wait_ge(v_kept, 2 * nb + 1)
                            pe.wait_ge(silu_done, NCONV * nb + NCONV)
                            for u in range(4):
                                last = nc.tensor.transpose(bank[2][0:96, u * P:(u + 1) * P],
                                                           v_t[rb][:, 4 * g + u].rearrange("p a b -> p (a b)"), cst[:, C_ID])
                            last.then_inc(v_turned, 1)

                        def turn_units(g, src):
                            dst = bank[4 + g][:].bitcast(F16)
                            for u in range(4):
                                last = nc.tensor.transpose(dst[:, u * P:(u + 1) * P], src[:, u], ident16[:])
                            return last

                        @skip(sb_)
                        def turn0(g):
                            pe.wait_ge(l0_made, 2 * nb + g + 1)
                            turn_units(g, invt[g]).then_inc(l0_turned, 1)

                        @skip(sb_)
                        def level_x(l, g):
                            pe.wait_ge(levelled, nth(l, g) + 1)
                            if l == 1:
                                pe.wait_ge(inv_made, 2 * nb + g + 1)
                            else:
                                pe.wait_ge(t_kept, nth(l - 1, g) + 1)
                            for u in range(4):
                                last = mm(bank[4 + g][:, u * P:(u + 1) * P], n_lev[g][l % 2][:, u], inv[g][:, u], start=True, stop=True)
                            last.then_inc(x_made, 1)

                        @skip(sb_)
                        def level_t(l, g):
                            pe.wait_ge(x_kept, nth(l, g) + 1)
                            if l > 1:
                                pe.wait_ge(tt_kept, nth(l - 1, g) + 1)
                            for u in range(4):
                                last = mm(bank[4 + g][:, u * P:(u + 1) * P], invt[g][:, u], xs[g][:, u], start=True, stop=True)
                            last.then_inc(t_made, 1)

                        @skip(sb_)
                        def level_tt(l, g):
                            pe.wait_ge(x_kept, nth(l, g) + 1)
                            if l == 1:
                                pe.wait_ge(n_made, UN * nb + UN)
                            at_least(pe, tt_kept, nth(l, g))
                            for u in range(4):
                                last = mm(bank[3][:, u * P:(u + 1) * P], xs[g][:, u], invt[g][:, u], start=True, stop=True)
                            last.then_inc(tt_made, 1)

                        @skip(sb_)
                        def residual(g):
                            pe.wait_ge(t_kept, nth(LV, g) + 1)
                            pe.wait_ge(low_made, 2 * nb + g + 1)
                            flat = bank[4 + g][:]
                            mm(flat, ident16[:], rep16[:].rearrange("p a b -> p (a b)"), start=True, stop=False)
                            mm(flat, negid16[:], inv[g][:].rearrange("p a b -> p (a b)"), start=False, stop=False)
                            for part in (n_high, n_low):
                                for u in range(4):
                                    last = mm(flat[:, u * P:(u + 1) * P], part[g][:, u], inv[g][:, u], start=False,
                                              stop=(part is n_low and u == 3))
                            last.then_inc(res_made, 1)

                        @skip(sb_)
                        def fix(g):
                            pe.wait_ge(res_kept, 2 * nb + g + 1)
                            pe.wait_ge(tt_kept, nth(LV, g) + 1)
                            flat = bank[4 + g][:]
                            mm(flat, ident16[:], invt[g][:].rearrange("p a b -> p (a b)"), start=True, stop=False)
                            for u in range(4):
                                last = mm(flat[:, u * P:(u + 1) * P], xs[g][:, u], invt[g][:, u], start=False, stop=(u == 3))
                            last.then_inc(fix_made, 1)

                        @skip(sc)
                        def from_state(c):
                            if c == 0:
                                pe.wait_ge(fix_kept, 2 * r + 2)
                                pe.wait_ge(zeroed, 1)
                            at_least(pe, stated, UN * r + c)
                            mm(KS, kq_t[rc][:, c].rearrange("p a b -> p (a b)"), state[:], start=True, stop=True)\
                                .then_inc(ks_made, 1)

                        @skip(sc)
                        def solve(c):
                            pe.wait_ge(rhs_made, UN * r + c + 1)
                            mm(KS, inv_t[rc][:, c], rhs[c % 2][:], start=True, stop=True).then_inc(sol_made, 1)

                        @skip(sc)
                        def output(c):
                            pe.wait_ge(rhs_made, UN * r + c + 1)
                            if c == 0:
                                at_least(pe, normed, r)
                            mm(OUT[:, c * CH:(c + 1) * CH], rhs[c % 2][:], inv_t[rc][:, c, 96:128], start=True,
                               stop=True).then_inc(out_made, 1)

                        @skip(sc)
                        def update(c):
                            pe.wait_ge(sol_kept, UN * r + c + 1)
                            mm(KS, k_rows[rc][:, c], w_sol[c % 2][:], start=True, stop=True).then_inc(upd_made, 1)

                        @skip(sc)
                        def variance():
                            pe.wait_ge(osq_made, r + 1)
                            mm(VAR, over_dh[:], o_sq[:], start=True, stop=False)
                            mm(VAR, eps_dh[:], squares[rc][:, :, 3, :], start=False, stop=True).then_inc(var_made, 1)

                        from_state(0)
                        decays(0)
                        gram(0)
                        decays(1)
                        gram(1)
                        solve(0)
                        project(0)
                        update(0)
                        turn_keys(0)
                        from_state(1)
                        output(0)
                        project(1)
                        output(1)
                        solve(1)
                        turn0(0)
                        turn0(1)
                        update(1)
                        level_x(1, 0)
                        from_state(2)
                        level_x(1, 1)
                        level_t(1, 0)
                        level_tt(1, 0)
                        solve(2)
                        project(2)
                        update(2)
                        level_x(2, 0)
                        output(2)
                        level_t(1, 1)
                        level_tt(1, 1)
                        from_state(3)
                        level_t(2, 0)
                        level_x(2, 1)
                        level_tt(2, 0)
                        solve(3)
                        level_x(3, 0)
                        output(3)
                        level_t(2, 1)
                        level_tt(2, 1)
                        update(3)
                        project(3)
                        level_x(3, 1)
                        level_t(3, 0)
                        from_state(4)
                        level_tt(3, 0)
                        turn_keys(1)
                        level_t(3, 1)
                        level_x(4, 0)
                        solve(4)
                        output(4)
                        level_tt(3, 1)
                        update(4)
                        level_x(4, 1)
                        level_t(4, 0)
                        level_tt(4, 0)
                        project(4)
                        level_x(5, 0)
                        level_t(4, 1)
                        from_state(5)
                        level_tt(4, 1)
                        turn_values(0)
                        level_t(5, 0)
                        solve(5)
                        level_x(5, 1)
                        level_tt(5, 0)
                        project(5)
                        update(5)
                        level_t(5, 1)
                        level_x(6, 0)
                        output(5)
                        level_tt(5, 1)
                        from_state(6)
                        turn_values(1)
                        level_x(6, 1)
                        level_t(6, 0)
                        level_tt(6, 0)
                        solve(6)
                        output(6)
                        project(6)
                        update(6)
                        level_t(6, 1)
                        residual(0)
                        from_state(7)
                        level_tt(6, 1)
                        residual(1)
                        solve(7)
                        project(7)
                        output(7)
                        fix(0)
                        update(7)
                        fix(1)
                        norms()
                        variance()

                    run_bodies(pe, body)

                @block.scalar
                def _(act):
                    a = nc.scalar.activation

                    def body(n, turn, res):
                        sa, sb_, sc, sd = (stage(n, turn, res, k) for k in range(4))
                        nb, rb = sb_[1:3]

                        def nth(l, g):
                            return 2 * LV * nb + 2 * (l - 1) + g

                        r = sc[1]
                        d = sd[1]

                        @skip(sa)
                        def first_tap(c):
                            act.wait_ge(projected, NTILE * n + c + 1)
                            at_least(act, silu_done, NCONV * n + max(c - 1, 0))
                            a(conv_acc[c % 2][:], bank[c % 2][:, 0:TB], ACT.Copy, scale=c_cur[res][:, c, 0:1]).then_inc(tap0, 1)

                        @skip(sa)
                        def silu(c):
                            act.wait_ge(tapped, NCONV * n + c + 1)
                            if c == 0:
                                dst = kq_t[res][:, :, 3, :]
                            elif c < 4:
                                dst = kq_t[res][:, :, c - 1, :]
                            else:
                                dst = v_t[res][:, :, c - 4, :]
                            a(dst, conv_acc[c % 2][:].rearrange("p (u t) -> p u t", u=UN), ACT.Silu).then_inc(silu_done, 1)

                        @skip(sa)
                        def gate_silu():
                            act.wait_ge(projected, NTILE * n + NTILE)
                            at_least(act, gated, n - 2)
                            a(gate[res][:], bank[1][:, TAPS - 1:PW], ACT.Silu).then_inc(gate_done, 1)

                        @skip(sb_)
                        def exp_decay(g):
                            act.wait_ge(decay_sum, 2 * nb + g + 1)
                            a(decay[g][:].rearrange("p a b -> p (a b)"), bank[4 + g][:], ACT.Exp).then_inc(decayed, 1)

                        @skip(sb_)
                        def key_norms():
                            act.wait_ge(k_sq_made, nb + 1)
                            a(ln_k[:], k_sq[:], ACT.Ln).then_inc(ln_made, 1)
                            act.wait_ge(ln_made, nb + 1)
                            at_least(act, v_kept, 2 * nb)
                            a(sv[:], ln_k[:], ACT.Exp, scale=0.5).then_inc(norm_made, 1)

                        @skip(sd)
                        def root_variance():
                            act.wait_ge(var_made, d + 1)
                            act.wait_ge(zeroed, 1)
                            a(ln_v[:], VAR, ACT.Ln, bias=eps_var[:, 0:1]).then_inc(var_ln, 1)
                            act.wait_ge(var_ln, d + 1)
                            a(rstd[:], ln_v[:], ACT.Exp, scale=-0.5).then_inc(rstd_made, 1)

                        @skip(sb_)
                        def high(g):
                            act.wait_ge(n_made, UN * nb + 4 * g + 4)
                            a(n_high[g][:], n_t[g][:], ACT.Copy).then_inc(high_made, 1)

                        @skip(sb_)
                        def keep0(g):
                            act.wait_ge(l0_turned, 2 * nb + g + 1)
                            a(inv[g][:].rearrange("p a b -> p (a b)"), bank[4 + g][:].bitcast(F16)[:, 0:4 * P], ACT.Copy)\
                                .then_inc(inv_made, 1)

                        @skip(sb_)
                        def keep_t(l, g):
                            act.wait_ge(t_made, nth(l, g) + 1)
                            a(inv[g][:].rearrange("p a b -> p (a b)"), bank[4 + g][:], ACT.Copy).then_inc(t_kept, 1)

                        @skip(sb_)
                        def keep_tt(l, g):
                            act.wait_ge(tt_made, nth(l, g) + 1)
                            a(invt[g][:].rearrange("p a b -> p (a b)"), bank[3][:], ACT.Copy).then_inc(tt_kept, 1)

                        @skip(sb_)
                        def keep_res(g):
                            act.wait_ge(res_made, 2 * nb + g + 1)
                            a(xs[g][:].rearrange("p a b -> p (a b)"), bank[4 + g][:], ACT.Copy).then_inc(res_kept, 1)

                        @skip(sb_)
                        def keep_fix(g):
                            act.wait_ge(fix_made, 2 * nb + g + 1)
                            a(inv_t[rb][:, 4 * g:4 * g + 4].rearrange("p a b -> p (a b)"), bank[4 + g][:], ACT.Copy)\
                                .then_inc(fix_kept, 1)

                        @skip(sc)
                        def keep_w(c):
                            act.wait_ge(sol_made, UN * r + c + 1)
                            a(w_sol[c % 2][:], KS, ACT.Copy).then_inc(sol_kept, 1)

                        @skip(sc)
                        def square_out():
                            act.wait_ge(out_made, UN * r + UN)
                            a(o_sq[:], OUT, ACT.Square).then_inc(osq_made, 1)

                        nc.scalar.preload_act_table_set("natural_log_exp_and_others")
                        root_variance()
                        exp_decay(0)
                        exp_decay(1)
                        key_norms()
                        keep_w(0)
                        high(0)
                        first_tap(0)
                        high(1)
                        first_tap(1)
                        keep_w(1)
                        keep0(0)
                        keep0(1)
                        silu(0)
                        keep_t(1, 0)
                        keep_w(2)
                        keep_tt(1, 0)
                        first_tap(2)
                        keep_t(1, 1)
                        keep_tt(1, 1)
                        keep_t(2, 0)
                        keep_tt(2, 0)
                        keep_w(3)
                        keep_t(2, 1)
                        silu(1)
                        keep_tt(2, 1)
                        keep_t(3, 0)
                        keep_tt(3, 0)
                        first_tap(3)
                        keep_t(3, 1)
                        keep_w(4)
                        keep_tt(3, 1)
                        keep_t(4, 0)
                        keep_tt(4, 0)
                        silu(2)
                        keep_t(4, 1)
                        keep_tt(4, 1)
                        first_tap(4)
                        keep_w(5)
                        keep_t(5, 0)
                        keep_tt(5, 0)
                        silu(3)
                        keep_t(5, 1)
                        first_tap(5)
                        keep_tt(5, 1)
                        keep_t(6, 0)
                        keep_w(6)
                        keep_tt(6, 0)
                        silu(4)
                        keep_t(6, 1)
                        first_tap(6)
                        keep_res(0)
                        keep_tt(6, 1)
                        silu(5)
                        keep_w(7)
                        keep_res(1)
                        square_out()
                        keep_fix(0)
                        keep_fix(1)
                        gate_silu()
                        silu(6)

                    run_bodies(act, body)

                @block.vector
                def _(dve):
                    v = nc.vector
                    v.memset(state[:], 0.0)
                    v.memset(eps_var[:], EPS_RMS * DH * EPS_K)
                    for i in range(RING):
                        last = v.memset(v_rows[i][96:128], 0.0)
                    last.then_inc(zeroed, 1)

                    def body(n, turn, res):
                        sa, sb_, sc, sd = (stage(n, turn, res, k) for k in range(4))
                        nb, rb = sb_[1:3]

                        def nth(l, g):
                            return 2 * LV * nb + 2 * (l - 1) + g

                        r, rc = sc[1:3]
                        d = sd[1]

                        @skip(sa)
                        def tap(c, i):
                            acc = conv_acc[c % 2][:]
                            if i == 1:
                                dve.wait_ge(tap0, NCONV * n + c + 1)
                            else:
                                dve.wait_ge(tap_step, (TAPS - 2) * (NCONV * n + c) + i - 1)
                            v.scalar_tensor_tensor(acc, bank[c % 2][:, i:i + TB], c_cur[res][:, c, i:i + 1], acc, ALU.mult,
                                                   ALU.add).then_inc(tap_step if i < TAPS - 1 else tapped, 1)

                        @skip(sa)
                        def small():
                            dve.wait_ge(summed, n + 1)
                            at_least(dve, ln_made, n)
                            v.tensor_scalar(k_sq[:], bank[0][:, 0:UN], EPS_K, None, ALU.add).then_inc(k_sq_made, 1)
                            dve.wait_ge(k_sq_made, n + 1)
                            v.reciprocal(r2[:], k_sq[:]).then_inc(small_step, 1)
                            dve.wait_ge(small_step, 3 * n + 1)
                            dve.wait_ge(tabled[res], 16 * (turn + 1))
                            v.tensor_tensor(c_n[:], r2[:], t_cur[res][:, 0, :], ALU.mult).then_inc(small_step, 1)
                            v.tensor_tensor(c_k[:], r2[:], t_cur[res][:, 1, :], ALU.mult).then_inc(small_step, 1)

                        @skip(sb_)
                        def system(g):
                            dve.wait_ge(small_step, 3 * nb + 3)
                            dve.wait_ge(grammed, 2 * nb + g + 1)
                            dve.wait_ge(decayed, 2 * nb + g + 1)
                            at_least(dve, low_made, 2 * nb)
                            for u in range(4):
                                v.scalar_tensor_tensor(n_t[g][:, u], bank[2 + g][:, u * P:(u + 1) * P],
                                                       c_n[:, 4 * g + u:4 * g + u + 1], decay[g][:, u],
                                                       ALU.mult, ALU.mult).then_inc(n_made, 1)

                        @skip(sb_)
                        def level0(g):
                            dve.wait_ge(high_made, 2 * nb + g + 1)
                            v.tensor_tensor(invt[g][:], n_high[g][:], mask_sb[:, 0, None, :].broadcast_to([P, 4, P]), ALU.mult)\
                                .then_inc(l0_step, 1)
                            dve.wait_ge(l0_step, 2 * nb + g + 1)
                            v.tensor_tensor(invt[g][:], invt[g][:], rep16[:], ALU.add).then_inc(l0_made, 1)

                        @skip(sb_)
                        def keep_k(g):
                            dve.wait_ge(k_turned, 2 * nb + g + 1)
                            v.tensor_tensor(k_rows[rb][:, 4 * g:4 * g + 4], bank[2][:].rearrange("p (a b) -> p a b", a=4),
                                            c_k[:, 4 * g:4 * g + 4, None].broadcast_to([P, 4, P]), ALU.mult).then_inc(k_kept, 1)

                        @skip(sb_)
                        def keep_v(g):
                            dve.wait_ge(v_turned, 2 * nb + g + 1)
                            dve.wait_ge(norm_made, nb + 1)
                            v.tensor_tensor(v_rows[rb][0:96, 4 * g:4 * g + 4],
                                            bank[2][0:96, :].rearrange("p (a b) -> p a b", a=4),
                                            sv[0:96, 4 * g:4 * g + 4, None].broadcast_to([96, 4, P]), ALU.mult).then_inc(v_kept, 1)

                        @skip(sb_)
                        def plus_one(l, g):
                            dve.wait_ge(x_made, nth(l, g) + 1)
                            v.tensor_tensor(xs[g][:], bank[4 + g][:].rearrange("p (a b) -> p a b", a=4), rep16[:], ALU.add)\
                                .then_inc(x_kept, 1)

                        @skip(sc)
                        def right_side(c):
                            dve.wait_ge(ks_made, UN * r + c + 1)
                            at_least(dve, out_made, UN * r + c - 1)
                            v.scalar_tensor_tensor(rhs[c % 2][:], KS, t_cur[rc][:, 2, c:c + 1], v_rows[rc][:, c],
                                                   ALU.mult, ALU.add).then_inc(rhs_made, 1)

                        @skip(sc)
                        def new_state(c):
                            dve.wait_ge(upd_made, UN * r + c + 1)
                            v.scalar_tensor_tensor(state[:], state[:], t_cur[rc][:, 3, c:c + 1], KS,
                                                   ALU.mult, ALU.add).then_inc(stated, 1)

                        @skip(sd)
                        def normalize():
                            dve.wait_ge(rstd_made, d + 1)
                            at_least(dve, gated, d)
                            v.scalar_tensor_tensor(o_norm[:], OUT, neg_rms[:, 0:1], rstd[:], ALU.mult, ALU.mult)\
                                .then_inc(normed, 1)

                        right_side(0)
                        normalize()
                        system(0)
                        system(1)
                        new_state(0)
                        level0(0)
                        right_side(1)
                        level0(1)
                        tap(0, 1)
                        tap(0, 2)
                        new_state(1)
                        plus_one(1, 0)
                        tap(0, 3)
                        right_side(2)
                        tap(1, 1)
                        plus_one(1, 1)
                        tap(1, 2)
                        new_state(2)
                        plus_one(2, 0)
                        keep_k(0)
                        right_side(3)
                        plus_one(2, 1)
                        tap(1, 3)
                        plus_one(3, 0)
                        tap(2, 1)
                        new_state(3)
                        tap(2, 2)
                        plus_one(3, 1)
                        right_side(4)
                        tap(2, 3)
                        keep_k(1)
                        plus_one(4, 0)
                        tap(3, 1)
                        plus_one(4, 1)
                        new_state(4)
                        tap(3, 2)
                        plus_one(5, 0)
                        right_side(5)
                        tap(3, 3)
                        keep_v(0)
                        plus_one(5, 1)
                        tap(4, 1)
                        new_state(5)
                        tap(4, 2)
                        plus_one(6, 0)
                        right_side(6)
                        tap(4, 3)
                        plus_one(6, 1)
                        tap(5, 1)
                        new_state(6)
                        tap(5, 2)
                        tap(5, 3)
                        right_side(7)
                        keep_v(1)
                        tap(6, 1)
                        tap(6, 2)
                        tap(6, 3)
                        new_state(7)
                        small()

                    run_bodies(dve, body)

                @block.gpsimd
                def _(pool):
                    tt = nc.gpsimd.tensor_tensor

                    def body(n, turn, res):
                        sa, sb_, sd = (stage(n, turn, res, k) for k in (0, 1, 3))
                        nb = sb_[1]
                        _, d, rd, turns_d = sd

                        @skip(sa)
                        def g_rows():
                            pool.wait_ge(loaded[res], 64 * (turn + 1))
                            at_least(pool, decay_sum, 2 * n)
                            tt(g_upto[:], g_cur[res][0:96, :, None].broadcast_to([96, UN, CH]),
                               uptob[0:96, None, 0:CH].broadcast_to([96, UN, CH]), ALU.mult).then_inc(g_made, 1)

                        @skip(sa)
                        def square():
                            pool.wait_ge(silu_done, NCONV * n + 4)
                            tt(squares[res][:], kq_t[res][:], kq_t[res][:], ALU.mult).then_inc(squared, 1)

                        @skip(sb_)
                        def low(g):
                            pool.wait_ge(high_made, 2 * nb + g + 1)
                            at_least(pool, res_made, 2 * nb)
                            tt(n_low[g][:], n_t[g][:], n_high[g][:], ALU.subtract).then_inc(low_made, 1)

                        @skip(sb_)
                        def level_rows(l, g):
                            before = 2 * LV * nb + 2 * (l - 1) + g
                            pool.wait_ge(high_made, 2 * nb + g + 1)
                            at_least(pool, x_made, before - 3)
                            tt(n_lev[g][l % 2][:], n_high[g][:], mask_sb[:, l, None, :].broadcast_to([P, 4, P]), ALU.mult)\
                                .then_inc(levelled, 1)

                        @skip(sd)
                        def gated_out():
                            pool.wait_ge(normed, d + 1)
                            pool.wait_ge(gate_done, d + 1)
                            at_least(pool, stored[rd], 16 * turns_d)
                            tt(y_buf[rd][:], o_norm[:], gate[rd][:], ALU.mult).then_inc(gated, 1)

                        level_rows(1, 0)
                        level_rows(1, 1)
                        level_rows(2, 0)
                        level_rows(2, 1)
                        level_rows(3, 0)
                        level_rows(3, 1)
                        level_rows(4, 0)
                        level_rows(4, 1)
                        g_rows()
                        level_rows(5, 0)
                        low(0)
                        level_rows(5, 1)
                        low(1)
                        gated_out()
                        level_rows(6, 0)
                        level_rows(6, 1)
                        square()
                    run_bodies(pool, body, PEELED + RING)

        attention_scope.close()
        experts(nc, ctx, bank, y_dram, x_rows, w_o, consts, gate_w, gate_b, up_w, up_b, gp_w, gp_b, down_w, down_b, out)


def experts(nc, ctx, bank, y_dram, x_rows, w_o, consts, gate_w, gate_b, up_w, up_b, gp_w, gp_b, down_w, down_b, out):
    def sem(name):
        return ctx.enter_context(nc.semaphore(name))

    def sb(name, shape, dt):
        return ctx.enter_context(nc.sbuf_tensor(name, shape, dt))

    wo = sb("wo", [P, H, D], F32)
    x2 = sb("x2", [P, NTT, D], F32)
    x2_parts = sb("x2_parts", [P, 2, KT, B * T], U16)
    y_in = [sb(f"y_in{i}", [P, H, P], F32) for i in range(2)]
    x_in_b = [sb(f"x_in{i}", [P, D], F32) for i in range(2)]
    xr = [sb(f"xr{i}", [P, D], F32) for i in range(2)]
    x2t = [sb(f"x2t{i}", [P, KT, P], F32) for i in range(2)]
    stats = sb("stats", [P, 6], F32)
    mv = sb("mv", [P, NTT, 2], F32)
    sd = sb("sd", [P, NTT], F32)
    rs = sb("rs", [P, NTT], F32)
    eps_ln = sb("eps_ln", [P, 1], F32)
    idf = sb("idf", [P, P], F32)
    gw = sb("gw", [P, KT, E], F32)
    gb = sb("gb", [P, E], F32)
    logits = sb("logits", [P, NTT, E], F32)
    top = sb("top", [P, NTT, 8], F32)
    topi = sb("topi", [P, NTT, 8], U32)
    topf = sb("topf", [P, NTT, 8], F32)
    prob = sb("prob", [P, NTT, E], F32)
    tmp = sb("tmp", [P, NTT, E], F32)
    pick = sb("pick", [P, NTT, E], F32)
    zsum = sb("zsum", [P, NTT], F32)
    idx = sb("idx", [P, E], F32)
    comb_t = [sb(f"comb_t{i}", [E, P], F32) for i in range(2)]
    dbias = sb("dbias", [E, D], F32)
    upb = sb("upb", [P, E, FT], F32)
    gpb = sb("gpb", [P, E, FT], F32)
    WCOL = max(KT * FP, FT * D)
    stage = sb("stage", [P, WCOL], F32)
    wparts = [[sb(f"ew{i}_{k}", [P, 2, WCOL], U16) for k in range(3)] for i in range(2)]
    u_sb = [sb(f"u_sb{i}", [P, 512], F32) for i in range(2)]
    prod = [sb(f"prod{i}", [P, 512], F32) for i in range(2)]
    h_sb = [sb(f"h_sb{i}", [P, 512], F32) for i in range(2)]
    h_hi = sb("h_hi", [P, FT, 512], F16)
    h_lo = sb("h_lo", [P, FT, 512], BF16)

    b_small = sem("b_small")
    y_ld = [sem("y_ld0"), sem("y_ld1")]
    (outp, added, st_made, ag_made, rs_made, x2_made, x2_turn, x2t_kept, x2_hi, x2_lo, logit, logit_kept) = map(sem, (
        "outp", "added", "st_made", "ag_made", "rs_made", "x2_made", "x2_turn", "x2t_kept", "x2_hi", "x2_lo", "logit",
        "logit_kept"))
    idx_set = sem("idx_set")
    sd_made = sem("sd_made")
    with nc.Block() as block:
        @block.sync
        def _(sp):
            for dst, src in ((wo[:].rearrange("p a b -> p (a b)"), w_o), (idf[:], consts[:, 0:P]),
                             (gw[:].rearrange("p a b -> p (a b)"), gate_w), (gb[:], gate_b), (dbias[:], down_b),
                             (upb[:].rearrange("p a b -> p (a b)"), up_b), (gpb[:].rearrange("p a b -> p (a b)"), gp_b)):
                sp.dma_start(dst, src).then_inc(b_small, 16)
            yv = y_dram.rearrange("(b h t) p c -> b t p h c", b=B, h=H)
            for i in range(NTT):
                b, tb, half = i // (NTT // B), (i % (NTT // B)) // 2, i % 2
                if i >= 2:
                    sp.wait_ge(outp, i - 1)
                    sp.wait_ge(added, i - 1)
                sp.dma_start(y_in[i % 2][:], yv[b, tb, :, :, half * P:(half + 1) * P]).then_inc(y_ld[i % 2], 16)
                sp.dma_start(x_in_b[i % 2][:], x_rows[i * P:(i + 1) * P, :]).then_inc(y_ld[i % 2], 16)

        @block.gpsimd
        def _(pool):
            nc.gpsimd.memset(eps_ln[:], EPS_LN).then_inc(idx_set, 1)
            nc.gpsimd.iota(topi[:, 0, :], pattern=[[1, E]], base=0, channel_multiplier=0).then_inc(idx_set, 1)
            pool.wait_ge(idx_set, 2)
            nc.gpsimd.tensor_copy(idx[:], topi[:, 0, :]).then_inc(idx_set, 1)
            for i in range(NTT):
                pool.wait_ge(x2_hi, i + 1)
                nc.gpsimd.tensor_tensor(x2_parts[:, 1, :, i * P:(i + 1) * P].bitcast(BF16), x2t[i % 2][:],
                                        x2_parts[:, 0, :, i * P:(i + 1) * P].bitcast(F16), ALU.subtract).then_inc(x2_lo, 1)

        @block.scalar
        def _(act):
            act.wait_ge(idx_set, 2)

            def deviation(i):
                act.wait_ge(ag_made, i + 1)
                nc.scalar.activation(sd[:, i:i + 1], mv[:, i, 1:2], ACT.Sqrt, bias=eps_ln[:, 0:1]).then_inc(sd_made, 1)

            deviation(0)
            for i in range(NTT):
                if i + 1 < NTT:
                    deviation(i + 1)
                act.wait_ge(x2_turn, i + 1)
                if i >= 2:
                    act.wait_ge(x2_lo, i - 1)
                    act.wait_ge(logit, i - 1)
                nc.scalar.activation(x2t[i % 2][:].rearrange("p a b -> p (a b)"), bank[2 + i % 2][:, 0:D], ACT.Copy).then_inc(x2t_kept, 1)
                act.wait_ge(x2t_kept, i + 1)
                nc.scalar.activation(x2_parts[:, 0, :, i * P:(i + 1) * P].bitcast(F16), x2t[i % 2][:], ACT.Copy).then_inc(x2_hi, 1)
                act.wait_ge(logit, i + 1)
                nc.scalar.activation(logits[:, i], bank[4 + i % 2][:, 0:E], ACT.Copy).then_inc(logit_kept, 1)

        @block.tensor
        def _(pe):
            mm = nc.tensor.matmul

            def project(i):
                pe.wait_ge(y_ld[i % 2], 32 * (i // 2 + 1))
                if i == 0:
                    pe.wait_ge(b_small, 112)
                if i >= 2:
                    pe.wait_ge(added, i - 1)
                for h in range(H):
                    last = mm(bank[i % 2][:, 0:D], y_in[i % 2][:, h], wo[:, h], start=(h == 0), stop=(h == H - 1))
                last.then_inc(outp, 1)

            def route(i):
                pe.wait_ge(x2_made, i + 1)
                if i >= 2:
                    pe.wait_ge(x2t_kept, i - 1)
                for k in range(KT):
                    last = nc.tensor.transpose(bank[2 + i % 2][:, k * P:(k + 1) * P], x2[:, i, k * P:(k + 1) * P], idf[:])
                last.then_inc(x2_turn, 1)
                pe.wait_ge(x2t_kept, i + 1)
                if i >= 2:
                    pe.wait_ge(logit_kept, i - 1)
                for k in range(KT):
                    last = mm(bank[4 + i % 2][:, 0:E], x2t[i % 2][:, k], gw[:, k], start=(k == 0), stop=(k == KT - 1))
                last.then_inc(logit, 1)

            project(0)
            for i in range(NTT):
                if i + 1 < NTT:
                    project(i + 1)
                route(i)

        @block.vector
        def _(dve):
            v = nc.vector

            def scale_rows(i):
                dve.wait_ge(sd_made, i + 1)
                v.reciprocal(rs[:, i:i + 1], sd[:, i:i + 1]).then_inc(rs_made, 1)
                dve.wait_ge(rs_made, i + 1)
                v.tensor_scalar(x2[:, i], xr[i % 2][:], mv[:, i, 0:1], rs[:, i:i + 1], ALU.subtract, ALU.mult)\
                    .then_inc(x2_made, 1)

            for i in range(NTT):
                dve.wait_ge(outp, i + 1)
                dve.wait_ge(y_ld[i % 2], 32 * (i // 2 + 1))
                v.tensor_tensor(xr[i % 2][:], bank[i % 2][:, 0:D], x_in_b[i % 2][:], ALU.add).then_inc(added, 1)
                dve.wait_ge(added, i + 1)
                v.bn_stats(stats[:], xr[i % 2][:]).then_inc(st_made, 1)
                dve.wait_ge(st_made, i + 1)
                v.bn_aggr(mv[:, i], stats[:]).then_inc(ag_made, 1)
                if i:
                    scale_rows(i - 1)
            scale_rows(NTT - 1)

    rt, ra, r_top, comb_turn, comb_kept, bias_made, acc_made = map(sem, (
        "route_dve", "route_act", "route_top", "comb_turn", "comb_kept", "bias_made", "acc_made"))
    with nc.Block() as block:
        @block.scalar
        def _(act):
            act.wait_ge(rt, 3)
            nc.scalar.activation(prob[:], tmp[:], ACT.Exp).then_inc(ra, 1)
            for i in range(NTT):
                act.wait_ge(comb_turn, i + 1)
                if i >= 2:
                    act.wait_ge(bias_made, i - 1)
                nc.scalar.activation(comb_t[i % 2][:], bank[i % 2][0:E, 0:P], ACT.Copy).then_inc(comb_kept, 1)

        @block.tensor
        def _(pe):
            pe.wait_ge(rt, 13)
            for i in range(NTT):
                if i >= 2:
                    pe.wait_ge(comb_kept, i - 1)
                nc.tensor.transpose(bank[i % 2][0:E, 0:P], pick[:, i], idf[:]).then_inc(comb_turn, 1)
                pe.wait_ge(comb_kept, i + 1)
                if i >= 2:
                    pe.wait_ge(acc_made, i - 1)
                nc.tensor.matmul(bank[2 + i % 2][:, 0:D], comb_t[i % 2][:], dbias[:], start=True, stop=True).then_inc(bias_made, 1)

        @block.vector
        def _(dve):
            v = nc.vector

            def step(ins, value):
                ins.then_inc(rt, 1)
                dve.wait_ge(rt, value)
            step(v.tensor_tensor(logits[:], logits[:], gb[:, None, :].broadcast_to([P, NTT, E]), ALU.add), 1)
            step(v.tensor_reduce(zsum[:], logits[:], AX.X, ALU.max), 2)
            step(v.tensor_tensor(tmp[:], logits[:], zsum[:, :, None].broadcast_to([P, NTT, E]), ALU.subtract), 3)
            dve.wait_ge(ra, 1)
            step(v.tensor_reduce(zsum[:], prob[:], AX.X, ALU.add), 4)
            step(v.reciprocal(zsum[:], zsum[:]), 5)
            step(v.tensor_tensor(prob[:], prob[:], zsum[:, :, None].broadcast_to([P, NTT, E]), ALU.mult), 6)
            for i in range(NTT):
                v.max(top[:, i], prob[:, i]).then_inc(r_top, 1)
            dve.wait_ge(r_top, NTT)
            for i in range(NTT):
                v.max_index(topi[:, i], top[:, i], prob[:, i]).then_inc(r_top, 1)
            dve.wait_ge(r_top, 2 * NTT)
            step(v.tensor_copy(topf[:], topi[:]), 7)
            ib = idx[:, None, :].broadcast_to([P, NTT, E])
            v.tensor_tensor(pick[:], ib, topf[:, :, 0:1].broadcast_to([P, NTT, E]), ALU.is_equal)
            step(v.tensor_tensor(tmp[:], ib, topf[:, :, 1:2].broadcast_to([P, NTT, E]), ALU.is_equal), 8)
            step(v.tensor_tensor(pick[:], pick[:], tmp[:], ALU.add), 9)
            step(v.tensor_tensor(zsum[:], top[:, :, 0], top[:, :, 1], ALU.add), 10)
            v.tensor_tensor(pick[:], pick[:], prob[:], ALU.mult)
            step(v.tensor_scalar(zsum[:], zsum[:], 1e-20, None, ALU.add), 11)
            step(v.reciprocal(zsum[:], zsum[:]), 12)
            step(v.tensor_tensor(pick[:], pick[:], zsum[:, :, None].broadcast_to([P, NTT, E]), ALU.mult), 13)
            for i in range(NTT):
                dve.wait_ge(bias_made, i + 1)
                v.tensor_tensor(x2[:, i], bank[2 + i % 2][:, 0:D], x2[:, i], ALU.add).then_inc(acc_made, 1)

    w_in = sem("ew_in")
    (w_hi, w_lo, ups, gates, u_kept, prods, h_made, h_high, h_low, downs, accs) = map(sem, (
        "ew_hi", "ew_lo", "ups", "gates", "u_kept", "prods", "h_made", "h_high", "h_low", "downs", "accs"))
    srcs = (up_w, gp_w, down_w)
    with nc.Block() as block:
        def width(k):
            return KT * FP if k < 2 else FT * D

        @block.sync
        def _(sp):
            for e in range(E):
                for k in range(3):
                    if e or k:
                        sp.wait_ge(w_lo, 3 * e + k)
                    sp.dma_start(stage[:, 0:width(k)], srcs[k][e]).then_inc(w_in, 16)

        @block.gpsimd
        def _(pool):
            def split(e):
                i = e % 2
                for k in range(3):
                    if e >= 2:
                        pool.wait_ge(downs, 4 * NB * (e - 1))
                    pool.wait_ge(w_in, 16 * (3 * e + k + 1))
                    nc.gpsimd.tensor_copy(wparts[i][k][:, 0, 0:width(k)].bitcast(F16), stage[:, 0:width(k)]).then_inc(w_hi, 1)
                    pool.wait_ge(w_hi, 3 * e + k + 1)
                    nc.gpsimd.tensor_tensor(wparts[i][k][:, 1, 0:width(k)].bitcast(BF16), stage[:, 0:width(k)],
                                            wparts[i][k][:, 0, 0:width(k)].bitcast(F16), ALU.subtract).then_inc(w_lo, 1)

            for e in range(E):
                split(e)

        @block.tensor
        def _(pe):
            mm = nc.tensor.matmul

            def three(out_ap, w, x, start, stop):
                pairs = ((0, 0), (0, 1), (1, 0))
                for j, (wp, xp) in enumerate(pairs):
                    last = mm(out_ap, w(wp), x(xp), start=(start and j == 0), stop=(stop and j == 2))
                return last

            for e in range(E):
                i = e % 2
                wu, wg, wd = wparts[i]
                pe.wait_ge(w_lo, 3 * e + 3)
                with pe.Fori(0, NB) as tb:
                    n = tb + e * NB
                    for f in range(FT):
                        m = P
                        ff = FT * n + f
                        for which, w in ((0, wu), (1, wg)):
                            b = bank[2 * (f % 2) + which]
                            if f >= 2 or e:
                                pe.wait_ge(prods, ff - 1)
                            for k in range(KT):
                                last = three(b[0:m, :],
                                             lambda wp: w[:, wp, k * FP + f * P:k * FP + f * P + m].bitcast(BF16 if wp else F16),
                                             lambda xp: x2_parts[:, xp, k, bass.ds(tb * 512, 512)].bitcast(BF16 if xp else F16),
                                             k == 0, k == KT - 1)
                            last.then_inc(ups if which == 0 else gates, 1)
                    pe.wait_ge(h_low, FT * (n + 1))
                    for s in range(4):
                        b = bank[4 + s]
                        if e:
                            pe.wait_ge(accs, 4 * (n - 1) + s + 1)
                        for f in range(FT):
                            m = P
                            last = three(b[:, 0:D],
                                         lambda hp: (h_lo if hp else h_hi)[0:m, f, s * P:(s + 1) * P],
                                         lambda wp: wd[0:m, wp, f * D:(f + 1) * D].bitcast(BF16 if wp else F16),
                                         f == 0, f == FT - 1)
                        last.then_inc(downs, 1)

        @block.scalar
        def _(act):
            a = nc.scalar.activation
            for e in range(E):
                with act.Fori(0, NB) as tb:
                    n = tb + e * NB

                    def silu(f):
                        m = P
                        act.wait_ge(prods, FT * n + f + 1)
                        if f >= 2 or e:
                            act.wait_ge(h_low, FT * n + f - 1)
                        a(h_sb[f % 2][0:m, :], prod[f % 2][0:m, :], ACT.Silu).then_inc(h_made, 1)
                        if f == 0 and e:
                            act.wait_ge(downs, 4 * n)
                        act.wait_ge(h_made, FT * n + f + 1)
                        a(h_hi[0:m, f, :], h_sb[f % 2][0:m, :], ACT.Copy).then_inc(h_high, 1)

                    for f in range(FT):
                        m = P
                        act.wait_ge(ups, FT * n + f + 1)
                        if f >= 2 or e:
                            act.wait_ge(prods, FT * n + f - 1)
                        a(u_sb[f % 2][0:m, :], bank[2 * (f % 2)][0:m, :], ACT.Identity, bias=upb[0:m, e, f:f + 1]).then_inc(u_kept, 1)
                        if f:
                            silu(f - 1)
                    silu(FT - 1)

        @block.vector
        def _(dve):
            v = nc.vector
            for e in range(E):
                with dve.Fori(0, NB) as tb:
                    n = tb + e * NB

                    def low(f):
                        m = P
                        dve.wait_ge(h_high, FT * n + f + 1)
                        v.tensor_tensor(h_lo[0:m, f, :], h_sb[f % 2][0:m, :], h_hi[0:m, f, :], ALU.subtract).then_inc(h_low, 1)

                    for f in range(FT):
                        m = P
                        dve.wait_ge(u_kept, FT * n + f + 1)
                        dve.wait_ge(gates, FT * n + f + 1)
                        if f >= 2 or e:
                            dve.wait_ge(h_made, FT * n + f - 1)
                        v.scalar_tensor_tensor(prod[f % 2][0:m, :], bank[2 * (f % 2) + 1][0:m, :], gpb[0:m, e, f:f + 1],
                                               u_sb[f % 2][0:m, :], ALU.add, ALU.mult).then_inc(prods, 1)
                        if f:
                            low(f - 1)
                    low(FT - 1)
                    for s in range(4):
                        dve.wait_ge(downs, 4 * n + s + 1)
                        acc = x2[:].rearrange("p a b -> p (a b)")[:, bass.ds((tb * 4 + s) * D, D)]
                        w = pick[:].rearrange("p a b -> p (a b)")[:, bass.ds((tb * 4 + s) * E + e, 1)]
                        v.scalar_tensor_tensor(acc, bank[4 + s][:, 0:D], w, acc, ALU.mult, ALU.add).then_inc(accs, 1)

    o_buf = [sb(f"o_buf{i}", [P, D], F32) for i in range(2)]
    f_stats = [sb(f"f_stats{i}", [P, 6], F32) for i in range(2)]
    f_st, f_ag, f_sd, f_rs, f_made = map(sem, ("f_st", "f_ag", "f_sd", "f_rs", "f_made"))
    f_out = [sem("f_out0"), sem("f_out1")]
    with nc.Block() as block:
        @block.sync
        def _(sp):
            for i in range(NTT):
                sp.wait_ge(f_made, i + 1)
                sp.dma_start(out[i * P:(i + 1) * P, :], o_buf[i % 2][:]).then_inc(f_out[i % 2], 16)
            for i in range(2):
                sp.wait_ge(f_out[i], 16 * (NTT // 2))

        @block.scalar
        def _(act):
            act.wait_ge(f_ag, NTT)
            nc.scalar.activation(sd[:], mv[:, :, 1], ACT.Sqrt, bias=eps_ln[:, 0:1]).then_inc(f_sd, 1)

        @block.vector
        def _(dve):
            v = nc.vector
            for i in range(NTT):
                if i >= 2:
                    dve.wait_ge(f_ag, i - 1)
                v.bn_stats(f_stats[i % 2][:], x2[:, i]).then_inc(f_st, 1)
                dve.wait_ge(f_st, i + 1)
                v.bn_aggr(mv[:, i], f_stats[i % 2][:]).then_inc(f_ag, 1)
            dve.wait_ge(f_sd, 1)
            v.reciprocal(rs[:], sd[:]).then_inc(f_rs, 1)
            dve.wait_ge(f_rs, 1)
            for i in range(NTT):
                if i >= 2:
                    dve.wait_ge(f_out[i % 2], 16 * (i // 2))
                v.tensor_scalar(o_buf[i % 2][:], x2[:, i], mv[:, i, 0:1], rs[:, i:i + 1], ALU.subtract, ALU.mult)\
                    .then_inc(f_made, 1)






def kernel(**inputs):
    import concourse.bacc as _bacc
    from concourse.bass_utils import run_bass_kernel_spmd as _run

    g = {k.replace("L0_attn_", "a_").replace("L0_ffn_", "f_"): np.asarray(v) for k, v in inputs.items()}
    x = g["a_x"]
    xt = np.zeros((P, KT, B, XW), np.float32)
    xt[:, :, :, TAPS - 1:TAPS - 1 + T] = x.reshape(B, T, KT, P).transpose(3, 2, 0, 1)

    def heads(w, n):
        return w.reshape(KT, P, n, H, DH).transpose(3, 1, 0, 2, 4)
    w_all = np.concatenate([heads(g["a_Wq"], 1), heads(g["a_Wk"], NH), heads(g["a_Wv"], NH), heads(g["a_Wg"], 1)], 3)
    wz = np.concatenate([g["a_Wb"], g["a_Wa"]], 1).reshape(KT, P, 32).transpose(1, 0, 2)

    def convs(w, n):
        return w.reshape(n, H, DH, TAPS).transpose(2, 1, 0, 3)
    cw = np.concatenate([convs(g["a_conv_q"], 1), convs(g["a_conv_k"], NH), convs(g["a_conv_v"], NH)], 2)
    consts, masks = constants()

    def padded(b):
        z = np.zeros((E, FT * P), np.float32)
        z[:, :F] = b
        return z.reshape(E, FT, P).transpose(2, 0, 1).reshape(P, E * FT)
    dw = np.zeros((E, FT * P, D), np.float32)
    dw[:, :F] = g["f_down_w"].transpose(0, 2, 1)

    def up(w):
        z = np.zeros((E, D, FP), np.float32)
        z[:, :, :F] = w.transpose(0, 2, 1)
        return z.reshape(E, KT, P, FP).transpose(0, 2, 1, 3).reshape(E, P, KT * FP)
    arrays = {
        "x_t": xt.reshape(P, -1), "x_rows": x.reshape(B * T, D), "w_all": w_all.reshape(H, P, KT * HC),
        "w_z": wz.reshape(P, -1), "conv_w": cw.reshape(P, -1),
        "a_log": np.broadcast_to(g["a_A_log"][None], (96, H)), "dt_bias": np.broadcast_to(g["a_dt_bias"][None], (96, H)),
        "rms_w": g["a_rms_weight"].reshape(P, 1),
        "w_o": g["a_Wo"].reshape(H, DH, D).transpose(1, 0, 2).reshape(P, H * D), "consts": consts, "masks": masks,
        "gate_w": g["f_gate_w"].T.reshape(KT, P, E).transpose(1, 0, 2).reshape(P, KT * E),
        "gate_b": np.broadcast_to(g["f_gate_b"][None], (P, E)),
        "up_w": up(g["f_up_w"]), "up_b": padded(g["f_up_b"]), "gp_w": up(g["f_gp_w"]), "gp_b": padded(g["f_gp_b"]),
        "down_w": dw.reshape(E, FT, P, D).transpose(0, 2, 1, 3).reshape(E, P, FT * D), "down_b": g["f_down_b"],
    }
    nc = _bacc.Bacc("TRN2", target_bir_lowering=False, num_devices=1)
    args, feed = [], {}
    for name, a in arrays.items():
        a = np.ascontiguousarray(a)
        feed["in_" + name] = a
        args.append(nc.dram_tensor("in_" + name, a.shape, mybir.dt.from_np(a.dtype), kind="ExternalInput").ap())
    args.append(nc.dram_tensor("out_y", (B * T, D), F32, kind="ExternalOutput").ap())
    build(nc, *args)
    r = _run(nc, [feed], core_ids=[0])
    return r.results[0]["out_y"].reshape(B, T, D)
```
